# Optimizing a Trainium2 kernel written in Bass

```python
import numpy as np
import jax
import jax.numpy as jnp

def _softmax(x, axis=-1):
    return jax.nn.softmax(x, axis=axis)

def _gelu(x):
    return jax.nn.gelu(x, approximate=True)

def _silu(x):
    return jax.nn.silu(x)

def _sigmoid(x):
    return jax.nn.sigmoid(x)

def _layernorm(x, axis=-1, eps=1e-05):
    m = jnp.mean(x, axis=axis, keepdims=True)
    v = jnp.var(x, axis=axis, keepdims=True)
    return (x - m) / jnp.sqrt(v + eps)

def _scatter_add(tgt, idx, src, axis=0):
    return tgt.at[idx].add(src)

def _segment_sum(src, seg, n):
    return jax.ops.segment_sum(src, seg, n)
kernel_name = 'mk_adj_ffn_d2_adj_r2_089a06'

def setup_inputs(seed: int=0):
    np.random.seed(seed)
    _w = jnp.asarray

    def _rec_inputs():
        import jax
        import jax.numpy as jnp
        _gk = jax.random.key(seed)
        x = -0.0002928 + 1 * jax.random.normal(jax.random.fold_in(_gk, 1), (128, 128, 128), jnp.float32)
        _a = jax.random.bernoulli(jax.random.fold_in(_gk, 2), 0.125, (128, 128))
        _a = jnp.logical_or(_a, jnp.eye(128, dtype=bool))
        _af = _a.astype(jnp.float32)
        adj = _af
        return (x, adj)
    x, adj = _rec_inputs()

    def _L0_gnn_setup():
        import jax, jax.numpy as jnp
        import numpy as np
        ALPHA = 0.2
        key = jax.random.key(seed)
        k1, k2, k3, k4 = jax.random.split(key, 4)
        B, N, Fin, Fout = (8, 1024, 128, 128)
        h = jax.random.normal(k1, (B, N, Fin), dtype=jnp.float32)
        adj = jax.random.randint(k2, (N, N), 0, 2).astype(jnp.float32)
        adj = jnp.maximum(adj, jnp.eye(N, dtype=jnp.float32))

        def xavier(k, shape, gain=1.414):
            fan_in, fan_out = (shape[0], shape[1])
            a = gain * np.sqrt(6.0 / (fan_in + fan_out))
            return jax.random.uniform(k, shape, dtype=jnp.float32, minval=-a, maxval=a)
        W = xavier(k3, (Fin, Fout))
        a = xavier(k4, (2 * Fout, 1))
        return {'h': h, 'adj_matrix': adj, 'W': W, 'a': a}
    _L0_gnn_all = _L0_gnn_setup()
    _L0_gnn_in = {k: v for k, v in _L0_gnn_all.items() if k in ('W', 'a')}
    del _L0_gnn_all

    def _L0_ffn_setup():
        import jax, jax.numpy as jnp
        import numpy as np
        D_MODEL = 128
        N_EXPERTS = 16
        HIDDEN = 256
        SCALE = 0.02
        key = jax.random.key(seed)
        ks = jax.random.split(key, 5)
        x = jax.random.normal(ks[0], (4, 4096, D_MODEL), dtype=jnp.float32)
        gate_w = jax.random.normal(ks[1], (D_MODEL, N_EXPERTS), dtype=jnp.float32) * SCALE
        gate_b = jnp.zeros((N_EXPERTS,), dtype=jnp.float32)
        w1 = jax.random.normal(ks[2], (N_EXPERTS, D_MODEL, HIDDEN), dtype=jnp.float32) * SCALE
        w2 = jax.random.normal(ks[3], (N_EXPERTS, D_MODEL, HIDDEN), dtype=jnp.float32) * SCALE
        w3 = jax.random.normal(ks[4], (N_EXPERTS, HIDDEN, D_MODEL), dtype=jnp.float32) * SCALE
        return {'x': x, 'gate_w': gate_w, 'gate_b': gate_b, 'w1': w1, 'w2': w2, 'w3': w3}
    _L0_ffn_all = _L0_ffn_setup()
    _L0_ffn_in = {k: v for k, v in _L0_ffn_all.items() if k in ('gate_w', 'gate_b', 'w1', 'w2', 'w3')}
    del _L0_ffn_all

    def _L1_gnn_setup():
        import jax, jax.numpy as jnp
        import numpy as np
        N = 3445
        B = 32
        IN_DIM = 128
        HID_DIM = 128

        def _make_adj(key):
            a = jax.random.uniform(key, (N, N), dtype=jnp.float32)
            a = (a < 0.001).astype(jnp.float32)
            a = jnp.maximum(a, a.T)
            deg = jnp.sum(a, axis=1, keepdims=True)
            return a / jnp.maximum(deg, 1.0)

        def _graph_conv(x, adj, w_loop, w_neigh, b):
            loop = jnp.einsum('bnd,dh->bnh', x, w_loop)
            neigh = jnp.einsum('nm,bmh->bnh', adj, jnp.einsum('bnd,dh->bnh', x, w_neigh))
            return loop + neigh + b
        key = jax.random.key(seed)
        k = jax.random.split(key, 8)
        s1 = 1.0 / np.sqrt(IN_DIM)
        s2 = 1.0 / np.sqrt(HID_DIM)
        return {'x': jax.random.normal(k[0], (B, N, IN_DIM), dtype=jnp.float32), 'adj': _make_adj(k[1]), 'w1_loop': jax.random.normal(k[2], (IN_DIM, HID_DIM), dtype=jnp.float32) * s1, 'w1_neigh': jax.random.normal(k[3], (IN_DIM, HID_DIM), dtype=jnp.float32) * s1, 'b1': jnp.zeros((HID_DIM,), dtype=jnp.float32), 'w2_loop': jax.random.normal(k[4], (HID_DIM, IN_DIM), dtype=jnp.float32) * s2, 'w2_neigh': jax.random.normal(k[5], (HID_DIM, IN_DIM), dtype=jnp.float32) * s2, 'b2': jnp.zeros((IN_DIM,), dtype=jnp.float32)}
    _L1_gnn_all = _L1_gnn_setup()
    _L1_gnn_in = {k: v for k, v in _L1_gnn_all.items() if k in ('w1_loop', 'w1_neigh', 'b1', 'w2_loop', 'w2_neigh', 'b2')}
    del _L1_gnn_all

    def _L1_ffn_setup():
        import jax, jax.numpy as jnp
        import numpy as np
        B, H, E, IN, OUT = (2048, 1, 8, 128, 128)

        @jax.custom_vjp
        def bin_active(x):
            return jnp.sign(x)

        def _ba_fwd(x):
            return (jnp.sign(x), x)

        def _ba_bwd(x, g):
            return (g * (jnp.abs(x) <= 1.0).astype(g.dtype),)
        bin_active.defvjp(_ba_fwd, _ba_bwd)

        @jax.custom_vjp
        def bin_gate(x):
            return (x > 0.5).astype(x.dtype)

        def _bg_fwd(x):
            return ((x > 0.5).astype(x.dtype), None)

        def _bg_bwd(_, g):
            return (g,)
        bin_gate.defvjp(_bg_fwd, _bg_bwd)
        key = jax.random.key(seed)
        k1, k2, k3, k4, k5 = jax.random.split(key, 5)
        x = jax.random.normal(k1, (B, H, IN), dtype=jnp.float32)
        weight = jax.random.normal(k2, (H, E, IN, OUT), dtype=jnp.float32) * 0.05
        proj_w = jax.random.normal(k3, (E, IN), dtype=jnp.float32) * 0.05
        proj_b = jax.random.normal(k4, (E,), dtype=jnp.float32) * 0.05
        scale = jax.random.normal(k5, (H, 1, OUT), dtype=jnp.float32) * 0.1
        return {'x': x, 'weight': weight, 'proj_w': proj_w, 'proj_b': proj_b, 'scale': scale}
    _L1_ffn_all = _L1_ffn_setup()
    _L1_ffn_in = {k: v for k, v in _L1_ffn_all.items() if k in ('weight', 'proj_w', 'proj_b', 'scale')}
    del _L1_ffn_all
    return {'x': x, 'adj': adj, 'L0_gnn_W': _L0_gnn_in['W'], 'L0_gnn_a': _L0_gnn_in['a'], 'L0_ffn_gate_w': _L0_ffn_in['gate_w'], 'L0_ffn_gate_b': _L0_ffn_in['gate_b'], 'L0_ffn_w1': _L0_ffn_in['w1'], 'L0_ffn_w2': _L0_ffn_in['w2'], 'L0_ffn_w3': _L0_ffn_in['w3'], 'L1_gnn_w1_loop': _L1_gnn_in['w1_loop'], 'L1_gnn_w1_neigh': _L1_gnn_in['w1_neigh'], 'L1_gnn_b1': _L1_gnn_in['b1'], 'L1_gnn_w2_loop': _L1_gnn_in['w2_loop'], 'L1_gnn_w2_neigh': _L1_gnn_in['w2_neigh'], 'L1_gnn_b2': _L1_gnn_in['b2'], 'L1_ffn_weight': _L1_ffn_in['weight'], 'L1_ffn_proj_w': _L1_ffn_in['proj_w'], 'L1_ffn_proj_b': _L1_ffn_in['proj_b'], 'L1_ffn_scale': _L1_ffn_in['scale']}

def reference(x, adj, L0_gnn_W, L0_gnn_a, L0_ffn_gate_w, L0_ffn_gate_b, L0_ffn_w1, L0_ffn_w2, L0_ffn_w3, L1_gnn_w1_loop, L1_gnn_w1_neigh, L1_gnn_b1, L1_gnn_w2_loop, L1_gnn_w2_neigh, L1_gnn_b2, L1_ffn_weight, L1_ffn_proj_w, L1_ffn_proj_b, L1_ffn_scale):
    import jax
    import jax.numpy as jnp

    def _L0_gnn_ref(h, adj_matrix, W, a):
        import jax, jax.numpy as jnp
        import numpy as np
        ALPHA = 0.2
        Fout = W.shape[1]
        Wh = jnp.einsum('bnf,fo->bno', h, W)
        a1, a2 = (a[:Fout, 0], a[Fout:, 0])
        s1 = Wh @ a1
        s2 = Wh @ a2
        e = s1[:, :, None] + s2[:, None, :]
        e = jnp.where(e >= 0, e, ALPHA * e)
        e = jnp.where(adj_matrix[None] == 0, -jnp.inf, e)
        attention = jax.nn.softmax(e, axis=-1)
        h_prime = jnp.einsum('bij,bjo->bio', attention, Wh)
        return h_prime

    def _L0_ffn_ref(x, gate_w, gate_b, w1, w2, w3):
        import jax, jax.numpy as jnp
        import numpy as np
        D_MODEL = 128
        N_EXPERTS = 16
        HIDDEN = 256
        SCALE = 0.02
        n_experts = w1.shape[0]
        logits = jnp.einsum('bsd,de->bse', x, gate_w) + gate_b
        probs = jax.nn.softmax(logits, axis=-1)
        top_probs, top_idx = jax.lax.top_k(probs, 2)
        top_probs = top_probs / jnp.sum(top_probs, axis=-1, keepdims=True)
        dispatch = jnp.sum(jax.nn.one_hot(top_idx, n_experts, dtype=x.dtype) * top_probs[..., None], axis=-2)
        h1 = jnp.einsum('bsd,edh->bseh', x, w1)
        h2 = jnp.einsum('bsd,edh->bseh', x, w2)
        hidden = jax.nn.silu(h1) * h2
        expert_out = jnp.einsum('bseh,eho->bseo', hidden, w3)
        return jnp.einsum('bseo,bse->bso', expert_out, dispatch)

    def _L1_gnn_ref(x, adj, w1_loop, w1_neigh, b1, w2_loop, w2_neigh, b2):
        import jax, jax.numpy as jnp
        import numpy as np
        N = 3445
        B = 32
        IN_DIM = 128
        HID_DIM = 128

        def _make_adj(key):
            a = jax.random.uniform(key, (N, N), dtype=jnp.float32)
            a = (a < 0.001).astype(jnp.float32)
            a = jnp.maximum(a, a.T)
            deg = jnp.sum(a, axis=1, keepdims=True)
            return a / jnp.maximum(deg, 1.0)

        def _graph_conv(x, adj, w_loop, w_neigh, b):
            loop = jnp.einsum('bnd,dh->bnh', x, w_loop)
            neigh = jnp.einsum('nm,bmh->bnh', adj, jnp.einsum('bnd,dh->bnh', x, w_neigh))
            return loop + neigh + b
        h = jax.nn.relu(_graph_conv(x, adj, w1_loop, w1_neigh, b1))
        h = jax.nn.relu(_graph_conv(h, adj, w2_loop, w2_neigh, b2))
        return (x + h) * 0.5

    def _L1_ffn_ref(x, weight, proj_w, proj_b, scale):
        import jax, jax.numpy as jnp
        import numpy as np
        B, H, E, IN, OUT = (2048, 1, 8, 128, 128)

        @jax.custom_vjp
        def bin_active(x):
            return jnp.sign(x)

        def _ba_fwd(x):
            return (jnp.sign(x), x)

        def _ba_bwd(x, g):
            return (g * (jnp.abs(x) <= 1.0).astype(g.dtype),)
        bin_active.defvjp(_ba_fwd, _ba_bwd)

        @jax.custom_vjp
        def bin_gate(x):
            return (x > 0.5).astype(x.dtype)

        def _bg_fwd(x):
            return ((x > 0.5).astype(x.dtype), None)

        def _bg_bwd(_, g):
            return (g,)
        bin_gate.defvjp(_bg_fwd, _bg_bwd)
        xh = jnp.transpose(x, (1, 0, 2))
        gate = jax.nn.sigmoid(jnp.einsum('hbi,ei->hbe', xh, proj_w) + proj_b)
        gate = bin_gate(gate)
        w = jnp.einsum('hbe,heio->hbio', gate, weight)
        xb = bin_active(xh)
        wb = bin_active(w)
        y = jnp.einsum('hbi,hbio->hbo', xb, wb)
        y = y * scale
        return jnp.transpose(y, (1, 0, 2))
    x = x + _L0_gnn_ref(_layernorm(x, axis=-1), adj, L0_gnn_W, L0_gnn_a)
    x = x + _L0_ffn_ref(_layernorm(x, axis=-1), L0_ffn_gate_w, L0_ffn_gate_b, L0_ffn_w1, L0_ffn_w2, L0_ffn_w3)
    x = x + _L1_gnn_ref(_layernorm(x, axis=-1), adj, L1_gnn_w1_loop, L1_gnn_w1_neigh, L1_gnn_b1, L1_gnn_w2_loop, L1_gnn_w2_neigh, L1_gnn_b2)
    x = x + _L1_ffn_ref(_layernorm(x, axis=-1), L1_ffn_weight, L1_ffn_proj_w, L1_ffn_proj_b, L1_ffn_scale)
    return x

_drawn_inputs = setup_inputs


def setup_inputs(seed=0):
    import zlib

    import numpy as np

    out = dict(_drawn_inputs(seed))
    spreads = {'L0_ffn_gate_b': (0.0, 0.8), 'L1_gnn_b1': (0.0, 0.389), 'L1_gnn_b2': (0.0, 2.0)}
    factors = {'L0_ffn_gate_w': 8.0,
     'L0_ffn_w1': 8.0,
     'L0_ffn_w2': 8.0,
     'L0_ffn_w3': 8.0,
     'L1_ffn_proj_b': 2.973}
    for name, (base, spread) in spreads.items():
        noise = np.random.default_rng([zlib.crc32(name.encode()), seed]).standard_normal(out[name].shape)
        drawn = base * np.exp(spread * noise) if base else spread * noise
        out[name] = jnp.asarray(drawn.astype(out[name].dtype))
    for name, factor in factors.items():
        out[name] = (out[name] * factor).astype(out[name].dtype)
    return out
```

```python
import concourse.bass as bass
from concourse import mybir
from contextlib import ExitStack

F32 = mybir.dt.float32
BF16 = mybir.dt.bfloat16
I32 = mybir.dt.int32
U32 = mybir.dt.uint32
ALU = mybir.AluOpType
ACT = mybir.ActivationFunctionType
AX = mybir.AxisListType

P = 128
BATCH = 128
G = 4
NG = BATCH // G
GW = G * P
TOKENS = BATCH * P
E0 = 16
HID = 256
MT = 2 * TOKENS // P + E0
E1 = 8
PAT = 1 << E1
PB = 32
PT = (TOKENS // PB + PAT) * PB // P
NB = P // PB
EPS = 1e-5
SLOPE = 0.2
MASKED = -1e30


def steps(eng, stages, groups, ring=4):
    last = max(lag for lag, _ in stages)
    head = last
    while (groups - head) % ring:
        head += 1

    def step(i):
        for lag, work in stages:
            if 0 <= i - lag < groups:
                work((i - lag) // ring, (i - lag) % ring)

    for i in range(head):
        step(i)
    if groups > head:
        with eng.Fori(0, (groups - head) // ring) as n:
            for u in range(ring):
                for lag, work in stages:
                    work(n + (head + u - lag) // ring, (head + u - lag) % ring)
    for i in range(groups, groups + last):
        step(i)


def group(q, r, ring=4):
    return ring * q + r


def as3(ap, n=G):
    return ap.rearrange("p (g c) -> p g c", g=n)


CREDIT = 4


def wait_done(eng, sem, t):
    eng.wait_ge(sem, t + (1 + CREDIT))


def wait_free(eng, sem, t, ring):
    eng.wait_ge(sem, t + (1 + CREDIT - ring))


def wait_loaded(eng, sem, q, copies=1):
    eng.wait_ge(sem, (q + 1) * (16 * copies))


def wait_stored(eng, sem, q):
    eng.wait_ge(sem, (q + 1) * 16)


class Links:

    def __init__(self, eng, sem, per_group=0):
        self.eng, self.sem, self.per_group, self.base, self.n = eng, sem, per_group, 0, 0

    def at(self, t):
        self.base, self.n = t * self.per_group, 0

    def then(self, ins):
        self.n += 1
        assert not self.per_group or self.n <= self.per_group
        ins.then_inc(self.sem, 1)
        self.eng.wait_ge(self.sem, self.base + self.n)


def alone(eng, ticks):
    eng.sem_inc(ticks, 1)


def ln_stats(nc, link, ticks, stats, mv, src):
    for j in range(G):
        last = nc.vector.bn_stats(stats[:, j, :], src[:, j * P:(j + 1) * P])
    link.then(last)
    alone(nc.vector, ticks)
    for j in range(G - 1):
        nc.vector.bn_aggr(mv[:, j, :], stats[:, j, :])
    return nc.vector.bn_aggr(mv[:, G - 1, :], stats[:, G - 1, :])


def build(nc, xt, adj, adjT, W, WT, a12, gate_w, w12, w3, w1l, w1n, w2l, w2n, b1, b2, rows, wgt, projT, out, stop=9):
    ctx = ExitStack()
    scope = [ctx]
    taken = set()

    def sb(name, shape, dt=F32):
        name = f"{name}_{len(taken)}" if name in taken else name
        taken.add(name)
        return scope[-1].enter_context(nc.sbuf_tensor(name, shape, dt))

    stage_sems = []

    def sem(name):
        stage_sems.append(nc.alloc_semaphore(name=name))
        return stage_sems[-1]

    def end_stage():
        nc.clear_and_free_semaphores(stage_sems)
        stage_sems.clear()
        nc.all_engine_barrier()

    ticks = {}
    for name in ("pool", "vector", "scalar", "tensor", "sync"):
        ticks[name] = ctx.enter_context(nc.semaphore(f"{name}_ticks"))
    vt, pt = ticks["vector"], ticks["pool"]

    def sems(name, n=4):
        return [sem(f"{name}{i}") for i in range(n)]

    with ctx:
        x1_d = nc.dram_tensor("x1_d", [P, BATCH * P], F32, kind="Internal").ap()
        x2_d = nc.dram_tensor("x2_d", [P, BATCH * P], F32, kind="Internal").ap()
        xn_d = nc.dram_tensor("xn_d", [TOKENS, P], F32, kind="Internal").ap()
        y_d = nc.dram_tensor("y_d", [MT * P, P], F32, kind="Internal").ap()
        sx_d = nc.dram_tensor("sx_d", [TOKENS, P], BF16, kind="Internal").ap()
        yb_d = nc.dram_tensor("yb_d", [PT * P, P], BF16, kind="Internal").ap()
        xt_v = xt.rearrange("n b f -> n (b f)")
        out_v = out.rearrange("n b f -> n (b f)")
        xn_v = xn_d.rearrange("(n b) f -> n (b f)", b=BATCH)
        sx_v = sx_d.rearrange("(n b) f -> n (b f)", b=BATCH)

        psum = [ctx.enter_context(nc.psum_tensor(f"bank{i}", [P, 512], F32)) for i in range(8)]

        ident = sb("ident", [P, P])
        ident_bf = sb("ident_bf", [P, P], BF16)
        before = sb("before", [P, P], BF16)
        not_before = sb("not_before", [P, P], BF16)
        ones_bf = sb("ones_bf", [P, P], BF16)
        zeros_bf = sb("zeros_bf", [P, P], BF16)
        ones_row = sb("ones_row", [1, P])
        mhalf = sb("mhalf", [P, G])
        count_i = sb("count_i", [P, NB * PT], I32)
        count = sb("count", [P, NB * PT])
        count_bf = sb("count_bf", [P, 256], BF16)
        tile_bf = sb("tile_bf", [P, MT], BF16)
        row_i = sb("row_i", [P, 1], I32)
        row_id = sb("row_id", [P, 1])
        mask = sb("mask", [P, P], BF16)
        W_s = sb("W_s", [P, P])
        WT_s = sb("WT_s", [P, P])
        a12_s = sb("a12_s", [P, 2])
        Waug = sb("Waug", [P, P + 2])
        wa2 = sb("wa2", [P, P])
        adj_s = sb("adj_s", [P, P])
        adjT_s = sb("adjT_s", [P, P])
        gw_s = sb("gw_s", [P, E0])
        rows_s = sb("rows_s", [1, E0 + E1 + P])
        rows_b = sb("rows_b", [P, E0 + E1 + P])
        gbias = rows_b[:, 0:E0]
        pbias = rows_b[:, E0:E0 + E1]
        scale = rows_b[:, E0 + E1:]
        w1l_s = sb("w1l_s", [P, P])
        w1n_s = sb("w1n_s", [P, P])
        w2l_s = sb("w2l_s", [P, P])
        w2n_s = sb("w2n_s", [P, P])
        b1_s = sb("b1_s", [P, 1])
        b2_s = sb("b2_s", [1, P])
        b2x = sb("b2x", [1, GW])
        projT_s = sb("projT_s", [P, E1])
        bits = sb("bits", [P, E1])
        expert = sb("expert", [P, BATCH, 2])
        top = sb("top", [P, BATCH, 2])
        share = sb("share", [P, BATCH, 2])
        slot = sb("slot", [P, BATCH, 2], I32)
        signs = sb("signs", [P, PAT, P], BF16)

        def pool_ln(pool, link, mv, ve, rstd):
            link.then(pool.tensor_scalar(ve, mv[:, :, 1], EPS, None, ALU.add))
            return pool.tensor_tensor(ve, ve, mhalf[:, :], ALU.pow)

        s_ld, s_pc, s_vc, s_mm, s_mv = sem("const_loaded"), sem("pool_consts"), sem("vector_consts"), sem("const_mm"), sem("const_mv")
        loads = [(W_s, W), (WT_s, WT), (a12_s, a12), (adj_s, adj), (adjT_s, adjT), (gw_s, gate_w), (rows_s, rows),
                 (w1l_s, w1l), (w1n_s, w1n), (w2l_s, w2l), (w2n_s, w2n), (b1_s, b1), (b2_s, b2), (projT_s, projT)]
        scope.append(ExitStack())
        wsum_lo = sb("wsum_lo", [P, 16, P])
        wsum_hi = sb("wsum_hi", [P, 16, P])
        wgt_s = sb("wgt_s", [P, E1, P])
        with nc.Block() as block:
            @block.sync
            def _(sp):
                for dst, src in loads:
                    sp.dma_start(dst[:, :], src).then_inc(s_ld, 16)
                sp.dma_start(wgt_s[:, :, :], wgt).then_inc(s_ld, 16)

            @block.gpsimd
            def _(pool):
                link = Links(pool, s_pc)
                pool.memset(zeros_bf[:, :], 0.0)
                pool.memset(ones_bf[:, :], 1.0)
                pool.memset(not_before[:, :], 1.0)
                pool.memset(ones_row[:, :], 1.0)
                pool.memset(mhalf[:, :], -0.5)
                pool.memset(ident[:, :], 0.0)
                pool.memset(ident_bf[:, :], 0.0)
                link.then(pool.memset(before[:, :], 0.0))
                pool.affine_select(out=ident[:, :], in_=ident[:, :], compare_op=ALU.not_equal, fill=1.0, base=0,
                                   pattern=[[-1, P]], channel_multiplier=1)
                pool.affine_select(out=ident_bf[:, :], in_=ident_bf[:, :], compare_op=ALU.not_equal, fill=1.0, base=0,
                                   pattern=[[-1, P]], channel_multiplier=1)
                pool.affine_select(out=before[:, :], in_=before[:, :], compare_op=ALU.is_ge, fill=1.0, base=0,
                                   pattern=[[-1, P]], channel_multiplier=1)
                pool.affine_select(out=not_before[:, :], in_=not_before[:, :], compare_op=ALU.is_ge, fill=0.0, base=0,
                                   pattern=[[-1, P]], channel_multiplier=1)
                pool.iota(row_i[:, :], pattern=[[0, 1]], base=0, channel_multiplier=P)
                link.then(pool.iota(count_i[:, :], pattern=[[1, NB * PT]], base=0, channel_multiplier=0))

            @block.vector
            def _(dve):
                link = Links(dve, s_vc)
                v = nc.vector
                dve.wait_ge(s_pc, 2)
                for g in range(E1):
                    v.memset(bits[:, g:g + 1], float(1 << g))
                v.tensor_copy(count[:, :], count_i[:, :])
                v.tensor_copy(row_id[:, :], row_i[:, :])
                v.memset(wsum_lo[:, 0, :], 0.0)
                v.memset(wsum_hi[:, 0, :], 0.0)
                link.then(v.tensor_copy(count_bf[:, :], count_i[:, 0:256]))
                v.tensor_scalar(tile_bf[:, :], count[:, 0:MT], float(MT // 2), None, ALU.subtract)
                dve.wait_ge(s_ld, 16 * (len(loads) + 1))
                v.tensor_scalar(mask[:, :], adj_s[:, :], 0.0, MASKED, ALU.is_equal, ALU.mult)
                for g in range(4):
                    n = 1 << g
                    v.tensor_tensor(wsum_lo[:, n:2 * n, :], wsum_lo[:, 0:n, :],
                                    wgt_s[:, g, :].unsqueeze(1).to_broadcast([P, n, P]), ALU.add)
                    link.then(v.tensor_tensor(wsum_hi[:, n:2 * n, :], wsum_hi[:, 0:n, :],
                                              wgt_s[:, 4 + g, :].unsqueeze(1).to_broadcast([P, n, P]), ALU.add))
                v.tensor_copy(Waug[:, 0:P], W_s[:, :])
                v.tensor_copy(b2x[:, :].rearrange("p (g c) -> p g c", g=G), b2_s[:, :].unsqueeze(1).to_broadcast([1, G, P]))
                dve.wait_ge(s_mm, 1)
                v.tensor_copy(Waug[:, P:P + 2], psum[0][:, 0:2])
                v.tensor_copy(wa2[:, :], psum[0][:, 1:2].to_broadcast([P, P]))
                dve.wait_ge(s_mm, 2)
                link.then(v.tensor_copy(rows_b[:, :], psum[1][:, 0:E0 + E1 + P]))

            @block.tensor
            def _(pe):
                pe.wait_ge(s_ld, 16 * (len(loads) + 1))
                pe.wait_ge(s_pc, 2)
                nc.tensor.matmul(psum[0][:, 0:2], WT_s[:, :], a12_s[:, :], start=True, stop=True).then_inc(s_mm, 1)
                nc.tensor.matmul(psum[1][:, 0:E0 + E1 + P], ones_row[:, :], rows_s[:, :], start=True, stop=True).then_inc(s_mm, 1)
        end_stage()

        xa_in, xd_in, x1_st, xn_st = sems("xa_in"), sems("xd_in"), sems("x1_st"), sems("xn_st")
        a_stats, a_xn, a_tr, a_xnT = sem("a_stats"), sem("a_xn"), sem("a_transposed"), sem("a_xnT")
        a_wh, a_whs, a_max, a_exp = sem("a_wh"), sem("a_wh_copied"), sem("a_max"), sem("a_exp")
        a_p = sem("a_p")
        a_sc = sem("a_scores")
        a_att, a_attT, a_av, a_x1 = sem("a_att"), sem("a_attT"), sem("a_av"), sem("a_x1")
        a_xn2, a_tr2, a_xn2T, a_gate, a_top = sem("a_xn2"), sem("a_transposed2"), sem("a_xn2T"), sem("a_gate"), sem("a_top")
        a_wt, a_sign = sem("a_wt"), sem("a_sign")
        a_va, a_vb, a_vd, a_ve, a_pa, a_pd, a_ac = [sem("a_link%d" % i) for i in range(7)]
        scope.append(ExitStack())
        xa, xd, xo = sb("xa", [P, 4, GW]), sb("xd", [P, 4, GW]), sb("xo", [P, 4, GW])
        stats, mv, ve = sb("stats", [P, 2, G, 6]), sb("mv", [P, 4, G, 2]), sb("ve", [P, 4, G])
        xn, xnT, wh = sb("xn", [P, 2, GW]), sb("xnT", [P, 2, GW]), sb("wh", [P, 4, 2, 2 * (P + 2)])
        rmax, shift, rsum = sb("rmax", [P, 3, G]), sb("shift", [P, 4, 2, G]), sb("rsum", [P, 4, G])
        pos, neg = sb("pos", [P, 2, GW]), sb("neg", [P, 2, GW])
        att, attT = sb("att", [P, 2, GW]), sb("attT", [P, 2, GW])
        stats2, mv2, ve2 = sb("stats2", [P, G, 6]), sb("mv2", [P, 4, G, 2]), sb("ve2", [P, 4, G])
        xn2, xn2T = sb("xn2", [P, 4, GW]), sb("xn2T", [P, 2, GW])
        lg, top8, idx8 = sb("lg", [P, G, E0]), sb("top8", [P, G, 8]), sb("idx8", [P, G, 8], U32)
        wt = sb("wt", [P, 2, 8, P])
        whp = [psum[1], psum[2]]

        with nc.Block() as block:
            @block.sync
            def _(sp):
                for r in range(4):
                    sp.sem_inc(x1_st[r], 16)
                    sp.sem_inc(xn_st[r], 16)

                def load_a(q, r):
                    wait_free(sp, a_xn, group(q, r), 4)
                    sp.dma_start(xa[:, r, :], xt_v[:, bass.ds(group(q, r) * GW, GW)]).then_inc(xa_in[r], 16)

                def load_d(q, r):
                    wait_free(sp, a_x1, group(q, r), 4)
                    sp.dma_start(xd[:, r, :], xt_v[:, bass.ds(group(q, r) * GW, GW)]).then_inc(xd_in[r], 16)

                def store(q, r):
                    wait_done(sp, a_x1, group(q, r))
                    sp.dma_start(x1_d[:, bass.ds(group(q, r) * GW, GW)], xo[:, r, :]).then_inc(x1_st[r], 16)
                    wait_done(sp, a_xn2, group(q, r))
                    sp.dma_start(xn_v[:, bass.ds(group(q, r) * GW, GW)], xn2[:, r, :]).then_inc(xn_st[r], 16)

                steps(sp, [(7, store), (2, load_d), (0, load_a)], NG)
                for r in range(4):
                    sp.wait_ge(x1_st[r], 16 * (NG // 4 + 1))
                    sp.wait_ge(xn_st[r], 16 * (NG // 4 + 1))

            @block.gpsimd
            def _(pool):
                for s in (a_xn, a_xn2, a_wt):
                    pool.sem_inc(s, CREDIT)
                la, ld = Links(pool, a_pa, 2), Links(pool, a_pd, 2)

                def norm_a(q, r):
                    t = group(q, r)
                    la.at(t)
                    wait_done(pool, a_stats, t)
                    alone(pool, pt)
                    la.then(pool.tensor_scalar(ve[:, r, :], mv[:, r, :, 1], EPS, None, ALU.add))
                    la.then(pool.tensor_tensor(ve[:, r, :], ve[:, r, :], mhalf[:, :], ALU.pow))
                    pool.wait_ge(xa_in[r], (q + 1) * 16)
                    wait_free(pool, a_tr, t, 2)
                    alone(pool, pt)
                    for j in range(G):
                        last = pool.tensor_scalar(xn[:, r % 2, j * P:(j + 1) * P], xa[:, r, j * P:(j + 1) * P],
                                                  mv[:, r, j, 0:1], ve[:, r, j:j + 1], ALU.subtract, ALU.mult)
                    last.then_inc(a_xn, 1)

                def norm_d(q, r):
                    t = group(q, r)
                    ld.at(t)
                    wait_done(pool, a_x1, t)
                    alone(pool, pt)
                    ld.then(pool.tensor_scalar(ve2[:, r, :], mv2[:, r, :, 1], EPS, None, ALU.add))
                    ld.then(pool.tensor_tensor(ve2[:, r, :], ve2[:, r, :], mhalf[:, :], ALU.pow))
                    wait_stored(pool, xn_st[r], q)
                    wait_free(pool, a_tr2, t, 4)
                    alone(pool, pt)
                    for j in range(G):
                        last = pool.tensor_scalar(xn2[:, r, j * P:(j + 1) * P], xo[:, r, j * P:(j + 1) * P],
                                                  mv2[:, r, j, 0:1], ve2[:, r, j:j + 1], ALU.subtract, ALU.mult)
                    last.then_inc(a_xn2, 1)

                def sum_weights(q, r):
                    t = group(q, r)
                    wait_free(pool, a_sign, t, 2)
                    alone(pool, pt)
                    pool.tensor_tensor(wt[:, r % 2, :, :], wsum_lo[:, (r % 2) * 8:(r % 2) * 8 + 8, :],
                                       wsum_hi[:, bass.ds(2 * q + r // 2, 1), :].to_broadcast([P, 8, P]),
                                       ALU.add).then_inc(a_wt, 1)

                def first(q, r):
                    norm_a(q, r)
                    sum_weights(q, r)

                steps(pool, [(4, norm_d), (0, first)], NG)

            @block.vector
            def _(dve):
                v = nc.vector
                for s in (a_stats, a_max, a_x1, a_top, a_p):
                    dve.sem_inc(s, CREDIT)
                la, lb, ld, le = Links(dve, a_va, 1), Links(dve, a_vb, 3), Links(dve, a_vd, 2), Links(dve, a_ve, 3)

                def stats_a(q, r):
                    t = group(q, r)
                    la.at(t)
                    wait_loaded(dve, xa_in[r], q)
                    wait_free(dve, a_xn, t, 4)
                    ln_stats(nc, la, vt, stats[:, r % 2], mv[:, r], xa[:, r, :]).then_inc(a_stats, 1)

                def max_b(q, r):
                    t = group(q, r)
                    lb.at(t)
                    wait_done(dve, a_sc, t)
                    lb.then(v.reduce_max(rmax[:, 0, :], as3(psum[3][:, :]), AX.X))
                    wait_done(dve, a_whs, t)
                    s1 = wh[:, r, :, :].rearrange("p a (b c) -> p a b c", b=2)[:, :, :, P].rearrange("p a b -> p (a b)")
                    lb.then(v.tensor_tensor(rmax[:, 1, :], rmax[:, 0, :], s1, ALU.add))
                    lb.then(v.scalar_tensor_tensor(rmax[:, 2, :], rmax[:, 1, :], SLOPE, rmax[:, 1, :], ALU.mult, ALU.max))
                    wait_free(dve, a_exp, t, 4)
                    v.tensor_tensor(shift[:, r, 0, :], s1, rmax[:, 2, :], ALU.subtract)
                    v.scalar_tensor_tensor(shift[:, r, 1, :], s1, SLOPE, rmax[:, 2, :], ALU.mult, ALU.subtract).then_inc(a_max, 1)

                def p_c(q, r):
                    t = group(q, r)
                    wait_done(dve, a_exp, t)
                    wait_free(dve, a_att, t, 2)
                    for j in range(G):
                        c = slice(j * P, (j + 1) * P)
                        last = v.scalar_tensor_tensor(att[:, r % 2, c], pos[:, r % 2, c], 1.0, neg[:, r % 2, c], ALU.mult,
                                                      ALU.max, accum_out=rsum[:, r, j:j + 1])
                    last.then_inc(a_p, 1)

                def add_d(q, r):
                    t = group(q, r)
                    ld.at(t)
                    ld.then(v.reciprocal(rsum[:, r, :], rsum[:, r, :]))
                    wait_done(dve, a_av, t)
                    wait_loaded(dve, xd_in[r], q)
                    wait_stored(dve, x1_st[r], q)
                    wait_free(dve, a_xn2, t, 4)
                    for j in range(G):
                        last = v.scalar_tensor_tensor(xo[:, r, j * P:(j + 1) * P], psum[5][:, j * P:(j + 1) * P],
                                                      rsum[:, r, j:j + 1], xd[:, r, j * P:(j + 1) * P], ALU.mult, ALU.add)
                    ld2.at(t)
                    ld2.then(last)
                    ln_stats(nc, ld, vt, stats2, mv2[:, r], xo[:, r, :]).then_inc(a_x1, 1)

                ld2 = Links(dve, a_ac, 1)

                def top_e(q, r):
                    t = group(q, r)
                    le.at(t)
                    wait_done(dve, a_gate, t)
                    le.then(v.tensor_tensor(lg[:, :, :], psum[7][:, 0:G * E0].rearrange("p (g c) -> p g c", g=G),
                                            gbias.unsqueeze(1).to_broadcast([P, G, E0]), ALU.add))
                    alone(dve, vt)
                    for j in range(G):
                        last = v.max(top8[:, j, :], lg[:, j, :])
                    le.then(last)
                    alone(dve, vt)
                    for j in range(G):
                        last = v.max_index(idx8[:, j, :], top8[:, j, :], lg[:, j, :])
                    le.then(last)
                    v.tensor_copy(expert[:, bass.ds(t * G, G), :], idx8[:, :, 0:2])
                    v.tensor_copy(top[:, bass.ds(t * G, G), :], top8[:, :, 0:2]).then_inc(a_top, 1)

                steps(dve, [(5, top_e), (4, add_d), (2, p_c), (1, max_b), (0, stats_a)], NG)

            @block.scalar
            def _(act):
                s_ = nc.scalar
                for s in (a_xnT, a_whs, a_attT, a_exp, a_xn2T, a_sign):
                    act.sem_inc(s, CREDIT)

                def xnT_a(q, r):
                    t = group(q, r)
                    wait_done(act, a_tr, t)
                    wait_free(act, a_sc, t, 2)
                    s_.activation(xnT[:, r % 2, :], psum[0][:, :], ACT.Copy).then_inc(a_xnT, 1)
                    wait_done(act, a_wt, t)
                    s_.activation(signs[:, bass.ds(t * 8, 8), :], wt[:, r % 2, :, :], ACT.Sign).then_inc(a_sign, 1)

                def wh_b(q, r):
                    t = group(q, r)
                    wait_done(act, a_wh, t)
                    wait_free(act, a_av, t, 4)
                    for h in range(2):
                        last = s_.activation(wh[:, r, h, :], whp[h][:, 0:2 * (P + 2)], ACT.Copy)
                    last.then_inc(a_whs, 1)

                def exp_c(q, r):
                    t = group(q, r)
                    wait_free(act, a_p, t, 2)
                    wait_done(act, a_max, t)
                    wait_done(act, a_sc, t)
                    for j in range(G):
                        c = slice(j * P, (j + 1) * P)
                        s_.activation(pos[:, r % 2, c], psum[3][:, c], ACT.Exp, bias=shift[:, r, 0, j:j + 1])
                        last = s_.activation(neg[:, r % 2, c], psum[3][:, c], ACT.Exp, bias=shift[:, r, 1, j:j + 1], scale=SLOPE)
                    last.then_inc(a_exp, 1)

                def attT_d(q, r):
                    t = group(q, r)
                    wait_done(act, a_att, t)
                    wait_free(act, a_av, t, 2)
                    s_.activation(attT[:, r % 2, :], psum[4][:, :], ACT.Copy).then_inc(a_attT, 1)

                def xnT_d(q, r):
                    t = group(q, r)
                    wait_done(act, a_tr2, t)
                    wait_free(act, a_gate, t, 2)
                    s_.activation(xn2T[:, r % 2, :], psum[6][:, :], ACT.Copy).then_inc(a_xn2T, 1)

                steps(act, [(5, xnT_d), (3, attT_d), (2, exp_c), (1, wh_b), (0, xnT_a)], NG)

            @block.tensor
            def _(pe):
                mm = nc.tensor.matmul
                for s in (a_tr, a_wh, a_sc, a_att, a_av, a_tr2, a_gate):
                    pe.sem_inc(s, CREDIT)

                def tr_a(q, r):
                    t = group(q, r)
                    wait_done(pe, a_xn, t)
                    wait_free(pe, a_xnT, t, 1)
                    for j in range(G):
                        last = nc.tensor.transpose(psum[0][:, j * P:(j + 1) * P], xn[:, r % 2, j * P:(j + 1) * P], ident[:, :])
                    last.then_inc(a_tr, 1)

                def wh_b(q, r):
                    t = group(q, r)
                    wait_done(pe, a_xnT, t)
                    wait_free(pe, a_whs, t, 1)
                    for j in range(G):
                        c = (j % 2) * (P + 2)
                        last = mm(whp[j // 2][:, c:c + P + 2], xnT[:, r % 2, j * P:(j + 1) * P], Waug[:, :], start=True, stop=True)
                    last.then_inc(a_wh, 1)
                    wait_free(pe, a_exp, t, 1)
                    mm(psum[3][:, :], wa2[:, :], xnT[:, r % 2, :], start=True, stop=False)
                    mm(psum[3][:, :], ident_bf[:, :], mask[:, :].unsqueeze(1).to_broadcast([P, G, P]),
                       start=False, stop=True).then_inc(a_sc, 1)

                def att_c(q, r):
                    t = group(q, r)
                    wait_done(pe, a_p, t)
                    wait_free(pe, a_attT, t, 1)
                    for j in range(G):
                        last = nc.tensor.transpose(psum[4][:, j * P:(j + 1) * P], att[:, r % 2, j * P:(j + 1) * P], ident[:, :])
                    last.then_inc(a_att, 1)

                def av_d(q, r):
                    t = group(q, r)
                    wait_done(pe, a_attT, t)
                    wait_free(pe, a_x1, t, 1)
                    for j in range(G):
                        c = (j % 2) * (P + 2)
                        last = mm(psum[5][:, j * P:(j + 1) * P], attT[:, r % 2, j * P:(j + 1) * P],
                                  wh[:, r, j // 2, c:c + P], start=True, stop=True)
                    last.then_inc(a_av, 1)

                def tr_e(q, r):
                    t = group(q, r)
                    wait_done(pe, a_xn2, t)
                    wait_free(pe, a_xn2T, t, 1)
                    for j in range(G):
                        last = nc.tensor.transpose(psum[6][:, j * P:(j + 1) * P], xn2[:, r, j * P:(j + 1) * P], ident[:, :])
                    last.then_inc(a_tr2, 1)
                    wait_done(pe, a_xn2T, t)
                    wait_free(pe, a_top, t, 1)
                    for j in range(G):
                        last = mm(psum[7][:, j * E0:(j + 1) * E0], xn2T[:, r % 2, j * P:(j + 1) * P], gw_s[:, :],
                                  start=True, stop=True)
                    last.then_inc(a_gate, 1)

                steps(pe, [(5, tr_e), (4, av_d), (3, att_c), (1, wh_b), (0, tr_a)], NG)
        end_stage()
        scope.pop().close()
        scope.pop().close()

        s_w, r_v, r_mm, r_pe = sem("expert_weights"), sem("route_v"), sem("route_counts"), sem("route_list")
        r_oh, r_used = sem("route_onehot"), sem("route_onehot_used")
        r_exp, r_tot, r_last, r_inside = sem("route_exp"), sem("route_totals"), sem("route_last_tile"), sem("route_inside")
        scope.append(ExitStack())
        w12_s, w3_s = sb("w12_s", [P, E0, 2 * HID]), sb("w3_s", [P, E0, HID // P, P])
        tile_token, tile_expert = sb("tile_token", [P, MT], I32), sb("tile_expert", [1, MT], I32)
        scope.append(ExitStack())
        oh = [sb(f"oh{k}", [P, E0, BATCH]) for k in range(2)]
        both, cum, rank = sb("both", [P, E0, BATCH]), sb("cum", [P, E0, BATCH]), sb("rank", [P, E0, BATCH])
        ends, tot, tot_bf = sb("ends", [P, E0 + 1]), sb("tot", [P, E0]), sb("tot_bf", [P, E0], BF16)
        need_i, need, last_tile, off = sb("need_i", [P, E0], I32), sb("need", [P, E0]), sb("last_tile", [P, E0]), sb("off", [P, E0])
        endcol, inside = sb("endcol", [E0, 1]), sb("inside", [E0, MT], BF16)
        slot_f = sb("slot_f", [P, BATCH, 2])
        lo_i, hi_i = sb("lo_i", [P, BATCH, 2], I32), sb("hi_i", [P, BATCH, 2], I32)
        lo, hi = sb("lo", [P, BATCH, 2]), sb("hi", [P, BATCH, 2])
        lo_row, lo_graph, hi_is = sb("lo_row", [P, 4, 2, P], BF16), sb("lo_graph", [P, 4, 2, P], BF16), sb("hi_is", [P, 4, 2, MT], BF16)
        pairs = psum[3]
        with nc.Block() as block:
            @block.sync
            def _(sp):
                sp.dma_start(w12_s[:, :, :], w12).then_inc(s_w, 16)
                sp.dma_start(w3_s[:, :, :, :], w3).then_inc(s_w, 16)
                sp.wait_ge(s_w, 32)

            @block.scalar
            def _(act):
                act.wait_ge(r_v, 1)
                nc.scalar.activation(share[:, :, 1], top[:, :, 1], ACT.Exp).then_inc(r_exp, 1)

            @block.vector
            def _(dve):
                v = nc.vector
                dve.sem_inc(r_oh, CREDIT)
                link = Links(dve, r_v)
                link.then(v.tensor_tensor(top[:, :, 1], top[:, :, 1], top[:, :, 0], ALU.subtract))
                for k in range(2):
                    v.tensor_tensor(oh[k][:, :, :], count[:, 0:E0].unsqueeze(2).to_broadcast([P, E0, BATCH]),
                                    expert[:, :, k].unsqueeze(1).to_broadcast([P, E0, BATCH]), ALU.is_equal)
                v.memset(ends[:, 0:1], 0.0)
                dve.wait_ge(r_exp, 1)
                link.then(v.tensor_scalar(share[:, :, 0], share[:, :, 1], 1.0, None, ALU.add))
                link.then(v.reciprocal(share[:, :, 0], share[:, :, 0]))
                v.tensor_tensor(share[:, :, 1], share[:, :, 1], share[:, :, 0], ALU.mult)
                link.then(v.tensor_tensor(both[:, :, :], oh[0][:, :, :], oh[1][:, :, :], ALU.add))
                flat = both[:, :, :].rearrange("p e b -> p (e b)")
                link.then(v.tensor_tensor_scan(cum[:, :, :].rearrange("p e b -> p (e b)"), flat, flat, 0.0, ALU.add, ALU.max))
                link.then(v.tensor_copy(ends[:, 1:], cum[:, :, BATCH - 1]))
                link.then(v.tensor_tensor(tot[:, :], ends[:, 1:], ends[:, 0:E0], ALU.subtract))
                v.tensor_copy(tot_bf[:, :], tot[:, :]).then_inc(r_tot, 1)
                dve.wait_ge(r_mm, 1)
                link.then(v.tensor_scalar(need[:, :], psum[0][:, E0:2 * E0], float(P - 1), None, ALU.add))
                link.then(v.tensor_copy(need_i[:, :], need[:, :]))
                link.then(v.tensor_scalar(need_i[:, :], need_i[:, :], 7, None, ALU.arith_shift_right))
                link.then(v.tensor_copy(need[:, :], need_i[:, :]))
                v.tensor_tensor_scan(last_tile[:, :], need[:, :], need[:, :], 0.0, ALU.add, ALU.max).then_inc(r_last, 1)
                dve.wait_ge(r_last, 1)
                link.then(v.tensor_tensor(off[:, :], last_tile[:, :], need[:, :], ALU.subtract))
                link.then(v.tensor_scalar(off[:, :], off[:, :], float(P), None, ALU.mult))
                link.then(v.tensor_tensor(off[:, :], off[:, :], psum[0][:, 0:E0], ALU.add))
                v.tensor_tensor(rank[:, :, :], cum[:, :, :], both[:, :, :], ALU.subtract)
                link.then(v.tensor_tensor(off[:, :], off[:, :], ends[:, 0:E0], ALU.subtract))
                link.then(v.tensor_tensor(rank[:, :, :], rank[:, :, :], off[:, :].unsqueeze(2).to_broadcast([P, E0, BATCH]), ALU.add))
                for k in range(2):
                    link.then(v.tensor_tensor(oh[k][:, :, :], oh[k][:, :, :], rank[:, :, :], ALU.mult))
                    link.then(v.tensor_reduce(slot_f[:, :, k], oh[k][:, :, :].rearrange("p e b -> p b e"), AX.X, ALU.add))
                link.then(v.tensor_copy(slot[:, :, :], slot_f[:, :, :]))
                v.tensor_scalar(lo_i[:, :, :], slot[:, :, :], P - 1, None, ALU.bitwise_and)
                link.then(v.tensor_scalar(hi_i[:, :, :], slot[:, :, :], 7, None, ALU.arith_shift_right))
                v.tensor_copy(lo[:, :, :], lo_i[:, :, :])
                link.then(v.tensor_copy(hi[:, :, :], hi_i[:, :, :]))
                link.then(v.tensor_scalar(hi[:, :, :], hi[:, :, :], float(MT // 2), None, ALU.subtract))

                dve.wait_ge(r_mm, 2)
                link.then(v.tensor_copy(endcol[:, :], psum[1][0:E0, 0:1]))
                v.tensor_scalar(inside[:, :], count[0:E0, 0:MT], endcol[:, :], None, ALU.is_ge).then_inc(r_inside, 1)
                dve.wait_ge(r_mm, 3)
                link.then(v.tensor_scalar(tile_expert[:, :], psum[2][0:1, 0:MT], float(E0 - 1), None, ALU.min))

                def onehots(q, r):
                    t = group(q, r)
                    wait_free(dve, r_used, t, 4)
                    for k in range(2):
                        v.tensor_scalar(lo_row[:, r, k, :], count_bf[:, 0:P], lo[:, bass.ds(t, 1), k], row_id[:, :],
                                        ALU.is_equal, ALU.mult)
                        v.tensor_scalar(lo_graph[:, r, k, :], count_bf[:, 0:P], lo[:, bass.ds(t, 1), k],
                                        count[:, bass.ds(t, 1)], ALU.is_equal, ALU.mult)
                        last = v.tensor_scalar(hi_is[:, r, k, :], tile_bf[:, :], hi[:, bass.ds(t, 1), k], None, ALU.is_equal)
                    last.then_inc(r_oh, 1)

                steps(dve, [(0, onehots)], BATCH)
                dve.wait_ge(r_pe, 1)
                link.then(v.tensor_copy(tile_token[:, :], pairs[:, 0:MT]))

            @block.tensor
            def _(pe):
                mm = nc.tensor.matmul
                pe.sem_inc(r_used, CREDIT)
                pe.wait_ge(r_tot, 1)
                mm(psum[0][:, 0:E0], before[:, :], tot_bf[:, :], start=True, stop=True)
                mm(psum[0][:, E0:2 * E0], ones_bf[:, :], tot_bf[:, :], start=True, stop=True).then_inc(r_mm, 1)
                pe.wait_ge(r_last, 1)
                nc.tensor.transpose(psum[1][0:E0, 0:P], last_tile[:, :], ident[:, :]).then_inc(r_mm, 1)
                pe.wait_ge(r_inside, 1)
                mm(psum[2][0:1, 0:MT], ones_bf[0:E0, 0:1], inside[:, :], start=True, stop=True).then_inc(r_mm, 1)

                mm(pairs[:, 0:MT], zeros_bf[:, :], tile_bf[:, :], start=True, stop=False)

                def fill(q, r):
                    wait_done(pe, r_oh, group(q, r))
                    for k in range(2):
                        mm(pairs[:, 0:MT], lo_row[:, r, k, :], hi_is[:, r, k, :], start=False, stop=False)
                        last = mm(pairs[:, 0:MT], lo_graph[:, r, k, :], hi_is[:, r, k, :], start=False, stop=False)
                    last.then_inc(r_used, 1)

                steps(pe, [(0, fill)], BATCH)
                mm(pairs[:, 0:MT], zeros_bf[:, :], tile_bf[:, :], start=False, stop=True).then_inc(r_pe, 1)
        end_stage()
        scope.pop().close()

        g_in, y_st = sems("g_in"), sems("y_st")
        m_ix, m_tr, m_xT, m_h, m_silu, m_hid = sem("m_index"), sem("m_transposed"), sem("m_xT"), sem("m_h"), sem("m_silu"), sem("m_hid")
        m_trh, m_hT, m_y, m_yo = sem("m_hid_transposed"), sem("m_hidT"), sem("m_y"), sem("m_y_copied")
        scope.append(ExitStack())
        ix = sb("ix", [P, 4], I32)
        xg, xgT = sb("xg", [P, 4, P]), sb("xgT", [P, 4, P])
        gate, hid, hidT, yo = sb("gate", [P, 4, HID]), sb("hid", [P, 4, HID]), sb("hidT", [P, 4, HID]), sb("yo", [P, 4, P])
        bx, bh, bt, by = [psum[0], psum[7]], [psum[1], psum[2]], [psum[3], psum[4]], [psum[5], psum[6]]
        with nc.Block() as block:
            @block.gpsimd
            def _(pool):
                pool.sem_inc(m_ix, CREDIT)

                def gather(q, r):
                    t = group(q, r)
                    wait_free(pool, m_tr, t, 4)
                    alone(pool, pt)
                    pool.tensor_copy(ix[:, r:r + 1], tile_token[:, bass.ds(t, 1)]).then_inc(m_ix, 1)
                    wait_done(pool, m_ix, t)
                    alone(pool, pt)
                    pool.indirect_dma_start(xg[:, r, :], None, xn_d, bass.IndirectOffsetOnAxis(ap=ix[:, r:r + 1], axis=0)).then_inc(g_in[r], 16)

                steps(pool, [(0, gather)], MT)

            @block.tensor
            def _(pe):
                mm = nc.tensor.matmul
                for s in (m_tr, m_h, m_trh, m_y):
                    pe.sem_inc(s, CREDIT)

                def expert_of(t):
                    return pe.value_load(tile_expert[0:1, bass.ds(t, 1)], min_val=0, max_val=E0 - 1)

                def tr(q, r):
                    t = group(q, r)
                    wait_loaded(pe, g_in[r], q)
                    wait_free(pe, m_xT, t, 2)
                    nc.tensor.transpose(bx[r % 2][:, 0:P], xg[:, r, :], ident[:, :]).then_inc(m_tr, 1)

                def up(q, r):
                    t = group(q, r)
                    e = expert_of(t)
                    wait_done(pe, m_xT, t)
                    wait_free(pe, m_hid, t, 2)
                    mm(bh[r % 2][:, :], xgT[:, r, :], w12_s[:, bass.ds(e, 1), :].rearrange("p a c -> p (a c)"),
                       start=True, stop=True).then_inc(m_h, 1)

                def tr_hid(q, r):
                    t = group(q, r)
                    wait_done(pe, m_hid, t)
                    wait_free(pe, m_hT, t, 2)
                    for c in range(HID // P):
                        last = nc.tensor.transpose(bt[r % 2][:, c * P:(c + 1) * P], hid[:, r, c * P:(c + 1) * P], ident[:, :])
                    last.then_inc(m_trh, 1)

                def down(q, r):
                    t = group(q, r)
                    e = expert_of(t)
                    wait_done(pe, m_hT, t)
                    wait_free(pe, m_yo, t, 2)
                    for c in range(HID // P):
                        last = mm(by[r % 2][:, 0:P], hidT[:, r, c * P:(c + 1) * P],
                                  w3_s[:, bass.ds(e, 1), c, :].rearrange("p a c -> p (a c)"), start=c == 0, stop=c == HID // P - 1)
                    last.then_inc(m_y, 1)

                steps(pe, [(4, down), (3, tr_hid), (1, up), (0, tr)], MT)

            @block.scalar
            def _(act):
                for s in (m_xT, m_silu, m_yo):
                    act.sem_inc(s, CREDIT)

                def xT(q, r):
                    t = group(q, r)
                    wait_done(act, m_tr, t)
                    wait_free(act, m_h, t, 4)
                    nc.scalar.activation(xgT[:, r, :], bx[r % 2][:, 0:P], ACT.Copy).then_inc(m_xT, 1)

                def silu(q, r):
                    t = group(q, r)
                    wait_done(act, m_h, t)
                    wait_free(act, m_hid, t, 4)
                    nc.scalar.activation(gate[:, r, :], bh[r % 2][:, 0:HID], ACT.Silu).then_inc(m_silu, 1)

                def y(q, r):
                    t = group(q, r)
                    wait_done(act, m_y, t)
                    wait_stored(act, y_st[r], q)
                    nc.scalar.activation(yo[:, r, :], by[r % 2][:, 0:P], ACT.Copy).then_inc(m_yo, 1)

                steps(act, [(4, y), (1, silu), (0, xT)], MT)

            @block.vector
            def _(dve):
                for s in (m_hid, m_hT):
                    dve.sem_inc(s, CREDIT)

                def mul(q, r):
                    t = group(q, r)
                    wait_done(dve, m_silu, t)
                    wait_free(dve, m_trh, t, 4)
                    nc.vector.tensor_tensor(hid[:, r, :], gate[:, r, :], bh[r % 2][:, HID:2 * HID], ALU.mult).then_inc(m_hid, 1)

                def hT(q, r):
                    t = group(q, r)
                    wait_done(dve, m_trh, t)
                    wait_free(dve, m_y, t, 4)
                    nc.vector.tensor_copy(hidT[:, r, :], bt[r % 2][:, 0:HID]).then_inc(m_hT, 1)

                steps(dve, [(3, hT), (1, mul)], MT)

            @block.sync
            def _(sp):
                for r in range(4):
                    sp.sem_inc(y_st[r], 16)

                def store(q, r):
                    t = group(q, r)
                    wait_done(sp, m_yo, t)
                    sp.dma_start(y_d[bass.ds(t * P, P), :], yo[:, r, :]).then_inc(y_st[r], 16)

                steps(sp, [(0, store)], MT)
                for r in range(4):
                    sp.wait_ge(y_st[r], 16 * (MT // 4 + 1))
        end_stage()
        scope.pop().close()
        scope.pop().close()

        c_x1, c_y, c_x3, c_sx = sems("c_x1"), sems("c_y"), sems("c_x3"), sems("c_sx")
        (c_ix, c_x2, c_p1, c_xn, c_tr, c_xnT, c_z, c_zs, c_h1, c_h1T, c_z2, c_z2s, c_h2, c_rl, c_xm, c_x3r, c_p2, c_xn4, c_sgn,
         c_tr4, c_xn4T, c_gate, c_oh, c_cntA, c_cntB, c_rkA, c_rkB, c_cnt) = [sem("c_" + n) for n in (
             "index x2 rstd xn transposed xnT z z_copied h1 h1T z2 z2_copied h2 relu xm x3 rstd3 xn3 sign transposed3 xn3T "
             "gate onehot countA countB rankA rankB counts").split()]
        c_vx, c_vs, c_vy, c_vp, c_pa, c_pb, c_v0 = [sem("c_link%d" % i) for i in range(7)]
        scope.append(ExitStack())
        pat = sb("pat", [P, BATCH])
        rank1 = sb("rank1", [P, BATCH])
        scope.append(ExitStack())
        ix8 = sb("ix8", [P, 4, G * 2], I32)
        xa, yg = sb("c_xa", [P, 4, GW]), sb("yg", [P, 4, G * 2, P])
        t1, x2 = sb("t1", [P, GW]), sb("x2", [P, 4, GW])
        stats, mv, ve, nb = sb("stats", [P, G, 6]), sb("mv", [P, 4, G, 2]), sb("ve", [P, 4, G]), sb("nb", [P, 4, G])
        stats3, mv3, ve3, nb3 = sb("stats3", [P, G, 6]), sb("mv3", [P, 4, G, 2]), sb("ve3", [P, 4, G]), sb("nb3", [P, 4, G])
        xn, xnT, xm = sb("xn", [P, 4, GW]), sb("xnT", [P, 2, GW]), sb("xm", [P, 4, GW])
        zs, h1T, z2s, rl = sb("zs", [P, 2, GW]), sb("h1T", [P, 2, GW]), sb("z2s", [P, 2, GW]), sb("rl", [P, 2, GW])
        x3, xn4, xn4T, sx = sb("x3", [P, 4, GW]), sb("xn4", [P, 2, GW]), sb("xn4T", [P, 2, GW]), sb("sx", [P, 4, GW], BF16)
        zb, gbit = sb("zb", [P, G, E1]), sb("gbit", [P, G, E1])
        oh = sb("oh", [P, 4, G, PAT], BF16)
        junk = sb("junk", [P, G, PAT], BF16)
        bT, bZ, bH1, bZ2, bH2, bT4, bG, bR = psum
        with nc.Block() as block:
            @block.sync
            def _(sp):
                for r in range(4):
                    sp.sem_inc(c_x3[r], 16)
                    sp.sem_inc(c_sx[r], 16)

                def load(q, r):
                    t = group(q, r)
                    wait_free(sp, c_x2, t, 4)
                    alone(sp, ticks["sync"])
                    sp.dma_start(xa[:, r, :], x1_d[:, bass.ds(t * GW, GW)]).then_inc(c_x1[r], 16)

                def store_x(q, r):
                    t = group(q, r)
                    wait_done(sp, c_x3r, t)
                    alone(sp, ticks["sync"])
                    sp.dma_start(x2_d[:, bass.ds(t * GW, GW)], x3[:, r, :]).then_inc(c_x3[r], 16)

                def store_s(q, r):
                    t = group(q, r)
                    wait_done(sp, c_sgn, t)
                    alone(sp, ticks["sync"])
                    sp.dma_start(sx_v[:, bass.ds(t * GW, GW)], sx[:, r, :]).then_inc(c_sx[r], 16)

                steps(sp, [(0, load), (10, store_x), (12, store_s)], NG)
                for r in range(4):
                    sp.wait_ge(c_x3[r], 16 * (NG // 4 + 1))
                    sp.wait_ge(c_sx[r], 16 * (NG // 4 + 1))

            @block.gpsimd
            def _(pool):
                for s in (c_ix, c_p1, c_p2):
                    pool.sem_inc(s, CREDIT)
                la, lb = Links(pool, c_pa, 3), Links(pool, c_pb, 3)

                def gather(q, r):
                    t = group(q, r)
                    wait_free(pool, c_x2, t, 4)
                    alone(pool, pt)
                    pool.tensor_copy(ix8[:, r, :], slot[:, bass.ds(t * G, G), :].rearrange("p g k -> p (g k)")).then_inc(c_ix, 1)
                    wait_done(pool, c_ix, t)
                    alone(pool, pt)
                    for c in range(2 * G):
                        pool.indirect_dma_start(yg[:, r, c, :], None, y_d,
                                                bass.IndirectOffsetOnAxis(ap=ix8[:, r, c:c + 1], axis=0)).then_inc(c_y[r], 16)

                def rstd(link, have, free, mv_, ve_, nb_, done):
                    def work(q, r):
                        t = group(q, r)
                        link.at(t)
                        wait_done(pool, have, t)
                        wait_free(pool, free, t, 4)
                        alone(pool, pt)
                        link.then(pool.tensor_scalar(ve_[:, r, :], mv_[:, r, :, 1], EPS, None, ALU.add))
                        link.then(pool.tensor_tensor(ve_[:, r, :], ve_[:, r, :], mhalf[:, :], ALU.pow))
                        link.then(pool.tensor_tensor(nb_[:, r, :], mv_[:, r, :, 0], ve_[:, r, :], ALU.mult))
                        alone(pool, pt)
                        pool.tensor_scalar(nb_[:, r, :], nb_[:, r, :], -1.0, None, ALU.mult).then_inc(done, 1)
                    return work

                steps(pool, [(9, rstd(lb, c_x3r, c_xn4, mv3, ve3, nb3, c_p2)), (2, rstd(la, c_x2, c_xn, mv, ve, nb, c_p1)),
                             (0, gather)], NG)

            @block.vector
            def _(dve):
                v = nc.vector
                for s in (c_x2, c_xm, c_x3r, c_oh, c_rkA, c_rkB, c_z2s):
                    dve.sem_inc(s, CREDIT)
                lx, ly, lp = Links(dve, c_vx, 3), Links(dve, c_vy, 2), Links(dve, c_vp, 3)

                def combine(q, r):
                    t = group(q, r)
                    lx.at(t)
                    wait_loaded(dve, c_x1[r], q)
                    wait_loaded(dve, c_y[r], q, 2 * G)
                    wait_free(dve, c_xm, t, 4)
                    alone(dve, vt)
                    for k in range(2):
                        for j in range(G):
                            c = slice(j * P, (j + 1) * P)
                            last = v.scalar_tensor_tensor(t1[:, c] if k == 0 else x2[:, r, c], yg[:, r, 2 * j + k, :],
                                                          share[:, bass.ds(t * G + j, 1), k],
                                                          xa[:, r, c] if k == 0 else t1[:, c], ALU.mult, ALU.add)
                        lx.then(last)
                    alone(dve, vt)
                    ln_stats(nc, lx, vt, stats, mv[:, r], x2[:, r, :]).then_inc(c_x2, 1)

                def half(q, r):
                    t = group(q, r)
                    wait_done(dve, c_xn, t)
                    wait_free(dve, c_x3r, t, 4)
                    v.scalar_tensor_tensor(xm[:, r, :], xn[:, r, :], 0.5, x2[:, r, :], ALU.mult, ALU.add).then_inc(c_xm, 1)

                def copy_z2(q, r):
                    t = group(q, r)
                    wait_done(dve, c_z2, t)
                    wait_free(dve, c_h2, t, 2)
                    v.tensor_copy(z2s[:, r % 2, :], bZ2[:, :]).then_inc(c_z2s, 1)

                def add_x3(q, r):
                    t = group(q, r)
                    ly.at(t)
                    wait_done(dve, c_rl, t)
                    wait_stored(dve, c_x3[r], q)
                    wait_free(dve, c_xn4, t, 4)
                    ly.then(v.tensor_tensor(x3[:, r, :], xm[:, r, :], rl[:, r % 2, :], ALU.add))
                    alone(dve, vt)
                    ln_stats(nc, ly, vt, stats3, mv3[:, r], x3[:, r, :]).then_inc(c_x3r, 1)

                def patterns(q, r):
                    t = group(q, r)
                    lp.at(t)
                    wait_done(dve, c_gate, t)
                    lp.then(v.tensor_tensor(zb[:, :, :], bG[:, 0:G * E1].rearrange("p (g e) -> p g e", g=G),
                                            pbias.unsqueeze(1).to_broadcast([P, G, E1]), ALU.add))
                    lp.then(v.scalar_tensor_tensor(gbit[:, :, :], zb[:, :, :], 0.0, bits[:, :].unsqueeze(1).to_broadcast([P, G, E1]),
                                                   ALU.is_gt, ALU.mult))
                    lp.then(v.tensor_reduce(pat[:, bass.ds(t * G, G)], gbit[:, :, :], AX.X, ALU.add))
                    wait_free(dve, c_cntA, t, 3)
                    alone(dve, vt)
                    for j in range(G):
                        last = v.tensor_scalar(oh[:, r, j, :], count_bf[:, :], pat[:, bass.ds(t * G + j, 1)], None, ALU.is_equal)
                    last.then_inc(c_oh, 1)

                def ranks(h, counted, done):
                    def work(q, r):
                        t = group(q, r)
                        wait_done(dve, counted, t)
                        alone(dve, vt)
                        for j in range(2):
                            g = t * G + 2 * h + j
                            last = v.scalar_tensor_tensor(junk[:, 2 * h + j, :], count[:, 0:PAT], pat[:, bass.ds(g, 1)],
                                                          bR[:, j * PAT:(j + 1) * PAT], ALU.is_equal, ALU.mult,
                                                          accum_out=rank1[:, bass.ds(g, 1)])
                        last.then_inc(done, 1)
                    return work

                v.memset(oh[:, 3, 2, :], 0.0).then_inc(c_v0, 1)
                v.memset(oh[:, 3, 3, :], 0.0).then_inc(c_v0, 1)
                steps(dve, [(13, ranks(0, c_cntA, c_rkA)), (8, add_x3), (7, copy_z2), (4, half), (13, ranks(1, c_cntB, c_rkB)),
                            (12, patterns), (1, combine)], NG)

            @block.scalar
            def _(act):
                s_ = nc.scalar
                for s in (c_xn, c_xnT, c_zs, c_h1T, c_rl, c_xn4, c_sgn, c_xn4T):
                    act.sem_inc(s, CREDIT)

                def norm(q, r):
                    t = group(q, r)
                    wait_done(act, c_p1, t)
                    wait_free(act, c_tr, t, 4)
                    wait_free(act, c_xm, t, 4)
                    for j in range(G):
                        c = slice(j * P, (j + 1) * P)
                        last = s_.activation(xn[:, r, c], x2[:, r, c], ACT.Identity, bias=nb[:, r, j:j + 1], scale=ve[:, r, j:j + 1])
                    last.then_inc(c_xn, 1)

                def copy_T(q, r):
                    t = group(q, r)
                    wait_done(act, c_tr, t)
                    wait_free(act, c_h1, t, 2)
                    s_.activation(xnT[:, r % 2, :], bT[:, :], ACT.Copy).then_inc(c_xnT, 1)

                def copy_z(q, r):
                    t = group(q, r)
                    wait_done(act, c_z, t)
                    wait_free(act, c_h1, t, 2)
                    s_.activation(zs[:, r % 2, :], bZ[:, :], ACT.Copy).then_inc(c_zs, 1)

                def relu1(q, r):
                    t = group(q, r)
                    wait_done(act, c_h1, t)
                    wait_free(act, c_h2, t, 2)
                    s_.activation(h1T[:, r % 2, :], bH1[:, :], ACT.Relu, bias=b1_s[:, :]).then_inc(c_h1T, 1)

                def relu2(q, r):
                    t = group(q, r)
                    wait_done(act, c_h2, t)
                    wait_free(act, c_x3r, t, 2)
                    s_.activation(rl[:, r % 2, :], bH2[:, :], ACT.Relu, scale=0.5).then_inc(c_rl, 1)

                def norm4(q, r):
                    t = group(q, r)
                    wait_done(act, c_p2, t)
                    wait_free(act, c_tr4, t, 2)
                    for j in range(G):
                        c = slice(j * P, (j + 1) * P)
                        last = s_.activation(xn4[:, r % 2, c], x3[:, r, c], ACT.Identity, bias=nb3[:, r, j:j + 1], scale=ve3[:, r, j:j + 1])
                    last.then_inc(c_xn4, 1)
                    wait_done(act, c_xn4, t)
                    wait_stored(act, c_sx[r], q)
                    s_.activation(sx[:, r, :], xn4[:, r % 2, :], ACT.Sign).then_inc(c_sgn, 1)

                def copy_T4(q, r):
                    t = group(q, r)
                    wait_done(act, c_tr4, t)
                    wait_free(act, c_gate, t, 2)
                    s_.activation(xn4T[:, r % 2, :], bT4[:, :], ACT.Copy).then_inc(c_xn4T, 1)

                steps(act, [(8, relu2), (11, copy_T4), (6, relu1), (5, copy_z), (4, copy_T), (10, norm4), (3, norm)], NG)

            @block.tensor
            def _(pe):
                mm = nc.tensor.matmul
                for s in (c_tr, c_z, c_h1, c_z2, c_h2, c_tr4, c_gate, c_cntA, c_cntB):
                    pe.sem_inc(s, CREDIT)

                def cols(j):
                    return slice(j * P, (j + 1) * P)

                def tr(q, r):
                    t = group(q, r)
                    wait_done(pe, c_xn, t)
                    wait_free(pe, c_xnT, t, 1)
                    for j in range(G):
                        last = nc.tensor.transpose(bT[:, cols(j)], xn[:, r, cols(j)], ident[:, :])
                    last.then_inc(c_tr, 1)

                def first(q, r):
                    t = group(q, r)
                    wait_done(pe, c_xnT, t)
                    wait_free(pe, c_zs, t, 1)
                    for j in range(G):
                        last = mm(bZ[:, cols(j)], xnT[:, r % 2, cols(j)], w1n_s[:, :], start=True, stop=True)
                    last.then_inc(c_z, 1)

                def neigh1(q, r):
                    t = group(q, r)
                    wait_done(pe, c_zs, t)
                    wait_free(pe, c_h1T, t, 1)
                    mm(bH1[:, :], w1l_s[:, :], xnT[:, r % 2, :], start=True, stop=False)
                    for j in range(G):
                        last = mm(bH1[:, cols(j)], zs[:, r % 2, cols(j)], adjT_s[:, :], start=False, stop=j == G - 1)
                    last.then_inc(c_h1, 1)

                def second(q, r):
                    t = group(q, r)
                    wait_done(pe, c_h1T, t)
                    wait_free(pe, c_z2s, t, 1)
                    for j in range(G):
                        last = mm(bZ2[:, cols(j)], h1T[:, r % 2, cols(j)], w2n_s[:, :], start=True, stop=True)
                    last.then_inc(c_z2, 1)

                def neigh2(q, r):
                    t = group(q, r)
                    wait_done(pe, c_z2s, t)
                    wait_free(pe, c_rl, t, 1)
                    mm(bH2[:, :], ones_row[:, :], b2x[:, :], start=True, stop=False)
                    for j in range(G):
                        mm(bH2[:, cols(j)], h1T[:, r % 2, cols(j)], w2l_s[:, :], start=False, stop=False)
                    mm(bH2[:, :], adjT_s[:, :], z2s[:, r % 2, :], start=False, stop=True).then_inc(c_h2, 1)

                def tr4(q, r):
                    t = group(q, r)
                    wait_done(pe, c_xn4, t)
                    wait_free(pe, c_xn4T, t, 1)
                    for j in range(G):
                        last = nc.tensor.transpose(bT4[:, cols(j)], xn4[:, r % 2, cols(j)], ident[:, :])
                    last.then_inc(c_tr4, 1)

                def gates(q, r):
                    t = group(q, r)
                    wait_done(pe, c_xn4T, t)
                    wait_free(pe, c_oh, t, 1)
                    for j in range(G):
                        last = mm(bG[:, j * E1:(j + 1) * E1], xn4T[:, r % 2, cols(j)], projT_s[:, :], start=True, stop=True)
                    last.then_inc(c_gate, 1)

                def counts(r_was, h_was, r, h):
                    a, b, c, d = oh[:, r_was, 2 * h_was, :], oh[:, r_was, 2 * h_was + 1, :], oh[:, r, 2 * h, :], oh[:, r, 2 * h + 1, :]
                    for to, mine, whole, new in ((0, a, b, c), (1, b, c, d)):
                        reg = bR[:, to * PAT:(to + 1) * PAT]
                        mm(reg, not_before[:, :], mine, start=False, stop=False, skip_group_check=True)
                        mm(reg, ones_bf[:, :], whole, start=False, stop=False, skip_group_check=True)
                        last = mm(reg, before[:, :], new, start=False, stop=True, skip_group_check=True)
                    return last

                def countA(q, r):
                    t = group(q, r)
                    wait_done(pe, c_oh, t)
                    wait_free(pe, c_rkB, t, 1)
                    counts((r + 3) % 4, 1, r, 0).then_inc(c_cntA, 1)

                def countB(q, r):
                    t = group(q, r)
                    wait_done(pe, c_rkA, t)
                    counts(r, 0, r, 1).then_inc(c_cntB, 1)

                pe.wait_ge(c_v0, 2)
                mm(bR[:, :], zeros_bf[:, :], oh[:, 3, 2:4, :], start=True, stop=True, skip_group_check=True)
                steps(pe, [(13, countA), (7, neigh2), (6, second), (13, countB), (5, neigh1), (11, gates), (4, first), (10, tr4),
                           (3, tr)], NG)
                pe.wait_ge(c_rkB, NG + CREDIT)
                mm(bR[:, 0:PAT], not_before[:, :], oh[:, 3, 2, :], start=False, stop=False, skip_group_check=True)
                mm(bR[:, 0:PAT], ones_bf[:, :], oh[:, 3, 3, :], start=False, stop=True, skip_group_check=True).then_inc(c_cnt, 1)
        end_stage()
        scope.pop().close()

        d_v, d_mm, d_last, d_in, d_oh, d_used, d_pe = [sem("d_" + n) for n in "link mm last_block inside onehot used list".split()]
        d_st = sem("d_start_of")
        slot1 = sb("slot1", [P, BATCH], I32)
        tile_src, block_pat = sb("tile_src", [P, PT], I32), sb("block_pat", [1, NB * PT], I32)
        scope.append(ExitStack())
        need_i, need, last_b = sb("need_i", [P, PAT], I32), sb("need", [P, PAT]), sb("last_b", [P, PAT])
        start, endcol = sb("start", [P, PAT]), sb("endcol", [P, 2])
        inside = sb("inside", [P, 2, NB * PT], BF16)
        start_of, slot_f = sb("start_of", [P, BATCH]), sb("slot_f", [P, BATCH])
        lo_i, hi_i, lo, hi = sb("lo_i", [P, BATCH], I32), sb("hi_i", [P, BATCH], I32), sb("lo", [P, BATCH]), sb("hi", [P, BATCH])
        lo_row, lo_graph, hi_is = sb("lo_row", [P, 4, P], BF16), sb("lo_graph", [P, 4, P], BF16), sb("hi_is", [P, 4, PT], BF16)
        junk = sb("junk", [P, 4, PAT], BF16)
        HB = NB * PT // 2
        with nc.Block() as block:
            @block.vector
            def _(dve):
                v = nc.vector
                dve.sem_inc(d_oh, CREDIT)
                dve.sem_inc(d_st, CREDIT)
                link = Links(dve, d_v)
                counted = psum[7][:, 0:PAT]
                link.then(v.tensor_scalar(need[:, :], counted, float(PB - 1), None, ALU.add))
                link.then(v.tensor_copy(need_i[:, :], need[:, :]))
                link.then(v.tensor_scalar(need_i[:, :], need_i[:, :], 5, None, ALU.arith_shift_right))
                link.then(v.tensor_copy(need[:, :], need_i[:, :]))
                v.tensor_tensor_scan(last_b[:, :], need[:, :], need[:, :], 0.0, ALU.add, ALU.max).then_inc(d_last, 1)
                dve.wait_ge(d_last, 1)
                link.then(v.tensor_tensor(start[:, :], last_b[:, :], need[:, :], ALU.subtract))
                link.then(v.tensor_scalar(start[:, :], start[:, :], float(PB), None, ALU.mult))
                dve.wait_ge(d_mm, 1)
                for h in range(2):
                    last = v.tensor_copy(endcol[:, h:h + 1], psum[0][:, h * P:h * P + 1])
                link.then(last)
                for h in range(2):
                    last = v.tensor_scalar(inside[:, h, :], count[:, :], endcol[:, h:h + 1], None, ALU.is_ge)
                last.then_inc(d_in, 1)

                def starts(q, r):
                    t = group(q, r)
                    wait_free(dve, d_st, t, 4)
                    alone(dve, vt)
                    v.scalar_tensor_tensor(junk[:, r, :], count[:, 0:PAT], pat[:, bass.ds(t, 1)], start[:, :],
                                                  ALU.is_equal, ALU.mult, accum_out=start_of[:, bass.ds(t, 1)]).then_inc(d_st, 1)

                steps(dve, [(0, starts)], BATCH)
                dve.wait_ge(d_st, BATCH + CREDIT)
                link.then(v.tensor_tensor(slot_f[:, :], start_of[:, :], rank1[:, :], ALU.add))
                link.then(v.tensor_copy(slot1[:, :], slot_f[:, :]))
                v.tensor_scalar(lo_i[:, :], slot1[:, :], P - 1, None, ALU.bitwise_and)
                link.then(v.tensor_scalar(hi_i[:, :], slot1[:, :], 7, None, ALU.arith_shift_right))
                v.tensor_copy(lo[:, :], lo_i[:, :])
                link.then(v.tensor_copy(hi[:, :], hi_i[:, :]))
                dve.wait_ge(d_mm, 2)
                for h in range(2):
                    last = v.tensor_scalar(block_pat[:, h * HB:(h + 1) * HB], psum[1 + h][0:1, 0:HB], float(PAT - 1), None, ALU.min)
                link.then(last)

                def onehots(q, r):
                    t = group(q, r)
                    wait_free(dve, d_used, t, 4)
                    v.tensor_scalar(lo_row[:, r, :], count_bf[:, 0:P], lo[:, bass.ds(t, 1)], row_id[:, :], ALU.is_equal, ALU.mult)
                    v.tensor_scalar(lo_graph[:, r, :], count_bf[:, 0:P], lo[:, bass.ds(t, 1)], count[:, bass.ds(t, 1)],
                                    ALU.is_equal, ALU.mult)
                    v.tensor_scalar(hi_is[:, r, :], count_bf[:, 0:PT], hi[:, bass.ds(t, 1)], None, ALU.is_equal).then_inc(d_oh, 1)

                steps(dve, [(0, onehots)], BATCH)
                dve.wait_ge(d_pe, 1)
                link.then(v.tensor_copy(tile_src[:, :], psum[3][:, 0:PT]))

            @block.tensor
            def _(pe):
                mm = nc.tensor.matmul
                pe.sem_inc(d_used, CREDIT)
                pe.wait_ge(d_last, 1)
                for h in range(2):
                    last = nc.tensor.transpose(psum[0][:, h * P:(h + 1) * P], last_b[:, h * P:(h + 1) * P], ident[:, :])
                last.then_inc(d_mm, 1)
                pe.wait_ge(d_in, 1)
                for h in range(2):
                    for k in range(2):
                        last = mm(psum[1 + h][0:1, 0:HB], ones_bf[:, 0:1], inside[:, k, h * HB:(h + 1) * HB], start=k == 0, stop=k == 1)
                last.then_inc(d_mm, 1)
                rows_of = psum[3][:, 0:PT]
                mm(rows_of, zeros_bf[:, :], count_bf[:, 0:PT], start=True, stop=False)

                def fill(q, r):
                    wait_done(pe, d_oh, group(q, r))
                    mm(rows_of, lo_row[:, r, :], hi_is[:, r, :], start=False, stop=False)
                    mm(rows_of, lo_graph[:, r, :], hi_is[:, r, :], start=False, stop=False).then_inc(d_used, 1)

                steps(pe, [(0, fill)], BATCH)
                mm(rows_of, zeros_bf[:, :], count_bf[:, 0:PT], start=False, stop=True).then_inc(d_pe, 1)
        end_stage()
        scope.pop().close()

        b_in, b_st = sems("b_in"), sems("b_st")
        b_ix, b_tr, b_xT, b_y, b_yo = sem("b_index"), sem("b_transposed"), sem("b_xT"), sem("b_y"), sem("b_y_copied")
        scope.append(ExitStack())
        ix = sb("ix", [P, 4], I32)
        xs, xsT, yb_s = sb("xs", [P, 4, P], BF16), sb("xsT", [P, 4, P], BF16), sb("yb_s", [PB, 4, NB * P], BF16)
        bx = [psum[0], psum[1]]
        by = [psum[2], psum[3]]
        with nc.Block() as block:
            @block.gpsimd
            def _(pool):
                pool.sem_inc(b_ix, CREDIT)

                def gather(q, r):
                    t = group(q, r)
                    wait_free(pool, b_tr, t, 4)
                    alone(pool, pt)
                    pool.tensor_copy(ix[:, r:r + 1], tile_src[:, bass.ds(t, 1)]).then_inc(b_ix, 1)
                    wait_done(pool, b_ix, t)
                    alone(pool, pt)
                    pool.indirect_dma_start(xs[:, r, :], None, sx_d, bass.IndirectOffsetOnAxis(ap=ix[:, r:r + 1], axis=0)).then_inc(b_in[r], 16)

                steps(pool, [(0, gather)], PT)

            @block.tensor
            def _(pe):
                mm = nc.tensor.matmul
                for s in (b_tr, b_y):
                    pe.sem_inc(s, CREDIT)

                def tr(q, r):
                    t = group(q, r)
                    wait_loaded(pe, b_in[r], q)
                    wait_free(pe, b_xT, t, 2)
                    nc.tensor.transpose(bx[r % 2][:, 0:P // 2].bitcast(BF16), xs[:, r, :], ident_bf[:, :]).then_inc(b_tr, 1)

                def apply(q, r):
                    t = group(q, r)
                    pats = [pe.value_load(block_pat[0:1, bass.ds(t * NB + j, 1)], min_val=0, max_val=PAT - 1) for j in range(NB)]
                    wait_done(pe, b_xT, t)
                    wait_free(pe, b_yo, t, 2)
                    for j in range(NB):
                        last = mm(by[r % 2][0:PB, j * P:(j + 1) * P], xsT[:, r, j * PB:(j + 1) * PB],
                                  signs[:, bass.ds(pats[j], 1), :].rearrange("p a c -> p (a c)"), start=True, stop=True)
                    last.then_inc(b_y, 1)

                steps(pe, [(1, apply), (0, tr)], PT)

            @block.scalar
            def _(act):
                act.sem_inc(b_xT, CREDIT)

                def xT(q, r):
                    t = group(q, r)
                    wait_done(act, b_tr, t)
                    wait_free(act, b_y, t, 4)
                    nc.scalar.activation(xsT[:, r, :], bx[r % 2][:, 0:P // 2].bitcast(BF16), ACT.Copy).then_inc(b_xT, 1)

                steps(act, [(0, xT)], PT)

            @block.vector
            def _(dve):
                dve.sem_inc(b_yo, CREDIT)

                def y(q, r):
                    t = group(q, r)
                    wait_done(dve, b_y, t)
                    wait_stored(dve, b_st[r], q)
                    alone(dve, vt)
                    nc.vector.tensor_copy(yb_s[:, r, :], by[r % 2][0:PB, :]).then_inc(b_yo, 1)

                steps(dve, [(0, y)], PT)

            @block.sync
            def _(sp):
                for r in range(4):
                    sp.sem_inc(b_st[r], 16)

                def store(q, r):
                    t = group(q, r)
                    wait_done(sp, b_yo, t)
                    alone(sp, ticks["sync"])
                    sp.dma_start(yb_d[bass.ds(t * P, P), :].rearrange("(j p) o -> p j o", j=NB),
                                 yb_s[:, r, :].rearrange("p (j o) -> p j o", j=NB)).then_inc(b_st[r], 16)

                steps(sp, [(0, store)], PT)
                for r in range(4):
                    sp.wait_ge(b_st[r], 16 * (PT // 4 + 1))
        end_stage()
        scope.pop().close()

        e_x, e_y, e_st = sems("e_x"), sems("e_y"), sems("e_st")
        e_ix, e_o, e_l = sem("e_index"), sem("e_out"), sem("e_link")
        scope.append(ExitStack())
        ix4 = sb("ix4", [P, 4, G], I32)
        xe, ye, oe = sb("xe", [P, 4, GW]), sb("ye", [P, 4, G, P], BF16), sb("oe", [P, 4, GW])
        with nc.Block() as block:
            @block.sync
            def _(sp):
                for r in range(4):
                    sp.sem_inc(e_st[r], 16)

                def load(q, r):
                    t = group(q, r)
                    wait_free(sp, e_o, t, 4)
                    alone(sp, ticks["sync"])
                    sp.dma_start(xe[:, r, :], x2_d[:, bass.ds(t * GW, GW)]).then_inc(e_x[r], 16)

                def store(q, r):
                    t = group(q, r)
                    wait_done(sp, e_o, t)
                    alone(sp, ticks["sync"])
                    sp.dma_start(out_v[:, bass.ds(t * GW, GW)], oe[:, r, :]).then_inc(e_st[r], 16)

                steps(sp, [(2, store), (0, load)], NG)
                for r in range(4):
                    sp.wait_ge(e_st[r], 16 * (NG // 4 + 1))

            @block.gpsimd
            def _(pool):
                pool.sem_inc(e_ix, CREDIT)

                def gather(q, r):
                    t = group(q, r)
                    wait_free(pool, e_o, t, 4)
                    alone(pool, pt)
                    pool.tensor_copy(ix4[:, r, :], slot1[:, bass.ds(t * G, G)]).then_inc(e_ix, 1)
                    wait_done(pool, e_ix, t)
                    alone(pool, pt)
                    for j in range(G):
                        pool.indirect_dma_start(ye[:, r, j, :], None, yb_d,
                                                bass.IndirectOffsetOnAxis(ap=ix4[:, r, j:j + 1], axis=0)).then_inc(e_y[r], 16)

                steps(pool, [(0, gather)], NG)

            @block.vector
            def _(dve):
                v = nc.vector
                dve.sem_inc(e_o, CREDIT)
                link = Links(dve, e_l, 1)

                def add(q, r):
                    t = group(q, r)
                    link.at(t)
                    wait_loaded(dve, e_x[r], q)
                    wait_loaded(dve, e_y[r], q, G)
                    wait_stored(dve, e_st[r], q)
                    link.then(v.tensor_tensor(as3(oe[:, r, :]), ye[:, r, :, :], scale.unsqueeze(1).to_broadcast([P, G, P]), ALU.mult))
                    v.tensor_tensor(oe[:, r, :], oe[:, r, :], xe[:, r, :], ALU.add).then_inc(e_o, 1)

                steps(dve, [(0, add)], NG)
        end_stage()
        while len(scope) > 1:
            scope.pop().close()


_OUTS = [((P, BATCH, P), "float32")]


def kernel(x, adj, L0_gnn_W, L0_gnn_a, L0_ffn_gate_w, L0_ffn_gate_b, L0_ffn_w1, L0_ffn_w2, L0_ffn_w3, L1_gnn_w1_loop,
           L1_gnn_w1_neigh, L1_gnn_b1, L1_gnn_w2_loop, L1_gnn_w2_neigh, L1_gnn_b2, L1_ffn_weight, L1_ffn_proj_w,
           L1_ffn_proj_b, L1_ffn_scale):
    import numpy as _np
    import concourse.bacc as _bacc
    from concourse import mybir as _mybir
    from concourse.bass_utils import run_bass_kernel_spmd as _run

    w3 = _np.asarray(L0_ffn_w3).reshape(E0, HID // P, P, P)
    laid = {
        "xt": _np.asarray(x).transpose(1, 0, 2),
        "adj": adj, "adjT": _np.asarray(adj).T,
        "W": L0_gnn_W, "WT": _np.asarray(L0_gnn_W).T, "a12": _np.asarray(L0_gnn_a).reshape(2, P).T,
        "gate_w": L0_ffn_gate_w,
        "w12": _np.concatenate([_np.asarray(L0_ffn_w1), _np.asarray(L0_ffn_w2)], axis=2).transpose(1, 0, 2),
        "w3": w3.transpose(2, 0, 1, 3),
        "w1l": L1_gnn_w1_loop, "w1n": L1_gnn_w1_neigh, "w2l": L1_gnn_w2_loop, "w2n": L1_gnn_w2_neigh,
        "b1": _np.asarray(L1_gnn_b1).reshape(P, 1), "b2": _np.asarray(L1_gnn_b2).reshape(1, P),
        "rows": _np.concatenate([_np.asarray(L0_ffn_gate_b), _np.asarray(L1_ffn_proj_b),
                                 _np.asarray(L1_ffn_scale).reshape(P)]).reshape(1, E0 + E1 + P),
        "wgt": _np.asarray(L1_ffn_weight)[0].transpose(1, 0, 2),
        "projT": _np.asarray(L1_ffn_proj_w).T,
    }
    nc = _bacc.Bacc("TRN2", target_bir_lowering=False, num_devices=1)
    arrays, args = {}, []
    for name, a in laid.items():
        a = _np.ascontiguousarray(a)
        arrays[f"in_{name}_dram"] = a
        args.append(nc.dram_tensor(f"in_{name}_dram", a.shape, _mybir.dt.from_np(a.dtype), kind="ExternalInput").ap())
    for i, (shape, dtype) in enumerate(_OUTS):
        dt = _mybir.dt.from_np(_np.dtype(dtype))
        args.append(nc.dram_tensor(f"out_{i}_dram", shape, dt, kind="ExternalOutput").ap())
    build(nc, *args)
    r = _run(nc, [arrays], core_ids=[0])
    return r.results[0]["out_0_dram"].transpose(1, 0, 2)
```

```python
import concourse.bass as bass
from concourse import mybir
from contextlib import ExitStack

F32 = mybir.dt.float32
BF16 = mybir.dt.bfloat16
I32 = mybir.dt.int32
U32 = mybir.dt.uint32
ALU = mybir.AluOpType
ACT = mybir.ActivationFunctionType
AX = mybir.AxisListType

P = 128
BATCH = 128
G = 4
NG = BATCH // G
GW = G * P
TOKENS = BATCH * P
E0 = 16
HID = 256
MT = 2 * TOKENS // P + E0
E1 = 8
PAT = 1 << E1
PB = 32
PT = (TOKENS // PB + PAT) * PB // P
NB = P // PB
TG = 4
TE = 2
EPS = 1e-5
SLOPE = 0.2
MASKED = -1e30


def steps(eng, stages, groups, ring=4):
    last = max(lag for lag, _ in stages)
    head = last
    while (groups - head) % ring:
        head += 1

    def step(i):
        for lag, work in stages:
            if 0 <= i - lag < groups:
                work((i - lag) // ring, (i - lag) % ring)

    for i in range(head):
        step(i)
    if groups > head:
        with eng.Fori(0, (groups - head) // ring) as n:
            for u in range(ring):
                for lag, work in stages:
                    work(n + (head + u - lag) // ring, (head + u - lag) % ring)
    for i in range(groups, groups + last):
        step(i)


def group(q, r, ring=4):
    return ring * q + r


def as3(ap, n=G):
    return ap.rearrange("p (g c) -> p g c", g=n)


CREDIT = 4


def wait_done(eng, sem, t):
    eng.wait_ge(sem, t + (1 + CREDIT))


def wait_free(eng, sem, t, ring):
    eng.wait_ge(sem, t + (1 + CREDIT - ring))


def wait_loaded(eng, sem, q, copies=1):
    eng.wait_ge(sem, (q + 1) * (16 * copies))


def wait_stored(eng, sem, q):
    eng.wait_ge(sem, (q + 1) * 16)


class Links:

    def __init__(self, eng, sem, per_group=0):
        self.eng, self.sem, self.per_group, self.base, self.n = eng, sem, per_group, 0, 0

    def at(self, t):
        self.base, self.n = t * self.per_group, 0

    def then(self, ins):
        self.n += 1
        assert not self.per_group or self.n <= self.per_group
        ins.then_inc(self.sem, 1)
        self.eng.wait_ge(self.sem, self.base + self.n)


def alone(eng, ticks):
    eng.sem_inc(ticks, 1)


def load_indices(nc, row, limit):
    return nc.values_load_multi_w_load_instructions(
        row, engines=[mybir.EngineType.PE], min_val=0, max_val=limit - 1,
        skip_runtime_bounds_check_because="the table counts ranges that ended, and a minimum caps it at limit - 1")[1]


def ln_stats(nc, link, ticks, stats, mv, src):
    for j in range(G):
        last = nc.vector.bn_stats(stats[:, j, :], src[:, j * P:(j + 1) * P])
    link.then(last)
    alone(nc.vector, ticks)
    for j in range(G - 1):
        nc.vector.bn_aggr(mv[:, j, :], stats[:, j, :])
    return nc.vector.bn_aggr(mv[:, G - 1, :], stats[:, G - 1, :])


def build(nc, xt, adj, adjT, W, WT, a12, gate_w, w12, w3, w1l, w1n, w2l, w2n, b1, b2, rows, wgt, projT, out, stop=9):
    ctx = ExitStack()
    scope = [ctx]
    taken = set()

    def sb(name, shape, dt=F32):
        name = f"{name}_{len(taken)}" if name in taken else name
        taken.add(name)
        return scope[-1].enter_context(nc.sbuf_tensor(name, shape, dt))

    stage_sems = []

    def sem(name):
        stage_sems.append(nc.alloc_semaphore(name=name))
        return stage_sems[-1]

    def end_stage():
        nc.clear_and_free_semaphores(stage_sems)
        stage_sems.clear()
        nc.all_engine_barrier()

    ticks = {}
    for name in ("pool", "vector", "scalar", "tensor", "sync"):
        ticks[name] = ctx.enter_context(nc.semaphore(f"{name}_ticks"))
    vt, pt = ticks["vector"], ticks["pool"]

    def sems(name, n=4):
        return [sem(f"{name}{i}") for i in range(n)]

    with ctx:
        x1_d = nc.dram_tensor("x1_d", [P, BATCH * P], F32, kind="Internal").ap()
        x2_d = nc.dram_tensor("x2_d", [P, BATCH * P], F32, kind="Internal").ap()
        xn_d = nc.dram_tensor("xn_d", [TOKENS, P], F32, kind="Internal").ap()
        y_d = nc.dram_tensor("y_d", [MT * P, P], F32, kind="Internal").ap()
        sx_d = nc.dram_tensor("sx_d", [TOKENS, P], BF16, kind="Internal").ap()
        yb_d = nc.dram_tensor("yb_d", [PT * P, P], BF16, kind="Internal").ap()
        xt_v = xt.rearrange("n b f -> n (b f)")
        out_v = out.rearrange("n b f -> n (b f)")
        xn_v = xn_d.rearrange("(n b) f -> n (b f)", b=BATCH)
        sx_v = sx_d.rearrange("(n b) f -> n (b f)", b=BATCH)

        psum = [ctx.enter_context(nc.psum_tensor(f"bank{i}", [P, 512], F32)) for i in range(8)]

        ident = sb("ident", [P, P])
        ident_bf = sb("ident_bf", [P, P], BF16)
        before = sb("before", [P, P], BF16)
        not_before = sb("not_before", [P, P], BF16)
        ones_bf = sb("ones_bf", [P, P], BF16)
        zeros_bf = sb("zeros_bf", [P, P], BF16)
        ones_row = sb("ones_row", [1, P])
        mhalf = sb("mhalf", [P, G])
        count_i = sb("count_i", [P, NB * PT], I32)
        count = sb("count", [P, NB * PT])
        count_bf = sb("count_bf", [P, 256], BF16)
        hi_zero = sb("hi_zero", [P, MT + 1], BF16)
        row_i = sb("row_i", [P, 1], I32)
        row_id = sb("row_id", [P, 1])
        mask = sb("mask", [P, P], BF16)
        W_s = sb("W_s", [P, P])
        WT_s = sb("WT_s", [P, P])
        a12_s = sb("a12_s", [P, 2])
        Waug = sb("Waug", [P, P + 2])
        wa2 = sb("wa2", [P, P])
        adj_s = sb("adj_s", [P, P])
        adjT_s = sb("adjT_s", [P, P])
        gw_s = sb("gw_s", [P, E0])
        rows_s = sb("rows_s", [1, E0 + E1 + P])
        rows_b = sb("rows_b", [P, E0 + E1 + P])
        gbias = rows_b[:, 0:E0]
        pbias = rows_b[:, E0:E0 + E1]
        scale = rows_b[:, E0 + E1:]
        w1l_s = sb("w1l_s", [P, P])
        w1n_s = sb("w1n_s", [P, P])
        w2l_s = sb("w2l_s", [P, P])
        w2n_s = sb("w2n_s", [P, P])
        b1_s = sb("b1_s", [P, 1])
        b2_s = sb("b2_s", [1, P])
        b2x = sb("b2x", [1, GW])
        projT_s = sb("projT_s", [P, E1])
        bits = sb("bits", [P, E1])
        expert = sb("expert", [P, BATCH, 2])
        top = sb("top", [P, BATCH, 2])
        share = sb("share", [P, BATCH, 2])
        slot = sb("slot", [P, BATCH, 2], I32)
        signs = sb("signs", [P, PAT, P], BF16)

        def pool_ln(pool, link, mv, ve, rstd):
            link.then(pool.tensor_scalar(ve, mv[:, :, 1], EPS, None, ALU.add))
            return pool.tensor_tensor(ve, ve, mhalf[:, :], ALU.pow)

        s_ld, s_pc, s_vc, s_mm, s_mv = sem("const_loaded"), sem("pool_consts"), sem("vector_consts"), sem("const_mm"), sem("const_mv")
        loads = [(W_s, W), (WT_s, WT), (a12_s, a12), (adj_s, adj), (adjT_s, adjT), (gw_s, gate_w), (rows_s, rows),
                 (w1l_s, w1l), (w1n_s, w1n), (w2l_s, w2l), (w2n_s, w2n), (b1_s, b1), (b2_s, b2), (projT_s, projT)]
        scope.append(ExitStack())
        wsum_lo = sb("wsum_lo", [P, 16, P])
        wsum_hi = sb("wsum_hi", [P, 16, P])
        wgt_s = sb("wgt_s", [P, E1, P])
        with nc.Block() as block:
            @block.sync
            def _(sp):
                for dst, src in loads:
                    sp.dma_start(dst[:, :], src).then_inc(s_ld, 16)
                sp.dma_start(wgt_s[:, :, :], wgt).then_inc(s_ld, 16)

            @block.gpsimd
            def _(pool):
                link = Links(pool, s_pc)
                pool.memset(zeros_bf[:, :], 0.0)
                pool.memset(ones_bf[:, :], 1.0)
                pool.memset(not_before[:, :], 1.0)
                pool.memset(ones_row[:, :], 1.0)
                pool.memset(mhalf[:, :], -0.5)
                pool.memset(ident[:, :], 0.0)
                pool.memset(ident_bf[:, :], 0.0)
                link.then(pool.memset(before[:, :], 0.0))
                pool.affine_select(out=ident[:, :], in_=ident[:, :], compare_op=ALU.not_equal, fill=1.0, base=0,
                                   pattern=[[-1, P]], channel_multiplier=1)
                pool.affine_select(out=ident_bf[:, :], in_=ident_bf[:, :], compare_op=ALU.not_equal, fill=1.0, base=0,
                                   pattern=[[-1, P]], channel_multiplier=1)
                pool.affine_select(out=before[:, :], in_=before[:, :], compare_op=ALU.is_ge, fill=1.0, base=0,
                                   pattern=[[-1, P]], channel_multiplier=1)
                pool.affine_select(out=not_before[:, :], in_=not_before[:, :], compare_op=ALU.is_ge, fill=0.0, base=0,
                                   pattern=[[-1, P]], channel_multiplier=1)
                pool.iota(row_i[:, :], pattern=[[0, 1]], base=0, channel_multiplier=P)
                link.then(pool.iota(count_i[:, :], pattern=[[1, NB * PT]], base=0, channel_multiplier=0))

            @block.vector
            def _(dve):
                link = Links(dve, s_vc)
                v = nc.vector
                dve.wait_ge(s_pc, 2)
                for g in range(E1):
                    v.memset(bits[:, g:g + 1], float(1 << g))
                v.tensor_copy(count[:, :], count_i[:, :])
                v.tensor_copy(row_id[:, :], row_i[:, :])
                v.memset(wsum_lo[:, 0, :], 0.0)
                v.memset(wsum_hi[:, 0, :], 0.0)
                link.then(v.tensor_copy(count_bf[:, :], count_i[:, 0:256]))
                v.memset(hi_zero[:, :], 0.0)
                dve.wait_ge(s_ld, 16 * (len(loads) + 1))
                v.tensor_scalar(mask[:, :], adj_s[:, :], 0.0, MASKED, ALU.is_equal, ALU.mult)
                for g in range(4):
                    n = 1 << g
                    v.tensor_tensor(wsum_lo[:, n:2 * n, :], wsum_lo[:, 0:n, :],
                                    wgt_s[:, g, :].unsqueeze(1).to_broadcast([P, n, P]), ALU.add)
                    link.then(v.tensor_tensor(wsum_hi[:, n:2 * n, :], wsum_hi[:, 0:n, :],
                                              wgt_s[:, 4 + g, :].unsqueeze(1).to_broadcast([P, n, P]), ALU.add))
                v.tensor_copy(Waug[:, 0:P], W_s[:, :])
                v.tensor_copy(b2x[:, :].rearrange("p (g c) -> p g c", g=G), b2_s[:, :].unsqueeze(1).to_broadcast([1, G, P]))
                dve.wait_ge(s_mm, 1)
                v.tensor_copy(Waug[:, P:P + 2], psum[0][:, 0:2])
                v.tensor_copy(wa2[:, :], psum[0][:, 1:2].to_broadcast([P, P]))
                dve.wait_ge(s_mm, 2)
                link.then(v.tensor_copy(rows_b[:, :], psum[1][:, 0:E0 + E1 + P]))

            @block.tensor
            def _(pe):
                pe.wait_ge(s_ld, 16 * (len(loads) + 1))
                pe.wait_ge(s_pc, 2)
                nc.tensor.matmul(psum[0][:, 0:2], WT_s[:, :], a12_s[:, :], start=True, stop=True).then_inc(s_mm, 1)
                nc.tensor.matmul(psum[1][:, 0:E0 + E1 + P], ones_row[:, :], rows_s[:, :], start=True, stop=True).then_inc(s_mm, 1)
        end_stage()

        xa_in, xd_in, x1_st, xn_st = sems("xa_in"), sems("xd_in"), sems("x1_st"), sems("xn_st")
        a_stats, a_xn, a_tr, a_xnT = sem("a_stats"), sem("a_xn"), sem("a_transposed"), sem("a_xnT")
        a_wh, a_whs, a_max, a_exp = sem("a_wh"), sem("a_wh_copied"), sem("a_max"), sem("a_exp")
        a_p = sem("a_p")
        a_sc = sem("a_scores")
        a_att, a_attT, a_av, a_x1 = sem("a_att"), sem("a_attT"), sem("a_av"), sem("a_x1")
        a_xn2, a_tr2, a_xn2T, a_gate = sem("a_xn2"), sem("a_transposed2"), sem("a_xn2T"), sem("a_gate")
        a_wt, a_sign, a_ra, a_rd = sem("a_wt"), sem("a_sign"), sem("a_rstd"), sem("a_rstd2")
        a_va, a_vb, a_vd, a_ve, a_pa, a_pd = [sem("a_link%d" % i) for i in range(6)]
        a_avu, a_lg = sem("a_av_used"), sem("a_logits")
        scope.append(ExitStack())
        xa, xd, xo = sb("xa", [P, 4, GW]), sb("xd", [P, 4, GW]), sb("xo", [P, 4, GW])
        stats, mv, ve = sb("stats", [P, 2, G, 6]), sb("mv", [P, 4, G, 2]), sb("ve", [P, 4, G])
        xn, xnT, wh = sb("xn", [P, 2, GW]), sb("xnT", [P, 2, GW]), sb("wh", [P, 4, 2, 2 * (P + 2)])
        rmax, shift, rsum = sb("rmax", [P, 3, G]), sb("shift", [P, 4, 2, G]), sb("rsum", [P, 4, G])
        pos, neg = sb("pos", [P, 2, GW]), sb("neg", [P, 2, GW])
        att, attT = sb("att", [P, 2, GW]), sb("attT", [P, 2, GW])
        stats2, mv2, ve2, nb2 = sb("stats2", [P, G, 6]), sb("mv2", [P, 4, G, 2]), sb("ve2", [P, 4, G]), sb("nb2", [P, 4, G])
        xn2, xn2T = sb("xn2", [P, 4, GW]), sb("xn2T", [P, 2, GW])
        lg, top8, idx8 = sb("lg", [P, G, E0]), sb("top8", [P, G, 8]), sb("idx8", [P, G, 8], U32)
        wt = sb("wt", [P, 2, 8, P])
        whp = [psum[1], psum[2]]

        with nc.Block() as block:
            @block.sync
            def _(sp):
                for r in range(4):
                    sp.sem_inc(x1_st[r], 16)
                    sp.sem_inc(xn_st[r], 16)

                def load_a(q, r):
                    wait_free(sp, a_xn, group(q, r), 4)
                    sp.dma_start(xa[:, r, :], xt_v[:, bass.ds(group(q, r) * GW, GW)]).then_inc(xa_in[r], 16)

                def load_d(q, r):
                    wait_free(sp, a_x1, group(q, r), 4)
                    sp.dma_start(xd[:, r, :], xt_v[:, bass.ds(group(q, r) * GW, GW)]).then_inc(xd_in[r], 16)

                def store(q, r):
                    wait_done(sp, a_x1, group(q, r))
                    sp.dma_start(x1_d[:, bass.ds(group(q, r) * GW, GW)], xo[:, r, :]).then_inc(x1_st[r], 16)

                def store_xn(q, r):
                    wait_done(sp, a_xn2, group(q, r))
                    sp.dma_start(xn_v[:, bass.ds(group(q, r) * GW, GW)], xn2[:, r, :]).then_inc(xn_st[r], 16)

                steps(sp, [(10, store_xn), (9, store), (5, load_d), (0, load_a)], NG)
                for r in range(4):
                    sp.wait_ge(x1_st[r], 16 * (NG // 4 + 1))
                    sp.wait_ge(xn_st[r], 16 * (NG // 4 + 1))

            @block.gpsimd
            def _(pool):
                for s in (a_ra, a_rd, a_wt):
                    pool.sem_inc(s, CREDIT)
                la, ld = Links(pool, a_pa, 1), Links(pool, a_pd, 3)

                def rstd_a(q, r):
                    t = group(q, r)
                    la.at(t)
                    wait_done(pool, a_stats, t)
                    wait_free(pool, a_xn, t, 4)
                    alone(pool, pt)
                    la.then(pool.tensor_scalar(ve[:, r, :], mv[:, r, :, 1], EPS, None, ALU.add))
                    pool.tensor_tensor(ve[:, r, :], ve[:, r, :], mhalf[:, :], ALU.pow).then_inc(a_ra, 1)

                def rstd_d(q, r):
                    t = group(q, r)
                    ld.at(t)
                    wait_done(pool, a_x1, t)
                    wait_free(pool, a_xn2, t, 4)
                    alone(pool, pt)
                    ld.then(pool.tensor_scalar(ve2[:, r, :], mv2[:, r, :, 1], EPS, None, ALU.add))
                    ld.then(pool.tensor_tensor(ve2[:, r, :], ve2[:, r, :], mhalf[:, :], ALU.pow))
                    ld.then(pool.tensor_tensor(nb2[:, r, :], mv2[:, r, :, 0], ve2[:, r, :], ALU.mult))
                    alone(pool, pt)
                    pool.tensor_scalar(nb2[:, r, :], nb2[:, r, :], -1.0, None, ALU.mult).then_inc(a_rd, 1)

                def sum_weights(q, r):
                    t = group(q, r)
                    wait_free(pool, a_sign, t, 2)
                    alone(pool, pt)
                    pool.tensor_tensor(wt[:, r % 2, :, :], wsum_lo[:, (r % 2) * 8:(r % 2) * 8 + 8, :],
                                       wsum_hi[:, bass.ds(2 * q + r // 2, 1), :].to_broadcast([P, 8, P]),
                                       ALU.add).then_inc(a_wt, 1)

                steps(pool, [(8, rstd_d), (0, rstd_a), (0, sum_weights)], NG)

            @block.vector
            def _(dve):
                v = nc.vector
                for s in (a_stats, a_xn, a_max, a_avu, a_x1, a_lg, a_p):
                    dve.sem_inc(s, CREDIT)
                la, lb, ld, le = Links(dve, a_va, 1), Links(dve, a_vb, 3), Links(dve, a_vd, 2), Links(dve, a_ve, 2)

                def stats_a(q, r):
                    t = group(q, r)
                    la.at(t)
                    wait_loaded(dve, xa_in[r], q)
                    wait_free(dve, a_xn, t, 4)
                    ln_stats(nc, la, vt, stats[:, r % 2], mv[:, r], xa[:, r, :]).then_inc(a_stats, 1)

                def norm_a(q, r):
                    t = group(q, r)
                    wait_done(dve, a_ra, t)
                    wait_free(dve, a_tr, t, 2)
                    alone(dve, vt)
                    for j in range(G):
                        c = slice(j * P, (j + 1) * P)
                        last = v.tensor_scalar(xn[:, r % 2, c], xa[:, r, c], mv[:, r, j, 0:1], ve[:, r, j:j + 1], ALU.subtract, ALU.mult)
                    last.then_inc(a_xn, 1)

                def max_b(q, r):
                    t = group(q, r)
                    lb.at(t)
                    wait_done(dve, a_sc, t)
                    lb.then(v.reduce_max(rmax[:, 0, :], as3(psum[3][:, :]), AX.X))
                    wait_done(dve, a_whs, t)
                    s1 = wh[:, r, :, :].rearrange("p a (b c) -> p a b c", b=2)[:, :, :, P].rearrange("p a b -> p (a b)")
                    lb.then(v.tensor_tensor(rmax[:, 1, :], rmax[:, 0, :], s1, ALU.add))
                    lb.then(v.scalar_tensor_tensor(rmax[:, 2, :], rmax[:, 1, :], SLOPE, rmax[:, 1, :], ALU.mult, ALU.max))
                    wait_free(dve, a_exp, t, 4)
                    v.tensor_tensor(shift[:, r, 0, :], s1, rmax[:, 2, :], ALU.subtract)
                    v.scalar_tensor_tensor(shift[:, r, 1, :], s1, SLOPE, rmax[:, 2, :], ALU.mult, ALU.subtract).then_inc(a_max, 1)

                def p_c(q, r):
                    t = group(q, r)
                    wait_done(dve, a_exp, t)
                    wait_free(dve, a_att, t, 2)
                    for j in range(G):
                        c = slice(j * P, (j + 1) * P)
                        last = v.scalar_tensor_tensor(att[:, r % 2, c], pos[:, r % 2, c], 1.0, neg[:, r % 2, c], ALU.mult,
                                                      ALU.max, accum_out=rsum[:, r, j:j + 1])
                    last.then_inc(a_p, 1)

                def add_d(q, r):
                    t = group(q, r)
                    ld.at(t)
                    ld.then(v.reciprocal(rsum[:, r, :], rsum[:, r, :]))
                    wait_done(dve, a_av, t)
                    wait_loaded(dve, xd_in[r], q)
                    wait_stored(dve, x1_st[r], q)
                    wait_free(dve, a_xn2, t, 4)
                    for j in range(G):
                        last = v.scalar_tensor_tensor(xo[:, r, j * P:(j + 1) * P], psum[5][:, j * P:(j + 1) * P],
                                                      rsum[:, r, j:j + 1], xd[:, r, j * P:(j + 1) * P], ALU.mult, ALU.add)
                    last.then_inc(a_avu, 1)
                    wait_done(dve, a_avu, t)
                    ln_stats(nc, ld, vt, stats2, mv2[:, r], xo[:, r, :]).then_inc(a_x1, 1)

                def top_e(q, r):
                    t = group(q, r)
                    le.at(t)
                    wait_done(dve, a_gate, t)
                    v.tensor_tensor(lg[:, :, :], psum[7][:, 0:G * E0].rearrange("p (g c) -> p g c", g=G),
                                    gbias.unsqueeze(1).to_broadcast([P, G, E0]), ALU.add).then_inc(a_lg, 1)
                    wait_done(dve, a_lg, t)
                    alone(dve, vt)
                    for j in range(G):
                        last = v.max(top8[:, j, :], lg[:, j, :])
                    le.then(last)
                    alone(dve, vt)
                    for j in range(G):
                        last = v.max_index(idx8[:, j, :], top8[:, j, :], lg[:, j, :])
                    le.then(last)
                    v.tensor_copy(expert[:, bass.ds(t * G, G), :], idx8[:, :, 0:2])
                    v.tensor_copy(top[:, bass.ds(t * G, G), :], top8[:, :, 0:2])

                steps(dve, [(8, add_d), (5, p_c), (4, max_b), (12, top_e), (0, stats_a), (1, norm_a)], NG)

            @block.scalar
            def _(act):
                s_ = nc.scalar
                for s in (a_xnT, a_whs, a_attT, a_exp, a_xn2, a_xn2T, a_sign):
                    act.sem_inc(s, CREDIT)

                def xnT_a(q, r):
                    t = group(q, r)
                    wait_done(act, a_tr, t)
                    wait_free(act, a_sc, t, 2)
                    s_.activation(xnT[:, r % 2, :], psum[0][:, :], ACT.Copy).then_inc(a_xnT, 1)

                def sign(q, r):
                    t = group(q, r)
                    wait_done(act, a_wt, t)
                    s_.activation(signs[:, bass.ds(t * 8, 8), :], wt[:, r % 2, :, :], ACT.Sign).then_inc(a_sign, 1)

                def wh_b(q, r):
                    t = group(q, r)
                    wait_done(act, a_wh, t)
                    wait_free(act, a_av, t, 4)
                    for h in range(2):
                        last = s_.activation(wh[:, r, h, :], whp[h][:, 0:2 * (P + 2)], ACT.Copy)
                    last.then_inc(a_whs, 1)

                def exp_c(q, r):
                    t = group(q, r)
                    wait_free(act, a_p, t, 2)
                    wait_done(act, a_max, t)
                    wait_done(act, a_sc, t)
                    for j in range(G):
                        c = slice(j * P, (j + 1) * P)
                        s_.activation(pos[:, r % 2, c], psum[3][:, c], ACT.Exp, bias=shift[:, r, 0, j:j + 1])
                        last = s_.activation(neg[:, r % 2, c], psum[3][:, c], ACT.Exp, bias=shift[:, r, 1, j:j + 1], scale=SLOPE)
                    last.then_inc(a_exp, 1)

                def attT_d(q, r):
                    t = group(q, r)
                    wait_done(act, a_att, t)
                    wait_free(act, a_av, t, 2)
                    s_.activation(attT[:, r % 2, :], psum[4][:, :], ACT.Copy).then_inc(a_attT, 1)

                def norm_d(q, r):
                    t = group(q, r)
                    wait_done(act, a_rd, t)
                    wait_stored(act, xn_st[r], q)
                    wait_free(act, a_tr2, t, 4)
                    for j in range(G):
                        c = slice(j * P, (j + 1) * P)
                        last = s_.activation(xn2[:, r, c], xo[:, r, c], ACT.Identity, bias=nb2[:, r, j:j + 1], scale=ve2[:, r, j:j + 1])
                    last.then_inc(a_xn2, 1)

                def xnT_d(q, r):
                    t = group(q, r)
                    wait_done(act, a_tr2, t)
                    wait_free(act, a_gate, t, 2)
                    s_.activation(xn2T[:, r % 2, :], psum[6][:, :], ACT.Copy).then_inc(a_xn2T, 1)

                steps(act, [(6, attT_d), (4, exp_c), (9, norm_d), (10, xnT_d), (1, sign), (3, wh_b), (2, xnT_a)], NG)

            @block.tensor
            def _(pe):
                mm = nc.tensor.matmul
                for s in (a_tr, a_wh, a_sc, a_att, a_av, a_tr2, a_gate):
                    pe.sem_inc(s, CREDIT)

                def tr_a(q, r):
                    t = group(q, r)
                    wait_done(pe, a_xn, t)
                    wait_free(pe, a_xnT, t, 1)
                    for j in range(G):
                        last = nc.tensor.transpose(psum[0][:, j * P:(j + 1) * P], xn[:, r % 2, j * P:(j + 1) * P], ident[:, :])
                    last.then_inc(a_tr, 1)

                def wh_b(q, r):
                    t = group(q, r)
                    wait_done(pe, a_xnT, t)
                    wait_free(pe, a_whs, t, 1)
                    for j in range(G):
                        c = (j % 2) * (P + 2)
                        last = mm(whp[j // 2][:, c:c + P + 2], xnT[:, r % 2, j * P:(j + 1) * P], Waug[:, :], start=True, stop=True)
                    last.then_inc(a_wh, 1)
                    wait_free(pe, a_exp, t, 1)
                    mm(psum[3][:, :], wa2[:, :], xnT[:, r % 2, :], start=True, stop=False)
                    mm(psum[3][:, :], ident_bf[:, :], mask[:, :].unsqueeze(1).to_broadcast([P, G, P]),
                       start=False, stop=True).then_inc(a_sc, 1)

                def att_c(q, r):
                    t = group(q, r)
                    wait_done(pe, a_p, t)
                    wait_free(pe, a_attT, t, 1)
                    for j in range(G):
                        last = nc.tensor.transpose(psum[4][:, j * P:(j + 1) * P], att[:, r % 2, j * P:(j + 1) * P], ident[:, :])
                    last.then_inc(a_att, 1)

                def av_d(q, r):
                    t = group(q, r)
                    wait_done(pe, a_attT, t)
                    wait_free(pe, a_avu, t, 1)
                    for j in range(G):
                        c = (j % 2) * (P + 2)
                        last = mm(psum[5][:, j * P:(j + 1) * P], attT[:, r % 2, j * P:(j + 1) * P],
                                  wh[:, r, j // 2, c:c + P], start=True, stop=True)
                    last.then_inc(a_av, 1)

                def tr_e(q, r):
                    t = group(q, r)
                    wait_done(pe, a_xn2, t)
                    wait_free(pe, a_xn2T, t, 1)
                    for j in range(G):
                        last = nc.tensor.transpose(psum[6][:, j * P:(j + 1) * P], xn2[:, r, j * P:(j + 1) * P], ident[:, :])
                    last.then_inc(a_tr2, 1)

                def gate_e(q, r):
                    t = group(q, r)
                    wait_done(pe, a_xn2T, t)
                    wait_free(pe, a_lg, t, 1)
                    for j in range(G):
                        last = mm(psum[7][:, j * E0:(j + 1) * E0], xn2T[:, r % 2, j * P:(j + 1) * P], gw_s[:, :],
                                  start=True, stop=True)
                    last.then_inc(a_gate, 1)

                steps(pe, [(6, att_c), (7, av_d), (10, tr_e), (11, gate_e), (3, wh_b), (2, tr_a)], NG)
        end_stage()
        scope.pop().close()
        scope.pop().close()

        s_w, r_v, r_mm, r_pe = sem("expert_weights"), sem("route_v"), sem("route_counts"), sem("route_list")
        r_oh, r_used = sem("route_onehot"), sem("route_onehot_used")
        r_exp, r_tot, r_last, r_inside = sem("route_exp"), sem("route_totals"), sem("route_last_tile"), sem("route_inside")
        scope.append(ExitStack())
        w12_s, w3_s = sb("w12_s", [P, E0, 2 * HID]), sb("w3_s", [P, E0, HID // P, P])
        tile_token, tile_expert = sb("tile_token", [P, MT], I32), sb("tile_expert", [1, MT], I32)
        scope.append(ExitStack())
        oh = [sb(f"oh{k}", [P, E0, BATCH]) for k in range(2)]
        both, cum, rank = sb("both", [P, E0, BATCH]), sb("cum", [P, E0, BATCH]), sb("rank", [P, E0, BATCH])
        ends, tot, tot_bf = sb("ends", [P, E0 + 1]), sb("tot", [P, E0]), sb("tot_bf", [P, E0], BF16)
        need_i, need, last_tile, off = sb("need_i", [P, E0], I32), sb("need", [P, E0]), sb("last_tile", [P, E0]), sb("off", [P, E0])
        endcol, inside = sb("endcol", [E0, 1]), sb("inside", [E0, MT], BF16)
        slot_f = sb("slot_f", [P, BATCH, 2])
        lo_i, hi_i = sb("lo_i", [P, BATCH, 2], I32), sb("hi_i", [P, BATCH, 2], I32)
        lo, hi = sb("lo", [P, BATCH, 2]), sb("hi", [P, BATCH, 2])
        lo_row, lo_graph, hi_sign = sb("lo_row", [P, 4, 2, P], BF16), sb("lo_graph", [P, 4, 2, P], BF16), sb("hi_sign", [P, 4, 2, MT + 1], BF16)
        sums, twice = sb("sums", [P, MT + 1]), sb("twice", [P, MT])
        r_sign, r_hi = sem("route_sign"), sem("route_hi")
        pairs = psum[3][:, 0:MT + 1]
        with nc.Block() as block:
            @block.sync
            def _(sp):
                sp.dma_start(w12_s[:, :, :], w12).then_inc(s_w, 16)
                sp.dma_start(w3_s[:, :, :, :], w3).then_inc(s_w, 16)
                sp.wait_ge(s_w, 32)

            @block.scalar
            def _(act):
                act.wait_ge(r_v, 1)
                nc.scalar.activation(share[:, :, 1], top[:, :, 1], ACT.Exp).then_inc(r_exp, 1)
                act.sem_inc(r_sign, CREDIT)
                act.wait_ge(r_hi, 1)

                def signs_of_hi(q, r):
                    t = group(q, r)
                    wait_free(act, r_used, t, 4)
                    alone(act, ticks["scalar"])
                    for k in range(2):
                        last = nc.scalar.activation(hi_sign[:, r, k, :], count[:, 0:MT + 1], ACT.Sign, bias=hi[:, bass.ds(t, 1), k])
                    last.then_inc(r_sign, 1)

                steps(act, [(0, signs_of_hi)], BATCH)

            @block.vector
            def _(dve):
                v = nc.vector
                dve.sem_inc(r_oh, CREDIT)
                link = Links(dve, r_v)
                link.then(v.tensor_tensor(top[:, :, 1], top[:, :, 1], top[:, :, 0], ALU.subtract))
                for k in range(2):
                    v.tensor_tensor(oh[k][:, :, :], count[:, 0:E0].unsqueeze(2).to_broadcast([P, E0, BATCH]),
                                    expert[:, :, k].unsqueeze(1).to_broadcast([P, E0, BATCH]), ALU.is_equal)
                v.memset(ends[:, 0:1], 0.0)
                dve.wait_ge(r_exp, 1)
                link.then(v.tensor_scalar(share[:, :, 0], share[:, :, 1], 1.0, None, ALU.add))
                link.then(v.reciprocal(share[:, :, 0], share[:, :, 0]))
                v.tensor_tensor(share[:, :, 1], share[:, :, 1], share[:, :, 0], ALU.mult)
                link.then(v.tensor_tensor(both[:, :, :], oh[0][:, :, :], oh[1][:, :, :], ALU.add))
                flat = both[:, :, :].rearrange("p e b -> p (e b)")
                link.then(v.tensor_tensor_scan(cum[:, :, :].rearrange("p e b -> p (e b)"), flat, flat, 0.0, ALU.add, ALU.max))
                link.then(v.tensor_copy(ends[:, 1:], cum[:, :, BATCH - 1]))
                link.then(v.tensor_tensor(tot[:, :], ends[:, 1:], ends[:, 0:E0], ALU.subtract))
                v.tensor_copy(tot_bf[:, :], tot[:, :]).then_inc(r_tot, 1)
                dve.wait_ge(r_mm, 1)
                link.then(v.tensor_scalar(need[:, :], psum[0][:, E0:2 * E0], float(P - 1), None, ALU.add))
                link.then(v.tensor_copy(need_i[:, :], need[:, :]))
                link.then(v.tensor_scalar(need_i[:, :], need_i[:, :], 7, None, ALU.arith_shift_right))
                link.then(v.tensor_copy(need[:, :], need_i[:, :]))
                v.tensor_tensor_scan(last_tile[:, :], need[:, :], need[:, :], 0.0, ALU.add, ALU.max).then_inc(r_last, 1)
                dve.wait_ge(r_last, 1)
                link.then(v.tensor_tensor(off[:, :], last_tile[:, :], need[:, :], ALU.subtract))
                link.then(v.tensor_scalar(off[:, :], off[:, :], float(P), None, ALU.mult))
                link.then(v.tensor_tensor(off[:, :], off[:, :], psum[0][:, 0:E0], ALU.add))
                v.tensor_tensor(rank[:, :, :], cum[:, :, :], both[:, :, :], ALU.subtract)
                link.then(v.tensor_tensor(off[:, :], off[:, :], ends[:, 0:E0], ALU.subtract))
                link.then(v.tensor_tensor(rank[:, :, :], rank[:, :, :], off[:, :].unsqueeze(2).to_broadcast([P, E0, BATCH]), ALU.add))
                for k in range(2):
                    link.then(v.tensor_tensor(oh[k][:, :, :], oh[k][:, :, :], rank[:, :, :], ALU.mult))
                    link.then(v.tensor_reduce(slot_f[:, :, k], oh[k][:, :, :].rearrange("p e b -> p b e"), AX.X, ALU.add))
                link.then(v.tensor_copy(slot[:, :, :], slot_f[:, :, :]))
                v.tensor_scalar(lo_i[:, :, :], slot[:, :, :], P - 1, None, ALU.bitwise_and)
                link.then(v.tensor_scalar(hi_i[:, :, :], slot[:, :, :], 7, None, ALU.arith_shift_right))
                v.tensor_copy(lo[:, :, :], lo_i[:, :, :])
                link.then(v.tensor_copy(hi[:, :, :], hi_i[:, :, :]))
                v.tensor_scalar(hi[:, :, :], hi[:, :, :], -1.0, -0.5, ALU.mult, ALU.add).then_inc(r_hi, 1)

                dve.wait_ge(r_mm, 2)
                link.then(v.tensor_copy(endcol[:, :], psum[1][0:E0, 0:1]))
                v.tensor_scalar(inside[:, :], count[0:E0, 0:MT], endcol[:, :], None, ALU.is_ge).then_inc(r_inside, 1)
                dve.wait_ge(r_mm, 3)
                link.then(v.tensor_scalar(tile_expert[:, :], psum[2][0:1, 0:MT], float(E0 - 1), None, ALU.min))

                def onehots(q, r):
                    t = group(q, r)
                    wait_free(dve, r_used, t, 4)
                    for k in range(2):
                        v.tensor_scalar(lo_row[:, r, k, :], count_bf[:, 0:P], lo[:, bass.ds(t, 1), k], row_id[:, :],
                                        ALU.is_equal, ALU.mult)
                        last = v.tensor_scalar(lo_graph[:, r, k, :], count_bf[:, 0:P], lo[:, bass.ds(t, 1), k],
                                               count[:, bass.ds(t, 1)], ALU.is_equal, ALU.mult)
                    last.then_inc(r_oh, 1)

                steps(dve, [(0, onehots)], BATCH)
                dve.wait_ge(r_pe, 1)
                link.then(v.tensor_copy(sums[:, :], pairs))
                link.then(v.tensor_tensor(twice[:, :], sums[:, 1:], sums[:, 0:MT], ALU.subtract))
                link.then(v.tensor_scalar(tile_token[:, :], twice[:, :], 0.5, None, ALU.mult))

            @block.tensor
            def _(pe):
                mm = nc.tensor.matmul
                pe.sem_inc(r_used, CREDIT)
                pe.wait_ge(r_tot, 1)
                mm(psum[0][:, 0:E0], before[:, :], tot_bf[:, :], start=True, stop=True)
                mm(psum[0][:, E0:2 * E0], ones_bf[:, :], tot_bf[:, :], start=True, stop=True).then_inc(r_mm, 1)
                pe.wait_ge(r_last, 1)
                nc.tensor.transpose(psum[1][0:E0, 0:P], last_tile[:, :], ident[:, :]).then_inc(r_mm, 1)
                pe.wait_ge(r_inside, 1)
                mm(psum[2][0:1, 0:MT], ones_bf[0:E0, 0:1], inside[:, :], start=True, stop=True).then_inc(r_mm, 1)

                mm(pairs, zeros_bf[:, :], hi_zero[:, :], start=True, stop=False)

                def fill(q, r):
                    wait_done(pe, r_oh, group(q, r))
                    wait_done(pe, r_sign, group(q, r))
                    for k in range(2):
                        mm(pairs, lo_row[:, r, k, :], hi_sign[:, r, k, :], start=False, stop=False)
                        last = mm(pairs, lo_graph[:, r, k, :], hi_sign[:, r, k, :], start=False, stop=False)
                    last.then_inc(r_used, 1)

                steps(pe, [(0, fill)], BATCH)
                mm(pairs, zeros_bf[:, :], hi_zero[:, :], start=False, stop=True).then_inc(r_pe, 1)
        end_stage()
        scope.pop().close()

        g_in, y_st = sems("g_in"), sems("y_st")
        m_ix, m_tr, m_xT, m_h, m_silu, m_hid = sem("m_index"), sem("m_transposed"), sem("m_xT"), sem("m_h"), sem("m_silu"), sem("m_hid")
        m_trh, m_hT, m_y, m_yo = sem("m_hid_transposed"), sem("m_hidT"), sem("m_y"), sem("m_y_copied")
        scope.append(ExitStack())
        EG = MT // TE
        HC = HID // P
        ix = sb("ix", [P, 4, TE], I32)
        xg, xgT, yo = sb("xg", [P, 4, TE, P]), sb("xgT", [P, 4, TE, P]), sb("yo", [P, 4, TE, P])
        gate, hid, hidT = sb("gate", [P, 4, TE, HID]), sb("hid", [P, 4, TE, HID]), sb("hidT", [P, 4, TE, HID])
        bx, bh, bt, by = [psum[0], psum[1]], [[psum[2], psum[3]], [psum[4], psum[5]]], psum[6], psum[7]
        with nc.Block() as block:
            @block.gpsimd
            def _(pool):
                pool.sem_inc(m_ix, CREDIT)

                def index(q, r):
                    t = group(q, r)
                    wait_free(pool, m_tr, t, 4)
                    alone(pool, pt)
                    pool.tensor_copy(ix[:, r, :], tile_token[:, bass.ds(t * TE, TE)]).then_inc(m_ix, 1)

                def gather(q, r):
                    wait_done(pool, m_ix, group(q, r))
                    alone(pool, pt)
                    for k in range(TE):
                        pool.indirect_dma_start(xg[:, r, k, :], None, xn_d,
                                                bass.IndirectOffsetOnAxis(ap=ix[:, r, k:k + 1], axis=0)).then_inc(g_in[r], 16)

                steps(pool, [(0, index), (1, gather)], EG)

            @block.tensor
            def _(pe):
                mm = nc.tensor.matmul
                for s in (m_tr, m_h, m_trh, m_y):
                    pe.sem_inc(s, CREDIT)

                def tr(q, r):
                    t = group(q, r)
                    wait_loaded(pe, g_in[r], q, TE)
                    wait_free(pe, m_xT, t, 2)
                    for k in range(TE):
                        last = nc.tensor.transpose(bx[r % 2][:, k * P:(k + 1) * P], xg[:, r, k, :], ident[:, :])
                    last.then_inc(m_tr, 1)

                def up(q, r):
                    t = group(q, r)
                    experts = load_indices(nc, tile_expert[0:1, bass.ds(t * TE, TE)], E0)
                    wait_done(pe, m_xT, t)
                    wait_free(pe, m_hid, t, 2)
                    for k in range(TE):
                        last = mm(bh[r % 2][k][:, :], xgT[:, r, k, :], w12_s[:, bass.ds(experts[k], 1), :].rearrange("p a c -> p (a c)"),
                                  start=True, stop=True)
                    last.then_inc(m_h, 1)

                def tr_hid(q, r):
                    t = group(q, r)
                    wait_done(pe, m_hid, t)
                    wait_free(pe, m_hT, t, 1)
                    for k in range(TE):
                        for c in range(HC):
                            last = nc.tensor.transpose(bt[:, (k * HC + c) * P:(k * HC + c + 1) * P],
                                                       hid[:, r, k, c * P:(c + 1) * P], ident[:, :])
                    last.then_inc(m_trh, 1)

                def down(q, r):
                    t = group(q, r)
                    experts = load_indices(nc, tile_expert[0:1, bass.ds(t * TE, TE)], E0)
                    wait_done(pe, m_hT, t)
                    wait_free(pe, m_yo, t, 1)
                    for k in range(TE):
                        for c in range(HC):
                            last = mm(by[:, k * P:(k + 1) * P], hidT[:, r, k, c * P:(c + 1) * P],
                                      w3_s[:, bass.ds(experts[k], 1), c, :].rearrange("p a c -> p (a c)"), start=c == 0, stop=c == HC - 1)
                    last.then_inc(m_y, 1)

                steps(pe, [(4, down), (3, tr_hid), (1, up), (0, tr)], EG)

            @block.scalar
            def _(act):
                for s in (m_xT, m_silu, m_yo):
                    act.sem_inc(s, CREDIT)

                def xT(q, r):
                    t = group(q, r)
                    wait_done(act, m_tr, t)
                    wait_free(act, m_h, t, 4)
                    nc.scalar.activation(xgT[:, r, :, :], bx[r % 2][:, 0:TE * P], ACT.Copy).then_inc(m_xT, 1)

                def silu(q, r):
                    t = group(q, r)
                    wait_done(act, m_h, t)
                    wait_free(act, m_hid, t, 4)
                    for k in range(TE):
                        last = nc.scalar.activation(gate[:, r, k, :], bh[r % 2][k][:, 0:HID], ACT.Silu)
                    last.then_inc(m_silu, 1)

                def y(q, r):
                    t = group(q, r)
                    wait_done(act, m_y, t)
                    wait_stored(act, y_st[r], q)
                    nc.scalar.activation(yo[:, r, :, :], by[:, 0:TE * P], ACT.Copy).then_inc(m_yo, 1)

                steps(act, [(4, y), (1, silu), (0, xT)], EG)

            @block.vector
            def _(dve):
                for s in (m_hid, m_hT):
                    dve.sem_inc(s, CREDIT)

                def mul(q, r):
                    t = group(q, r)
                    wait_done(dve, m_silu, t)
                    wait_free(dve, m_trh, t, 4)
                    for k in range(TE):
                        last = nc.vector.tensor_tensor(hid[:, r, k, :], gate[:, r, k, :], bh[r % 2][k][:, HID:2 * HID], ALU.mult)
                    last.then_inc(m_hid, 1)

                def hT(q, r):
                    t = group(q, r)
                    wait_done(dve, m_trh, t)
                    wait_free(dve, m_y, t, 4)
                    nc.vector.tensor_copy(hidT[:, r, :, :], bt[:, :]).then_inc(m_hT, 1)

                steps(dve, [(3, hT), (1, mul)], EG)

            @block.sync
            def _(sp):
                for r in range(4):
                    sp.sem_inc(y_st[r], 16)

                def store(q, r):
                    t = group(q, r)
                    wait_done(sp, m_yo, t)
                    sp.dma_start(y_d[bass.ds(t * (TE * P), TE * P), :].rearrange("(k p) f -> p k f", p=P),
                                 yo[:, r, :, :]).then_inc(y_st[r], 16)

                steps(sp, [(0, store)], EG)
                for r in range(4):
                    sp.wait_ge(y_st[r], 16 * (EG // 4 + 1))
        end_stage()
        scope.pop().close()
        scope.pop().close()

        c_x1, c_y, c_x3, c_sx = sems("c_x1"), sems("c_y"), sems("c_x3"), sems("c_sx")
        (c_ix, c_x2, c_p1, c_xn, c_tr, c_xnT, c_z, c_zs, c_h1, c_h1T, c_z2, c_z2s, c_h2, c_rl, c_xm, c_x3r, c_p2, c_xn4, c_sgn,
         c_tr4, c_xn4T, c_gate, c_oh, c_cntA, c_cntB, c_rkA, c_rkB, c_cnt) = [sem("c_" + n) for n in (
             "index x2 rstd xn transposed xnT z z_copied h1 h1T z2 z2_copied h2 relu xm x3 rstd3 xn3 sign transposed3 xn3T "
             "gate onehot countA countB rankA rankB counts").split()]
        c_vx, c_vy, c_vp, c_v0, c_nb, c_nb3, c_zb = [sem("c_" + n) for n in "link_x2 link_x3 link_pattern zeroed shift shift3 gate_biased".split()]
        scope.append(ExitStack())
        pat = sb("pat", [P, BATCH])
        rank1 = sb("rank1", [P, BATCH])
        scope.append(ExitStack())
        ix8 = sb("ix8", [P, 4, G * 2], I32)
        xa, yg = sb("c_xa", [P, 4, GW]), sb("yg", [P, 4, G * 2, P])
        t1, x2 = sb("t1", [P, GW]), sb("x2", [P, 4, GW])
        stats, mv, ve, nb = sb("stats", [P, G, 6]), sb("mv", [P, 4, G, 2]), sb("ve", [P, 4, G]), sb("nb", [P, 4, G])
        stats3, mv3, ve3, nb3 = sb("stats3", [P, G, 6]), sb("mv3", [P, 4, G, 2]), sb("ve3", [P, 4, G]), sb("nb3", [P, 4, G])
        xn, xnT, xm = sb("xn", [P, 4, GW]), sb("xnT", [P, 2, GW]), sb("xm", [P, 4, GW])
        zs, h1T, z2s, rl = sb("zs", [P, 2, GW]), sb("h1T", [P, 2, GW]), sb("z2s", [P, 2, GW]), sb("rl", [P, 2, GW])
        x3, xn4, xn4T, sx = sb("x3", [P, 4, GW]), sb("xn4", [P, 2, GW]), sb("xn4T", [P, 2, GW]), sb("sx", [P, 4, GW], BF16)
        zb, gbit = sb("zb", [P, G, E1]), sb("gbit", [P, G, E1])
        oh = sb("oh", [P, 4, G, PAT], BF16)
        junk = sb("junk", [P, G, PAT], BF16)
        bT, bZ, bH1, bZ2, bH2, bT4, bG, bR = psum
        with nc.Block() as block:
            @block.sync
            def _(sp):
                for r in range(4):
                    sp.sem_inc(c_x3[r], 16)
                    sp.sem_inc(c_sx[r], 16)

                def load(q, r):
                    t = group(q, r)
                    wait_free(sp, c_x2, t, 4)
                    alone(sp, ticks["sync"])
                    sp.dma_start(xa[:, r, :], x1_d[:, bass.ds(t * GW, GW)]).then_inc(c_x1[r], 16)

                def store_x(q, r):
                    t = group(q, r)
                    wait_done(sp, c_x3r, t)
                    alone(sp, ticks["sync"])
                    sp.dma_start(x2_d[:, bass.ds(t * GW, GW)], x3[:, r, :]).then_inc(c_x3[r], 16)

                def store_s(q, r):
                    t = group(q, r)
                    wait_done(sp, c_sgn, t)
                    alone(sp, ticks["sync"])
                    sp.dma_start(sx_v[:, bass.ds(t * GW, GW)], sx[:, r, :]).then_inc(c_sx[r], 16)

                steps(sp, [(0, load), (10, store_x), (12, store_s)], NG)
                for r in range(4):
                    sp.wait_ge(c_x3[r], 16 * (NG // 4 + 1))
                    sp.wait_ge(c_sx[r], 16 * (NG // 4 + 1))

            @block.gpsimd
            def _(pool):
                for s in (c_ix, c_p1, c_p2):
                    pool.sem_inc(s, CREDIT)

                def gather(q, r):
                    t = group(q, r)
                    wait_free(pool, c_x2, t, 4)
                    alone(pool, pt)
                    pool.tensor_copy(ix8[:, r, :], slot[:, bass.ds(t * G, G), :].rearrange("p g k -> p (g k)")).then_inc(c_ix, 1)
                    wait_done(pool, c_ix, t)
                    alone(pool, pt)
                    for c in range(2 * G):
                        pool.indirect_dma_start(yg[:, r, c, :], None, y_d,
                                                bass.IndirectOffsetOnAxis(ap=ix8[:, r, c:c + 1], axis=0)).then_inc(c_y[r], 16)

                def rstd(have, ve_, done):
                    def work(q, r):
                        t = group(q, r)
                        wait_done(pool, have, t)
                        alone(pool, pt)
                        pool.tensor_tensor(ve_[:, r, :], ve_[:, r, :], mhalf[:, :], ALU.pow).then_inc(done, 1)
                    return work

                steps(pool, [(9, rstd(c_x3r, ve3, c_p2)), (2, rstd(c_x2, ve, c_p1)), (0, gather)], NG)

            @block.vector
            def _(dve):
                v = nc.vector
                for s in (c_zb, c_nb, c_nb3, c_x2, c_xm, c_x3r, c_oh, c_rkA, c_rkB, c_z2s):
                    dve.sem_inc(s, CREDIT)
                lx, ly, lp = Links(dve, c_vx, 4), Links(dve, c_vy, 3), Links(dve, c_vp, 2)

                def combine(q, r):
                    t = group(q, r)
                    lx.at(t)
                    wait_loaded(dve, c_x1[r], q)
                    wait_loaded(dve, c_y[r], q, 2 * G)
                    wait_free(dve, c_xm, t, 4)
                    alone(dve, vt)
                    for k in range(2):
                        for j in range(G):
                            c = slice(j * P, (j + 1) * P)
                            last = v.scalar_tensor_tensor(t1[:, c] if k == 0 else x2[:, r, c], yg[:, r, 2 * j + k, :],
                                                          share[:, bass.ds(t * G + j, 1), k],
                                                          xa[:, r, c] if k == 0 else t1[:, c], ALU.mult, ALU.add)
                        lx.then(last)
                    alone(dve, vt)
                    lx.then(ln_stats(nc, lx, vt, stats, mv[:, r], x2[:, r, :]))
                    v.tensor_scalar(ve[:, r, :], mv[:, r, :, 1], EPS, None, ALU.add).then_inc(c_x2, 1)

                def shifts(rstd_done, mv_, ve_, nb_, done):
                    def work(q, r):
                        wait_done(dve, rstd_done, group(q, r))
                        v.scalar_tensor_tensor(nb_[:, r, :], mv_[:, r, :, 0], -1.0, ve_[:, r, :], ALU.mult, ALU.mult).then_inc(done, 1)
                    return work

                def half(q, r):
                    t = group(q, r)
                    wait_done(dve, c_xn, t)
                    wait_free(dve, c_x3r, t, 4)
                    v.scalar_tensor_tensor(xm[:, r, :], xn[:, r, :], 0.5, x2[:, r, :], ALU.mult, ALU.add).then_inc(c_xm, 1)

                def copy_z2(q, r):
                    t = group(q, r)
                    wait_done(dve, c_z2, t)
                    wait_free(dve, c_h2, t, 2)
                    v.tensor_copy(z2s[:, r % 2, :], bZ2[:, :]).then_inc(c_z2s, 1)

                def add_x3(q, r):
                    t = group(q, r)
                    ly.at(t)
                    wait_done(dve, c_rl, t)
                    wait_stored(dve, c_x3[r], q)
                    wait_free(dve, c_xn4, t, 4)
                    ly.then(v.tensor_tensor(x3[:, r, :], xm[:, r, :], rl[:, r % 2, :], ALU.add))
                    alone(dve, vt)
                    ly.then(ln_stats(nc, ly, vt, stats3, mv3[:, r], x3[:, r, :]))
                    v.tensor_scalar(ve3[:, r, :], mv3[:, r, :, 1], EPS, None, ALU.add).then_inc(c_x3r, 1)

                def patterns(q, r):
                    t = group(q, r)
                    lp.at(t)
                    wait_done(dve, c_gate, t)
                    v.tensor_tensor(zb[:, :, :], bG[:, 0:G * E1].rearrange("p (g e) -> p g e", g=G),
                                    pbias.unsqueeze(1).to_broadcast([P, G, E1]), ALU.add).then_inc(c_zb, 1)
                    wait_done(dve, c_zb, t)
                    lp.then(v.scalar_tensor_tensor(gbit[:, :, :], zb[:, :, :], 0.0, bits[:, :].unsqueeze(1).to_broadcast([P, G, E1]),
                                                   ALU.is_gt, ALU.mult))
                    lp.then(v.tensor_reduce(pat[:, bass.ds(t * G, G)], gbit[:, :, :], AX.X, ALU.add))
                    wait_free(dve, c_cntA, t, 3)
                    alone(dve, vt)
                    for j in range(G):
                        last = v.tensor_scalar(oh[:, r, j, :], count_bf[:, :], pat[:, bass.ds(t * G + j, 1)], None, ALU.is_equal)
                    last.then_inc(c_oh, 1)

                def ranks(h, counted, done):
                    def work(q, r):
                        t = group(q, r)
                        wait_done(dve, counted, t)
                        alone(dve, vt)
                        for j in range(2):
                            g = t * G + 2 * h + j
                            last = v.scalar_tensor_tensor(junk[:, 2 * h + j, :], count[:, 0:PAT], pat[:, bass.ds(g, 1)],
                                                          bR[:, j * PAT:(j + 1) * PAT], ALU.is_equal, ALU.mult,
                                                          accum_out=rank1[:, bass.ds(g, 1)])
                        last.then_inc(done, 1)
                    return work

                v.memset(oh[:, 3, 2, :], 0.0).then_inc(c_v0, 1)
                v.memset(oh[:, 3, 3, :], 0.0).then_inc(c_v0, 1)
                steps(dve, [(13, ranks(0, c_cntA, c_rkA)), (8, add_x3), (4, half), (13, ranks(1, c_cntB, c_rkB)), (6, copy_z2),
                            (12, patterns), (9, shifts(c_p2, mv3, ve3, nb3, c_nb3)),
                            (2, shifts(c_p1, mv, ve, nb, c_nb)), (1, combine)], NG)

            @block.scalar
            def _(act):
                s_ = nc.scalar
                for s in (c_xn, c_xnT, c_zs, c_h1T, c_rl, c_xn4, c_sgn, c_xn4T):
                    act.sem_inc(s, CREDIT)

                def norm(q, r):
                    t = group(q, r)
                    wait_done(act, c_nb, t)
                    wait_free(act, c_tr, t, 4)
                    wait_free(act, c_xm, t, 4)
                    for j in range(G):
                        c = slice(j * P, (j + 1) * P)
                        last = s_.activation(xn[:, r, c], x2[:, r, c], ACT.Identity, bias=nb[:, r, j:j + 1], scale=ve[:, r, j:j + 1])
                    last.then_inc(c_xn, 1)

                def copy_T(q, r):
                    t = group(q, r)
                    wait_done(act, c_tr, t)
                    wait_free(act, c_h1, t, 2)
                    s_.activation(xnT[:, r % 2, :], bT[:, :], ACT.Copy).then_inc(c_xnT, 1)

                def copy_z(q, r):
                    t = group(q, r)
                    wait_done(act, c_z, t)
                    wait_free(act, c_h1, t, 2)
                    s_.activation(zs[:, r % 2, :], bZ[:, :], ACT.Copy).then_inc(c_zs, 1)

                def relu1(q, r):
                    t = group(q, r)
                    wait_done(act, c_h1, t)
                    wait_free(act, c_h2, t, 2)
                    s_.activation(h1T[:, r % 2, :], bH1[:, :], ACT.Relu, bias=b1_s[:, :]).then_inc(c_h1T, 1)

                def relu2(q, r):
                    t = group(q, r)
                    wait_done(act, c_h2, t)
                    wait_free(act, c_x3r, t, 2)
                    s_.activation(rl[:, r % 2, :], bH2[:, :], ACT.Relu, scale=0.5).then_inc(c_rl, 1)

                def norm4(q, r):
                    t = group(q, r)
                    wait_done(act, c_nb3, t)
                    wait_free(act, c_tr4, t, 2)
                    for j in range(G):
                        c = slice(j * P, (j + 1) * P)
                        last = s_.activation(xn4[:, r % 2, c], x3[:, r, c], ACT.Identity, bias=nb3[:, r, j:j + 1], scale=ve3[:, r, j:j + 1])
                    last.then_inc(c_xn4, 1)
                    wait_done(act, c_xn4, t)
                    wait_stored(act, c_sx[r], q)
                    s_.activation(sx[:, r, :], xn4[:, r % 2, :], ACT.Sign).then_inc(c_sgn, 1)

                def copy_T4(q, r):
                    t = group(q, r)
                    wait_done(act, c_tr4, t)
                    wait_free(act, c_gate, t, 2)
                    s_.activation(xn4T[:, r % 2, :], bT4[:, :], ACT.Copy).then_inc(c_xn4T, 1)

                steps(act, [(3, norm), (10, norm4), (7, relu2), (5, relu1), (4, copy_z), (10, copy_T4), (3, copy_T)], NG)

            @block.tensor
            def _(pe):
                mm = nc.tensor.matmul
                for s in (c_tr, c_z, c_h1, c_z2, c_h2, c_tr4, c_gate, c_cntA, c_cntB):
                    pe.sem_inc(s, CREDIT)

                def cols(j):
                    return slice(j * P, (j + 1) * P)

                def tr(q, r):
                    t = group(q, r)
                    wait_done(pe, c_xn, t)
                    wait_free(pe, c_xnT, t, 1)
                    for j in range(G):
                        last = nc.tensor.transpose(bT[:, cols(j)], xn[:, r, cols(j)], ident[:, :])
                    last.then_inc(c_tr, 1)

                def first(q, r):
                    t = group(q, r)
                    wait_done(pe, c_xnT, t)
                    wait_free(pe, c_zs, t, 1)
                    for j in range(G):
                        last = mm(bZ[:, cols(j)], xnT[:, r % 2, cols(j)], w1n_s[:, :], start=True, stop=True)
                    last.then_inc(c_z, 1)

                def neigh1(q, r):
                    t = group(q, r)
                    wait_done(pe, c_zs, t)
                    wait_free(pe, c_h1T, t, 1)
                    mm(bH1[:, :], w1l_s[:, :], xnT[:, r % 2, :], start=True, stop=False)
                    for j in range(G):
                        last = mm(bH1[:, cols(j)], zs[:, r % 2, cols(j)], adjT_s[:, :], start=False, stop=j == G - 1)
                    last.then_inc(c_h1, 1)

                def second(q, r):
                    t = group(q, r)
                    wait_done(pe, c_h1T, t)
                    wait_free(pe, c_z2s, t, 1)
                    for j in range(G):
                        last = mm(bZ2[:, cols(j)], h1T[:, r % 2, cols(j)], w2n_s[:, :], start=True, stop=True)
                    last.then_inc(c_z2, 1)

                def neigh2(q, r):
                    t = group(q, r)
                    wait_done(pe, c_z2s, t)
                    wait_free(pe, c_rl, t, 1)
                    mm(bH2[:, :], ones_row[:, :], b2x[:, :], start=True, stop=False)
                    for j in range(G):
                        mm(bH2[:, cols(j)], h1T[:, r % 2, cols(j)], w2l_s[:, :], start=False, stop=False)
                    mm(bH2[:, :], adjT_s[:, :], z2s[:, r % 2, :], start=False, stop=True).then_inc(c_h2, 1)

                def tr4(q, r):
                    t = group(q, r)
                    wait_done(pe, c_xn4, t)
                    wait_free(pe, c_xn4T, t, 1)
                    for j in range(G):
                        last = nc.tensor.transpose(bT4[:, cols(j)], xn4[:, r % 2, cols(j)], ident[:, :])
                    last.then_inc(c_tr4, 1)

                def gates(q, r):
                    t = group(q, r)
                    wait_done(pe, c_xn4T, t)
                    wait_free(pe, c_zb, t, 1)
                    for j in range(G):
                        last = mm(bG[:, j * E1:(j + 1) * E1], xn4T[:, r % 2, cols(j)], projT_s[:, :], start=True, stop=True)
                    last.then_inc(c_gate, 1)

                def counts(r_was, h_was, r, h):
                    a, b, c, d = oh[:, r_was, 2 * h_was, :], oh[:, r_was, 2 * h_was + 1, :], oh[:, r, 2 * h, :], oh[:, r, 2 * h + 1, :]
                    for to, mine, whole, new in ((0, a, b, c), (1, b, c, d)):
                        reg = bR[:, to * PAT:(to + 1) * PAT]
                        mm(reg, not_before[:, :], mine, start=False, stop=False, skip_group_check=True)
                        mm(reg, ones_bf[:, :], whole, start=False, stop=False, skip_group_check=True)
                        last = mm(reg, before[:, :], new, start=False, stop=True, skip_group_check=True)
                    return last

                def countA(q, r):
                    t = group(q, r)
                    wait_done(pe, c_oh, t)
                    wait_free(pe, c_rkB, t, 1)
                    counts((r + 3) % 4, 1, r, 0).then_inc(c_cntA, 1)

                def countB(q, r):
                    t = group(q, r)
                    wait_done(pe, c_rkA, t)
                    counts(r, 0, r, 1).then_inc(c_cntB, 1)

                pe.wait_ge(c_v0, 2)
                mm(bR[:, :], zeros_bf[:, :], oh[:, 3, 2:4, :], start=True, stop=True, skip_group_check=True)
                steps(pe, [(13, countA), (7, neigh2), (6, second), (13, countB), (5, neigh1), (4, first), (10, tr4),
                           (3, tr), (11, gates)], NG)
                pe.wait_ge(c_rkB, NG + CREDIT)
                mm(bR[:, 0:PAT], not_before[:, :], oh[:, 3, 2, :], start=False, stop=False, skip_group_check=True)
                mm(bR[:, 0:PAT], ones_bf[:, :], oh[:, 3, 3, :], start=False, stop=True, skip_group_check=True).then_inc(c_cnt, 1)
        end_stage()
        scope.pop().close()

        d_v, d_mm, d_last, d_in, d_oh, d_used, d_pe = [sem("d_" + n) for n in "link mm last_block inside onehot used list".split()]
        d_st = sem("d_start_of")
        slot1 = sb("slot1", [P, BATCH], I32)
        tile_src, block_pat = sb("tile_src", [P, PT], I32), sb("block_pat", [1, NB * PT], I32)
        scope.append(ExitStack())
        need_i, need, last_b = sb("need_i", [P, PAT], I32), sb("need", [P, PAT]), sb("last_b", [P, PAT])
        start, endcol = sb("start", [P, PAT]), sb("endcol", [P, 2])
        inside = sb("inside", [P, 2, NB * PT], BF16)
        start_of, slot_f = sb("start_of", [P, BATCH]), sb("slot_f", [P, BATCH])
        lo_i, hi_i, lo, hi = sb("lo_i", [P, BATCH], I32), sb("hi_i", [P, BATCH], I32), sb("lo", [P, BATCH]), sb("hi", [P, BATCH])
        lo_row, lo_graph, hi_is = sb("lo_row", [P, 4, P], BF16), sb("lo_graph", [P, 4, P], BF16), sb("hi_is", [P, 4, PT], BF16)
        junk = sb("junk", [P, 4, PAT], BF16)
        HB = NB * PT // 2
        with nc.Block() as block:
            @block.vector
            def _(dve):
                v = nc.vector
                dve.sem_inc(d_oh, CREDIT)
                dve.sem_inc(d_st, CREDIT)
                link = Links(dve, d_v)
                counted = psum[7][:, 0:PAT]
                link.then(v.tensor_scalar(need[:, :], counted, float(PB - 1), None, ALU.add))
                link.then(v.tensor_copy(need_i[:, :], need[:, :]))
                link.then(v.tensor_scalar(need_i[:, :], need_i[:, :], 5, None, ALU.arith_shift_right))
                link.then(v.tensor_copy(need[:, :], need_i[:, :]))
                v.tensor_tensor_scan(last_b[:, :], need[:, :], need[:, :], 0.0, ALU.add, ALU.max).then_inc(d_last, 1)
                dve.wait_ge(d_last, 1)
                link.then(v.tensor_tensor(start[:, :], last_b[:, :], need[:, :], ALU.subtract))
                link.then(v.tensor_scalar(start[:, :], start[:, :], float(PB), None, ALU.mult))
                dve.wait_ge(d_mm, 1)
                for h in range(2):
                    last = v.tensor_copy(endcol[:, h:h + 1], psum[0][:, h * P:h * P + 1])
                link.then(last)
                for h in range(2):
                    last = v.tensor_scalar(inside[:, h, :], count[:, :], endcol[:, h:h + 1], None, ALU.is_ge)
                last.then_inc(d_in, 1)

                def starts(q, r):
                    t = group(q, r)
                    wait_free(dve, d_st, t, 4)
                    alone(dve, vt)
                    v.scalar_tensor_tensor(junk[:, r, :], count[:, 0:PAT], pat[:, bass.ds(t, 1)], start[:, :],
                                                  ALU.is_equal, ALU.mult, accum_out=start_of[:, bass.ds(t, 1)]).then_inc(d_st, 1)

                steps(dve, [(0, starts)], BATCH)
                dve.wait_ge(d_st, BATCH + CREDIT)
                link.then(v.tensor_tensor(slot_f[:, :], start_of[:, :], rank1[:, :], ALU.add))
                link.then(v.tensor_copy(slot1[:, :], slot_f[:, :]))
                v.tensor_scalar(lo_i[:, :], slot1[:, :], P - 1, None, ALU.bitwise_and)
                link.then(v.tensor_scalar(hi_i[:, :], slot1[:, :], 7, None, ALU.arith_shift_right))
                v.tensor_copy(lo[:, :], lo_i[:, :])
                link.then(v.tensor_copy(hi[:, :], hi_i[:, :]))
                dve.wait_ge(d_mm, 2)
                for h in range(2):
                    last = v.tensor_scalar(block_pat[:, h * HB:(h + 1) * HB], psum[1 + h][0:1, 0:HB], float(PAT - 1), None, ALU.min)
                link.then(last)

                def onehots(q, r):
                    t = group(q, r)
                    wait_free(dve, d_used, t, 4)
                    v.tensor_scalar(lo_row[:, r, :], count_bf[:, 0:P], lo[:, bass.ds(t, 1)], row_id[:, :], ALU.is_equal, ALU.mult)
                    v.tensor_scalar(lo_graph[:, r, :], count_bf[:, 0:P], lo[:, bass.ds(t, 1)], count[:, bass.ds(t, 1)],
                                    ALU.is_equal, ALU.mult)
                    v.tensor_scalar(hi_is[:, r, :], count_bf[:, 0:PT], hi[:, bass.ds(t, 1)], None, ALU.is_equal).then_inc(d_oh, 1)

                steps(dve, [(0, onehots)], BATCH)
                dve.wait_ge(d_pe, 1)
                link.then(v.tensor_copy(tile_src[:, :], psum[3][:, 0:PT]))

            @block.tensor
            def _(pe):
                mm = nc.tensor.matmul
                pe.sem_inc(d_used, CREDIT)
                pe.wait_ge(d_last, 1)
                for h in range(2):
                    last = nc.tensor.transpose(psum[0][:, h * P:(h + 1) * P], last_b[:, h * P:(h + 1) * P], ident[:, :])
                last.then_inc(d_mm, 1)
                pe.wait_ge(d_in, 1)
                for h in range(2):
                    for k in range(2):
                        last = mm(psum[1 + h][0:1, 0:HB], ones_bf[:, 0:1], inside[:, k, h * HB:(h + 1) * HB], start=k == 0, stop=k == 1)
                last.then_inc(d_mm, 1)
                rows_of = psum[3][:, 0:PT]
                mm(rows_of, zeros_bf[:, :], count_bf[:, 0:PT], start=True, stop=False)

                def fill(q, r):
                    wait_done(pe, d_oh, group(q, r))
                    mm(rows_of, lo_row[:, r, :], hi_is[:, r, :], start=False, stop=False)
                    mm(rows_of, lo_graph[:, r, :], hi_is[:, r, :], start=False, stop=False).then_inc(d_used, 1)

                steps(pe, [(0, fill)], BATCH)
                mm(rows_of, zeros_bf[:, :], count_bf[:, 0:PT], start=False, stop=True).then_inc(d_pe, 1)
        end_stage()
        scope.pop().close()

        b_in, b_st = sems("b_in"), sems("b_st")
        b_ix, b_tr, b_xT, b_y, b_yv, b_ya = [sem("b_" + n) for n in "index transposed xT y y_vector y_scalar".split()]
        scope.append(ExitStack())
        ix = sb("ix", [P, 4, TG], I32)
        xs, xsT, yb_s = sb("xs", [P, 4, TG, P], BF16), sb("xsT", [P, 4, TG * P], BF16), sb("yb_s", [PB, 4, TG, NB * P], BF16)
        bx = [psum[0], psum[1]]
        by = [psum[2 + k] for k in range(TG)]
        with nc.Block() as block:
            @block.gpsimd
            def _(pool):
                pool.sem_inc(b_ix, CREDIT)

                def index(q, r):
                    t = group(q, r)
                    wait_free(pool, b_tr, t, 4)
                    alone(pool, pt)
                    pool.tensor_copy(ix[:, r, :], tile_src[:, bass.ds(t * TG, TG)]).then_inc(b_ix, 1)

                def gather(q, r):
                    wait_done(pool, b_ix, group(q, r))
                    alone(pool, pt)
                    for k in range(TG):
                        pool.indirect_dma_start(xs[:, r, k, :], None, sx_d,
                                                bass.IndirectOffsetOnAxis(ap=ix[:, r, k:k + 1], axis=0)).then_inc(b_in[r], 16)

                steps(pool, [(0, index), (1, gather)], PT // TG)

            @block.tensor
            def _(pe):
                mm = nc.tensor.matmul
                for s in (b_tr, b_y):
                    pe.sem_inc(s, CREDIT)

                def tr(q, r):
                    t = group(q, r)
                    wait_loaded(pe, b_in[r], q, TG)
                    wait_free(pe, b_xT, t, 2)
                    for k in range(TG):
                        last = nc.tensor.transpose(bx[r % 2][:, 0:2 * P].bitcast(BF16)[:, k * P:(k + 1) * P], xs[:, r, k, :],
                                                   ident_bf[:, :])
                    last.then_inc(b_tr, 1)

                def apply(q, r):
                    t = group(q, r)
                    for k in range(TG):
                        pats = load_indices(nc, block_pat[0:1, bass.ds(t * (TG * NB) + k * NB, NB)], PAT)
                        if k == 0:
                            wait_done(pe, b_xT, t)
                        wait_free(pe, b_ya if k % 2 else b_yv, t * 2 + k // 2, 2)
                        for j in range(NB):
                            c = k * P + j * PB
                            last = mm(by[k][0:PB, j * P:(j + 1) * P], xsT[:, r, c:c + PB],
                                      signs[:, bass.ds(pats[j], 1), :].rearrange("p a c -> p (a c)"), start=True, stop=True)
                        last.then_inc(b_y, 1)

                steps(pe, [(0, tr), (1, apply)], PT // TG)

            @block.scalar
            def _(act):
                for s in (b_xT, b_ya):
                    act.sem_inc(s, CREDIT)

                def xT(q, r):
                    t = group(q, r)
                    wait_done(act, b_tr, t)
                    nc.scalar.activation(xsT[:, r, :], bx[r % 2][:, 0:2 * P].bitcast(BF16), ACT.Copy).then_inc(b_xT, 1)

                def y(q, r):
                    t = group(q, r)
                    wait_stored(act, b_st[r], q)
                    for k in (1, 3):
                        wait_done(act, b_y, t * TG + k)
                        nc.scalar.activation(yb_s[:, r, k, :], by[k][0:PB, :], ACT.Copy).then_inc(b_ya, 1)

                steps(act, [(0, xT), (1, y)], PT // TG)

            @block.vector
            def _(dve):
                dve.sem_inc(b_yv, CREDIT)

                def y(q, r):
                    t = group(q, r)
                    wait_stored(dve, b_st[r], q)
                    for k in (0, 2):
                        wait_done(dve, b_y, t * TG + k)
                        alone(dve, vt)
                        nc.vector.tensor_copy(yb_s[:, r, k, :], by[k][0:PB, :]).then_inc(b_yv, 1)

                steps(dve, [(0, y)], PT // TG)

            @block.sync
            def _(sp):
                for r in range(4):
                    sp.sem_inc(b_st[r], 16)

                def store(q, r):
                    t = group(q, r)
                    wait_done(sp, b_yv, t * 2 + 1)
                    wait_done(sp, b_ya, t * 2 + 1)
                    alone(sp, ticks["sync"])
                    sp.dma_start(yb_d[bass.ds(t * (TG * P), TG * P), :].rearrange("(j p) o -> p j o", p=PB),
                                 yb_s[:, r, :, :].rearrange("p k (j o) -> p (k j) o", j=NB)).then_inc(b_st[r], 16)

                steps(sp, [(0, store)], PT // TG)
                for r in range(4):
                    sp.wait_ge(b_st[r], 16 * (PT // TG // 4 + 1))
        end_stage()
        scope.pop().close()

        e_x, e_y, e_st = sems("e_x"), sems("e_y"), sems("e_st")
        e_ix, e_o, e_l = sem("e_index"), sem("e_out"), sem("e_link")
        scope.append(ExitStack())
        ix4 = sb("ix4", [P, 4, G], I32)
        xe, ye, oe = sb("xe", [P, 4, GW]), sb("ye", [P, 4, G, P], BF16), sb("oe", [P, 4, GW])
        with nc.Block() as block:
            @block.sync
            def _(sp):
                for r in range(4):
                    sp.sem_inc(e_st[r], 16)

                def load(q, r):
                    t = group(q, r)
                    wait_free(sp, e_o, t, 4)
                    alone(sp, ticks["sync"])
                    sp.dma_start(xe[:, r, :], x2_d[:, bass.ds(t * GW, GW)]).then_inc(e_x[r], 16)

                def store(q, r):
                    t = group(q, r)
                    wait_done(sp, e_o, t)
                    alone(sp, ticks["sync"])
                    sp.dma_start(out_v[:, bass.ds(t * GW, GW)], oe[:, r, :]).then_inc(e_st[r], 16)

                steps(sp, [(2, store), (0, load)], NG)
                for r in range(4):
                    sp.wait_ge(e_st[r], 16 * (NG // 4 + 1))

            @block.gpsimd
            def _(pool):
                pool.sem_inc(e_ix, CREDIT)

                def gather(q, r):
                    t = group(q, r)
                    wait_free(pool, e_o, t, 4)
                    alone(pool, pt)
                    pool.tensor_copy(ix4[:, r, :], slot1[:, bass.ds(t * G, G)]).then_inc(e_ix, 1)
                    wait_done(pool, e_ix, t)
                    alone(pool, pt)
                    for j in range(G):
                        pool.indirect_dma_start(ye[:, r, j, :], None, yb_d,
                                                bass.IndirectOffsetOnAxis(ap=ix4[:, r, j:j + 1], axis=0)).then_inc(e_y[r], 16)

                steps(pool, [(0, gather)], NG)

            @block.vector
            def _(dve):
                v = nc.vector
                dve.sem_inc(e_o, CREDIT)
                link = Links(dve, e_l, 1)

                def add(q, r):
                    t = group(q, r)
                    link.at(t)
                    wait_loaded(dve, e_x[r], q)
                    wait_loaded(dve, e_y[r], q, G)
                    wait_stored(dve, e_st[r], q)
                    link.then(v.tensor_tensor(as3(oe[:, r, :]), ye[:, r, :, :], scale.unsqueeze(1).to_broadcast([P, G, P]), ALU.mult))
                    v.tensor_tensor(oe[:, r, :], oe[:, r, :], xe[:, r, :], ALU.add).then_inc(e_o, 1)

                steps(dve, [(0, add)], NG)
        end_stage()
        while len(scope) > 1:
            scope.pop().close()


_OUTS = [((P, BATCH, P), "float32")]


def kernel(x, adj, L0_gnn_W, L0_gnn_a, L0_ffn_gate_w, L0_ffn_gate_b, L0_ffn_w1, L0_ffn_w2, L0_ffn_w3, L1_gnn_w1_loop,
           L1_gnn_w1_neigh, L1_gnn_b1, L1_gnn_w2_loop, L1_gnn_w2_neigh, L1_gnn_b2, L1_ffn_weight, L1_ffn_proj_w,
           L1_ffn_proj_b, L1_ffn_scale):
    import numpy as _np
    import concourse.bacc as _bacc
    from concourse import mybir as _mybir
    from concourse.bass_utils import run_bass_kernel_spmd as _run

    w3 = _np.asarray(L0_ffn_w3).reshape(E0, HID // P, P, P)
    laid = {
        "xt": _np.asarray(x).transpose(1, 0, 2),
        "adj": adj, "adjT": _np.asarray(adj).T,
        "W": L0_gnn_W, "WT": _np.asarray(L0_gnn_W).T, "a12": _np.asarray(L0_gnn_a).reshape(2, P).T,
        "gate_w": L0_ffn_gate_w,
        "w12": _np.concatenate([_np.asarray(L0_ffn_w1), _np.asarray(L0_ffn_w2)], axis=2).transpose(1, 0, 2),
        "w3": w3.transpose(2, 0, 1, 3),
        "w1l": L1_gnn_w1_loop, "w1n": L1_gnn_w1_neigh, "w2l": L1_gnn_w2_loop, "w2n": L1_gnn_w2_neigh,
        "b1": _np.asarray(L1_gnn_b1).reshape(P, 1), "b2": _np.asarray(L1_gnn_b2).reshape(1, P),
        "rows": _np.concatenate([_np.asarray(L0_ffn_gate_b), _np.asarray(L1_ffn_proj_b),
                                 _np.asarray(L1_ffn_scale).reshape(P)]).reshape(1, E0 + E1 + P),
        "wgt": _np.asarray(L1_ffn_weight)[0].transpose(1, 0, 2),
        "projT": _np.asarray(L1_ffn_proj_w).T,
    }
    nc = _bacc.Bacc("TRN2", target_bir_lowering=False, num_devices=1)
    arrays, args = {}, []
    for name, a in laid.items():
        a = _np.ascontiguousarray(a)
        arrays[f"in_{name}_dram"] = a
        args.append(nc.dram_tensor(f"in_{name}_dram", a.shape, _mybir.dt.from_np(a.dtype), kind="ExternalInput").ap())
    for i, (shape, dtype) in enumerate(_OUTS):
        dt = _mybir.dt.from_np(_np.dtype(dtype))
        args.append(nc.dram_tensor(f"out_{i}_dram", shape, dt, kind="ExternalOutput").ap())
    build(nc, *args)
    r = _run(nc, [arrays], core_ids=[0])
    return r.results[0]["out_0_dram"].transpose(1, 0, 2)
```

```python
import concourse.bass as bass
from concourse import mybir
from contextlib import ExitStack

F32 = mybir.dt.float32
F32R = mybir.dt.float32r
BF16 = mybir.dt.bfloat16
I32 = mybir.dt.int32
U32 = mybir.dt.uint32
ALU = mybir.AluOpType
ACT = mybir.ActivationFunctionType
AX = mybir.AxisListType

P = 128
BATCH = 128
G = 4
NG = BATCH // G
GW = G * P
TOKENS = BATCH * P
E0 = 16
HID = 256
MT = 2 * TOKENS // P + E0
E1 = 8
PAT = 1 << E1
PB = 32
PT = (TOKENS // PB + PAT) * PB // P
NB = P // PB
TG = 8
TE = 2
EPS = 1e-5
SLOPE = 0.2
MASKED = -1e30


def steps(eng, stages, groups, ring=4):
    last = max(lag for lag, _ in stages)
    head = last
    while (groups - head) % ring:
        head += 1

    def step(i):
        for lag, work in stages:
            if 0 <= i - lag < groups:
                work((i - lag) // ring, (i - lag) % ring)

    for i in range(head):
        step(i)
    if groups > head:
        with eng.Fori(0, (groups - head) // ring) as n:
            for u in range(ring):
                for lag, work in stages:
                    work(n + (head + u - lag) // ring, (head + u - lag) % ring)
    for i in range(groups, groups + last):
        step(i)


def group(q, r, ring=4):
    return ring * q + r


def as3(ap, n=G):
    return ap.rearrange("p (g c) -> p g c", g=n)


CREDIT = 4


def wait_done(eng, sem, t):
    eng.wait_ge(sem, t + (1 + CREDIT))


def wait_free(eng, sem, t, ring):
    eng.wait_ge(sem, t + (1 + CREDIT - ring))


def wait_loaded(eng, sem, q, copies=1):
    eng.wait_ge(sem, (q + 1) * (16 * copies))


def wait_stored(eng, sem, q):
    eng.wait_ge(sem, (q + 1) * 16)


class Links:

    def __init__(self, eng, sem, per_group=0):
        self.eng, self.sem, self.per_group, self.base, self.n = eng, sem, per_group, 0, 0

    def at(self, t):
        self.base, self.n = t * self.per_group, 0

    def then(self, ins):
        self.n += 1
        assert not self.per_group or self.n <= self.per_group
        ins.then_inc(self.sem, 1)
        self.eng.wait_ge(self.sem, self.base + self.n)


def alone(eng, ticks):
    eng.sem_inc(ticks, 1)


def load_indices(nc, row, limit):
    return nc.values_load_multi_w_load_instructions(
        row, engines=[mybir.EngineType.PE], min_val=0, max_val=limit - 1,
        skip_runtime_bounds_check_because="the table counts ranges that ended, and a minimum caps it at limit - 1")[1]


def stats_of(nc, ticks, src, have, st, used, done):
    def work(q, r):
        wait_done(nc.vector, have, group(q, r))
        wait_free(nc.vector, used, group(q, r), 1)
        alone(nc.vector, ticks)
        for j in range(G):
            last = nc.vector.bn_stats(st[:, j, :], src[:, r, j * P:(j + 1) * P])
        last.then_inc(done, 1)
    return work


def moments(nc, ticks, st, have, mv, done):
    def work(q, r):
        wait_done(nc.vector, have, group(q, r))
        alone(nc.vector, ticks)
        for j in range(G):
            last = nc.vector.bn_aggr(mv[:, r, j, :], st[:, j, :])
        last.then_inc(done, 1)
    return work


def build(nc, xt, adj, adjT, W, WT, a12, gate_w, w12, w3, w1l, w1n, w2l, w2n, b1, b2, rows, wgt, projT, out):
    ctx = ExitStack()
    scope = [ctx]
    taken = set()

    def sb(name, shape, dt=F32):
        name = f"{name}_{len(taken)}" if name in taken else name
        taken.add(name)
        return scope[-1].enter_context(nc.sbuf_tensor(name, shape, dt))

    stage_sems = []

    def sem(name):
        stage_sems.append(nc.alloc_semaphore(name=name))
        return stage_sems[-1]

    def end_stage():
        nc.clear_and_free_semaphores(stage_sems)
        stage_sems.clear()
        nc.all_engine_barrier()

    ticks = {}
    for name in ("pool", "vector", "scalar", "tensor", "sync"):
        ticks[name] = ctx.enter_context(nc.semaphore(f"{name}_ticks"))
    vt, pt = ticks["vector"], ticks["pool"]

    def sems(name, n=4):
        return [sem(f"{name}{i}") for i in range(n)]

    with ctx:
        x1_d = nc.dram_tensor("x1_d", [P, BATCH * P], F32, kind="Internal").ap()
        x2_d = nc.dram_tensor("x2_d", [P, BATCH * P], F32, kind="Internal").ap()
        xn_d = nc.dram_tensor("xn_d", [TOKENS, P], F32, kind="Internal").ap()
        y_d = nc.dram_tensor("y_d", [MT * P, P], F32, kind="Internal").ap()
        sx_d = nc.dram_tensor("sx_d", [TOKENS, P], BF16, kind="Internal").ap()
        sorted_d = nc.dram_tensor("sorted_d", [PT * P, P], BF16, kind="Internal").ap()
        yb_d = nc.dram_tensor("yb_d", [PT * P, P], BF16, kind="Internal").ap()
        xt_v = xt.rearrange("n b f -> n (b f)")
        out_v = out.rearrange("n b f -> n (b f)")
        xn_v = xn_d.rearrange("(n b) f -> n (b f)", b=BATCH)
        sx_v = sx_d.rearrange("(n b) f -> n (b f)", b=BATCH)

        psum = [ctx.enter_context(nc.psum_tensor(f"bank{i}", [P, 512], F32)) for i in range(8)]

        ident = sb("ident", [P, P])
        ident_bf = sb("ident_bf", [P, P], BF16)
        before = sb("before", [P, P], BF16)
        not_before = sb("not_before", [P, P], BF16)
        ones_bf = sb("ones_bf", [P, P], BF16)
        zeros_bf = sb("zeros_bf", [P, P], BF16)
        ones_row = sb("ones_row", [1, P])
        mhalf = sb("mhalf", [P, G])
        eps_s = sb("eps_s", [P, 1])
        count_i = sb("count_i", [P, NB * PT], I32)
        count = sb("count", [P, NB * PT])
        count_bf = sb("count_bf", [P, 256], BF16)
        hi_zero = sb("hi_zero", [P, MT + 1], BF16)
        row_i = sb("row_i", [P, 1], I32)
        row_id = sb("row_id", [P, 1])
        mask = sb("mask", [P, P], BF16)
        W_s = sb("W_s", [P, P])
        WT_s = sb("WT_s", [P, P])
        a12_s = sb("a12_s", [P, 2])
        Waug = sb("Waug", [P, P + 2])
        wa2 = sb("wa2", [P, P])
        adj_s = sb("adj_s", [P, P])
        adjT_s = sb("adjT_s", [P, P])
        gw_s = sb("gw_s", [P, E0])
        rows_s = sb("rows_s", [1, E0 + E1 + P])
        rows_b = sb("rows_b", [P, E0 + E1 + P])
        gbias = rows_b[:, 0:E0]
        pbias = rows_b[:, E0:E0 + E1]
        scale = rows_b[:, E0 + E1:]
        w1l_s = sb("w1l_s", [P, P])
        w1n_s = sb("w1n_s", [P, P])
        w2l_s = sb("w2l_s", [P, P])
        w2n_s = sb("w2n_s", [P, P])
        b1_s = sb("b1_s", [P, 1])
        b2_s = sb("b2_s", [1, P])
        b2x = sb("b2x", [1, GW])
        projT_s = sb("projT_s", [P, E1])
        bits = sb("bits", [P, E1])
        expert = sb("expert", [P, BATCH, 2])
        top = sb("top", [P, BATCH, 2])
        share = sb("share", [P, BATCH, 2])
        slot = sb("slot", [P, BATCH, 2], I32)
        wsum_lo = sb("wsum_lo", [P, 16, P])
        wsum_hi = sb("wsum_hi", [P, 16, P])

        s_ld, s_pc, s_vc, s_mm = sem("const_loaded"), sem("pool_consts"), sem("vector_consts"), sem("const_mm")
        loads = [(W_s, W), (WT_s, WT), (a12_s, a12), (adj_s, adj), (adjT_s, adjT), (gw_s, gate_w), (rows_s, rows),
                 (w1l_s, w1l), (w1n_s, w1n), (w2l_s, w2l), (w2n_s, w2n), (b1_s, b1), (b2_s, b2), (projT_s, projT)]
        scope.append(ExitStack())
        wgt_s = sb("wgt_s", [P, E1, P])
        with nc.Block() as block:
            @block.sync
            def _(sp):
                for dst, src in loads:
                    sp.dma_start(dst[:, :], src).then_inc(s_ld, 16)
                sp.dma_start(wgt_s[:, :, :], wgt).then_inc(s_ld, 16)

            @block.gpsimd
            def _(pool):
                link = Links(pool, s_pc)
                pool.memset(zeros_bf[:, :], 0.0)
                pool.memset(ones_bf[:, :], 1.0)
                pool.memset(not_before[:, :], 1.0)
                pool.memset(ones_row[:, :], 1.0)
                pool.memset(mhalf[:, :], -0.5)
                pool.memset(eps_s[:, :], EPS)
                pool.memset(ident[:, :], 0.0)
                pool.memset(ident_bf[:, :], 0.0)
                link.then(pool.memset(before[:, :], 0.0))
                pool.affine_select(out=ident[:, :], in_=ident[:, :], compare_op=ALU.not_equal, fill=1.0, base=0,
                                   pattern=[[-1, P]], channel_multiplier=1)
                pool.affine_select(out=ident_bf[:, :], in_=ident_bf[:, :], compare_op=ALU.not_equal, fill=1.0, base=0,
                                   pattern=[[-1, P]], channel_multiplier=1)
                pool.affine_select(out=before[:, :], in_=before[:, :], compare_op=ALU.is_ge, fill=1.0, base=0,
                                   pattern=[[-1, P]], channel_multiplier=1)
                pool.affine_select(out=not_before[:, :], in_=not_before[:, :], compare_op=ALU.is_ge, fill=0.0, base=0,
                                   pattern=[[-1, P]], channel_multiplier=1)
                pool.iota(row_i[:, :], pattern=[[0, 1]], base=0, channel_multiplier=P)
                link.then(pool.iota(count_i[:, :], pattern=[[1, NB * PT]], base=0, channel_multiplier=0))

            @block.vector
            def _(dve):
                link = Links(dve, s_vc)
                v = nc.vector
                dve.wait_ge(s_pc, 2)
                for g in range(E1):
                    v.memset(bits[:, g:g + 1], float(1 << g))
                v.tensor_copy(count[:, :], count_i[:, :])
                v.tensor_copy(row_id[:, :], row_i[:, :])
                v.memset(wsum_lo[:, 0, :], 0.0)
                v.memset(wsum_hi[:, 0, :], 0.0)
                link.then(v.tensor_copy(count_bf[:, :], count_i[:, 0:256]))
                v.memset(hi_zero[:, :], 0.0)
                dve.wait_ge(s_ld, 16 * (len(loads) + 1))
                v.tensor_scalar(mask[:, :], adj_s[:, :], 0.0, MASKED, ALU.is_equal, ALU.mult)
                for g in range(4):
                    n = 1 << g
                    v.tensor_tensor(wsum_lo[:, n:2 * n, :], wsum_lo[:, 0:n, :],
                                    wgt_s[:, g, :].unsqueeze(1).to_broadcast([P, n, P]), ALU.add)
                    link.then(v.tensor_tensor(wsum_hi[:, n:2 * n, :], wsum_hi[:, 0:n, :],
                                              wgt_s[:, 4 + g, :].unsqueeze(1).to_broadcast([P, n, P]), ALU.add))
                v.tensor_copy(Waug[:, 0:P], W_s[:, :])
                v.tensor_copy(b2x[:, :].rearrange("p (g c) -> p g c", g=G), b2_s[:, :].unsqueeze(1).to_broadcast([1, G, P]))
                dve.wait_ge(s_mm, 1)
                v.tensor_copy(Waug[:, P:P + 2], psum[0][:, 0:2])
                v.tensor_copy(wa2[:, :], psum[0][:, 1:2].to_broadcast([P, P]))
                dve.wait_ge(s_mm, 2)
                link.then(v.tensor_copy(rows_b[:, :], psum[1][:, 0:E0 + E1 + P]))

            @block.tensor
            def _(pe):
                pe.wait_ge(s_ld, 16 * (len(loads) + 1))
                pe.wait_ge(s_pc, 2)
                nc.tensor.matmul(psum[0][:, 0:2], WT_s[:, :], a12_s[:, :], start=True, stop=True).then_inc(s_mm, 1)
                nc.tensor.matmul(psum[1][:, 0:E0 + E1 + P], ones_row[:, :], rows_s[:, :], start=True, stop=True).then_inc(s_mm, 1)
        end_stage()
        scope.pop().close()

        xa_in, xd_in, x1_st, xn_st = sems("xa_in"), sems("xd_in"), sems("x1_st"), sems("xn_st")
        a_stats, a_xn, a_tr, a_xnT = sem("a_stats"), sem("a_xn"), sem("a_transposed"), sem("a_xnT")
        a_wh, a_whs, a_max, a_exp = sem("a_wh"), sem("a_wh_copied"), sem("a_max"), sem("a_exp")
        a_p = sem("a_p")
        a_sc = sem("a_scores")
        a_att, a_attT, a_av, a_x1 = sem("a_att"), sem("a_attT"), sem("a_av"), sem("a_x1")
        a_xn2, a_tr2, a_xn2T, a_gate = sem("a_xn2"), sem("a_transposed2"), sem("a_xn2T"), sem("a_gate")
        a_rstd, a_rstd2, a_nb = sem("a_rstd"), sem("a_rstd2"), sem("a_shift2")
        a_st, a_maxs2, a_maxs, a_leaky, a_inv, a_st2, a_top, a_idx, a_kept = [sem("a_" + n) for n in (
            "x_stats max_s2 max_s leaky_max inverse_sum x1_stats top_values top_experts top_kept").split()]
        a_pa, a_pd = sem("a_link_rstd"), sem("a_link_rstd2")
        a_avu, a_lg = sem("a_av_used"), sem("a_logits")
        scope.append(ExitStack())
        xa, xd, xo = sb("xa", [P, 4, GW]), sb("xd", [P, 4, GW]), sb("xo", [P, 4, GW])
        stats, mv, ve = sb("stats", [P, G, 6]), sb("mv", [P, 4, G, 2]), sb("ve", [P, 4, G])
        xn, xnT, wh = sb("xn", [P, 2, GW]), sb("xnT", [P, 2, GW]), sb("wh", [P, 4, 2, 2 * (P + 2)])
        rmax, shift, rsum = sb("rmax", [P, 3, G]), sb("shift", [P, 4, 2, G]), sb("rsum", [P, 4, G])
        pos, neg = sb("pos", [P, 2, GW]), sb("neg", [P, 2, GW])
        att, attT = sb("att", [P, 2, GW]), sb("attT", [P, 2, GW])
        stats2, mv2, ve2, nb2 = sb("stats2", [P, G, 6]), sb("mv2", [P, 4, G, 2]), sb("ve2", [P, 4, G]), sb("nb2", [P, 4, G])
        xn2, xn2T = sb("xn2", [P, 4, GW]), sb("xn2T", [P, 2, GW])
        lg, top8, idx8 = sb("lg", [P, G, E0]), sb("top8", [P, G, 8]), sb("idx8", [P, G, 8], U32)
        whp = [psum[1], psum[2]]

        with nc.Block() as block:
            @block.sync
            def _(sp):
                for r in range(4):
                    sp.sem_inc(x1_st[r], 16)
                    sp.sem_inc(xn_st[r], 16)

                def load_a(q, r):
                    wait_free(sp, a_xn, group(q, r), 4)
                    sp.dma_start(xa[:, r, :], xt_v[:, bass.ds(group(q, r) * GW, GW)]).then_inc(xa_in[r], 16)

                def load_d(q, r):
                    wait_free(sp, a_x1, group(q, r), 4)
                    sp.dma_start(xd[:, r, :], xt_v[:, bass.ds(group(q, r) * GW, GW)]).then_inc(xd_in[r], 16)

                def store(q, r):
                    wait_done(sp, a_x1, group(q, r))
                    sp.dma_start(x1_d[:, bass.ds(group(q, r) * GW, GW)], xo[:, r, :]).then_inc(x1_st[r], 16)

                def store_xn(q, r):
                    wait_done(sp, a_xn2, group(q, r))
                    sp.dma_start(xn_v[:, bass.ds(group(q, r) * GW, GW)], xn2[:, r, :]).then_inc(xn_st[r], 16)

                steps(sp, [(12, store_xn), (11, store), (7, load_d), (0, load_a)], NG)
                for r in range(4):
                    sp.wait_ge(x1_st[r], 16 * (NG // 4 + 1))
                    sp.wait_ge(xn_st[r], 16 * (NG // 4 + 1))

            @block.gpsimd
            def _(pool):
                for s in (a_rstd, a_rstd2, a_xn):
                    pool.sem_inc(s, CREDIT)
                la, ld = Links(pool, a_pa, 1), Links(pool, a_pd, 1)

                def rstd_a(q, r):
                    t = group(q, r)
                    la.at(t)
                    wait_done(pool, a_stats, t)
                    wait_free(pool, a_xn, t, 4)
                    alone(pool, pt)
                    la.then(pool.tensor_scalar(ve[:, r, :], mv[:, r, :, 1], EPS, None, ALU.add))
                    pool.tensor_tensor(ve[:, r, :], ve[:, r, :], mhalf[:, :], ALU.pow).then_inc(a_rstd, 1)

                def norm_a(q, r):
                    t = group(q, r)
                    wait_done(pool, a_rstd, t)
                    wait_free(pool, a_tr, t, 2)
                    alone(pool, pt)
                    for j in range(G):
                        c = slice(j * P, (j + 1) * P)
                        last = pool.tensor_scalar(xn[:, r % 2, c], xa[:, r, c], mv[:, r, j, 0:1], ve[:, r, j:j + 1], ALU.subtract, ALU.mult)
                    last.then_inc(a_xn, 1)

                def rstd_d(q, r):
                    t = group(q, r)
                    ld.at(t)
                    wait_done(pool, a_x1, t)
                    wait_free(pool, a_xn2, t, 4)
                    alone(pool, pt)
                    ld.then(pool.tensor_scalar(ve2[:, r, :], mv2[:, r, :, 1], EPS, None, ALU.add))
                    pool.tensor_tensor(ve2[:, r, :], ve2[:, r, :], mhalf[:, :], ALU.pow).then_inc(a_rstd2, 1)

                steps(pool, [(8, rstd_d), (0, rstd_a), (1, norm_a)], NG)

            @block.vector
            def _(dve):
                v = nc.vector
                for s in (a_st, a_stats, a_maxs2, a_maxs, a_leaky, a_max, a_inv, a_avu, a_st2, a_x1, a_nb, a_lg, a_top, a_idx, a_kept, a_p):
                    dve.sem_inc(s, CREDIT)

                def s1_of(r):
                    return wh[:, r, :, :].rearrange("p a (b c) -> p a b c", b=2)[:, :, :, P].rearrange("p a b -> p (a b)")

                def stats_a(q, r):
                    t = group(q, r)
                    wait_loaded(dve, xa_in[r], q)
                    wait_free(dve, a_xn, t, 4)
                    wait_free(dve, a_stats, t, 1)
                    alone(dve, vt)
                    for j in range(G):
                        last = v.bn_stats(stats[:, j, :], xa[:, r, j * P:(j + 1) * P])
                    last.then_inc(a_st, 1)

                def max_s2(q, r):
                    wait_done(dve, a_sc, group(q, r))
                    v.reduce_max(rmax[:, 0, :], as3(psum[3][:, :]), AX.X).then_inc(a_maxs2, 1)

                def plus_s1(q, r):
                    t = group(q, r)
                    wait_done(dve, a_whs, t)
                    wait_done(dve, a_maxs2, t)
                    v.tensor_tensor(rmax[:, 1, :], rmax[:, 0, :], s1_of(r), ALU.add).then_inc(a_maxs, 1)

                def leaky(q, r):
                    wait_done(dve, a_maxs, group(q, r))
                    v.scalar_tensor_tensor(rmax[:, 2, :], rmax[:, 1, :], SLOPE, rmax[:, 1, :], ALU.mult, ALU.max).then_inc(a_leaky, 1)

                def shifts(q, r):
                    t = group(q, r)
                    wait_done(dve, a_leaky, t)
                    wait_free(dve, a_exp, t, 4)
                    v.tensor_tensor(shift[:, r, 0, :], s1_of(r), rmax[:, 2, :], ALU.subtract)
                    v.scalar_tensor_tensor(shift[:, r, 1, :], s1_of(r), SLOPE, rmax[:, 2, :], ALU.mult, ALU.subtract).then_inc(a_max, 1)

                def p_c(q, r):
                    t = group(q, r)
                    wait_done(dve, a_exp, t)
                    wait_free(dve, a_att, t, 2)
                    for j in range(G):
                        c = slice(j * P, (j + 1) * P)
                        last = v.scalar_tensor_tensor(att[:, r % 2, c], pos[:, r % 2, c], 1.0, neg[:, r % 2, c], ALU.mult,
                                                      ALU.max, accum_out=rsum[:, r, j:j + 1])
                    last.then_inc(a_p, 1)

                def inverse_sum(q, r):
                    wait_done(dve, a_p, group(q, r))
                    v.reciprocal(rsum[:, r, :], rsum[:, r, :]).then_inc(a_inv, 1)

                def add_d(q, r):
                    t = group(q, r)
                    wait_done(dve, a_inv, t)
                    wait_done(dve, a_av, t)
                    wait_loaded(dve, xd_in[r], q)
                    wait_stored(dve, x1_st[r], q)
                    wait_free(dve, a_xn2, t, 4)
                    for j in range(G):
                        last = v.scalar_tensor_tensor(xo[:, r, j * P:(j + 1) * P], psum[5][:, j * P:(j + 1) * P],
                                                      rsum[:, r, j:j + 1], xd[:, r, j * P:(j + 1) * P], ALU.mult, ALU.add)
                    last.then_inc(a_avu, 1)

                def shift_d(q, r):
                    t = group(q, r)
                    wait_done(dve, a_rstd2, t)
                    v.scalar_tensor_tensor(nb2[:, r, :], mv2[:, r, :, 0], -1.0, ve2[:, r, :], ALU.mult, ALU.mult).then_inc(a_nb, 1)

                def logits(q, r):
                    wait_done(dve, a_gate, group(q, r))
                    v.tensor_tensor(lg[:, :, :], psum[7][:, 0:G * E0].rearrange("p (g c) -> p g c", g=G),
                                    gbias.unsqueeze(1).to_broadcast([P, G, E0]), ALU.add).then_inc(a_lg, 1)

                def top_values(q, r):
                    wait_done(dve, a_lg, group(q, r))
                    wait_free(dve, a_kept, group(q, r), 1)
                    alone(dve, vt)
                    for j in range(G):
                        last = v.max(top8[:, j, :], lg[:, j, :])
                    last.then_inc(a_top, 1)

                def top_experts(q, r):
                    wait_done(dve, a_top, group(q, r))
                    alone(dve, vt)
                    for j in range(G):
                        last = v.max_index(idx8[:, j, :], top8[:, j, :], lg[:, j, :])
                    last.then_inc(a_idx, 1)

                def keep_top(q, r):
                    t = group(q, r)
                    wait_done(dve, a_idx, t)
                    v.tensor_copy(expert[:, bass.ds(t * G, G), :], idx8[:, :, 0:2])
                    v.tensor_copy(top[:, bass.ds(t * G, G), :], top8[:, :, 0:2]).then_inc(a_kept, 1)

                steps(dve, [(12, logits), (8, add_d), (12, top_values), (8, stats_of(nc, vt, xo, a_avu, stats2, a_x1, a_st2)),
                            (4, max_s2), (12, top_experts), (4, plus_s1), (8, moments(nc, vt, stats2, a_st2, mv2, a_x1)),
                            (4, leaky), (12, keep_top), (4, shifts), (5, p_c), (9, shift_d), (0, stats_a), (7, inverse_sum),
                            (0, moments(nc, vt, stats, a_st, mv, a_stats))], NG)

            @block.scalar
            def _(act):
                s_ = nc.scalar
                for s in (a_xnT, a_whs, a_attT, a_exp, a_xn2, a_xn2T):
                    act.sem_inc(s, CREDIT)

                def xnT_a(q, r):
                    t = group(q, r)
                    wait_done(act, a_tr, t)
                    wait_free(act, a_sc, t, 2)
                    s_.activation(xnT[:, r % 2, :], psum[0][:, :], ACT.Copy).then_inc(a_xnT, 1)

                def wh_b(q, r):
                    t = group(q, r)
                    wait_done(act, a_wh, t)
                    wait_free(act, a_av, t, 4)
                    for h in range(2):
                        last = s_.activation(wh[:, r, h, :], whp[h][:, 0:2 * (P + 2)], ACT.Copy)
                    last.then_inc(a_whs, 1)

                def exp_c(q, r):
                    t = group(q, r)
                    wait_free(act, a_p, t, 2)
                    wait_done(act, a_max, t)
                    wait_done(act, a_sc, t)
                    for j in range(G):
                        c = slice(j * P, (j + 1) * P)
                        s_.activation(pos[:, r % 2, c], psum[3][:, c], ACT.Exp, bias=shift[:, r, 0, j:j + 1])
                        last = s_.activation(neg[:, r % 2, c], psum[3][:, c], ACT.Exp, bias=shift[:, r, 1, j:j + 1], scale=SLOPE)
                    last.then_inc(a_exp, 1)

                def attT_d(q, r):
                    t = group(q, r)
                    wait_done(act, a_att, t)
                    wait_free(act, a_av, t, 2)
                    s_.activation(attT[:, r % 2, :], psum[4][:, :], ACT.Copy).then_inc(a_attT, 1)

                def norm_d(q, r):
                    t = group(q, r)
                    wait_done(act, a_nb, t)
                    wait_stored(act, xn_st[r], q)
                    wait_free(act, a_tr2, t, 4)
                    for j in range(G):
                        c = slice(j * P, (j + 1) * P)
                        last = s_.activation(xn2[:, r, c], xo[:, r, c], ACT.Identity, bias=nb2[:, r, j:j + 1], scale=ve2[:, r, j:j + 1])
                    last.then_inc(a_xn2, 1)

                def xnT_d(q, r):
                    t = group(q, r)
                    wait_done(act, a_tr2, t)
                    wait_free(act, a_gate, t, 2)
                    s_.activation(xn2T[:, r % 2, :], psum[6][:, :], ACT.Copy).then_inc(a_xn2T, 1)

                steps(act, [(6, attT_d), (4, exp_c), (9, norm_d), (10, xnT_d), (3, wh_b), (2, xnT_a)], NG)

            @block.tensor
            def _(pe):
                mm = nc.tensor.matmul
                for s in (a_tr, a_wh, a_sc, a_att, a_av, a_tr2, a_gate):
                    pe.sem_inc(s, CREDIT)

                def tr_a(q, r):
                    t = group(q, r)
                    wait_done(pe, a_xn, t)
                    wait_free(pe, a_xnT, t, 1)
                    for j in range(G):
                        last = nc.tensor.transpose(psum[0][:, j * P:(j + 1) * P], xn[:, r % 2, j * P:(j + 1) * P], ident[:, :])
                    last.then_inc(a_tr, 1)

                def wh_b(q, r):
                    t = group(q, r)
                    wait_done(pe, a_xnT, t)
                    wait_free(pe, a_whs, t, 1)
                    for j in range(G):
                        c = (j % 2) * (P + 2)
                        last = mm(whp[j // 2][:, c:c + P + 2], xnT[:, r % 2, j * P:(j + 1) * P], Waug[:, :], start=True, stop=True)
                    last.then_inc(a_wh, 1)
                    wait_free(pe, a_exp, t, 1)
                    mm(psum[3][:, :], wa2[:, :], xnT[:, r % 2, :], start=True, stop=False)
                    mm(psum[3][:, :], ident_bf[:, :], mask[:, :].unsqueeze(1).to_broadcast([P, G, P]),
                       start=False, stop=True).then_inc(a_sc, 1)

                def att_c(q, r):
                    t = group(q, r)
                    wait_done(pe, a_p, t)
                    wait_free(pe, a_attT, t, 1)
                    for j in range(G):
                        last = nc.tensor.transpose(psum[4][:, j * P:(j + 1) * P], att[:, r % 2, j * P:(j + 1) * P], ident[:, :])
                    last.then_inc(a_att, 1)

                def av_d(q, r):
                    t = group(q, r)
                    wait_done(pe, a_attT, t)
                    wait_free(pe, a_avu, t, 1)
                    for j in range(G):
                        c = (j % 2) * (P + 2)
                        last = mm(psum[5][:, j * P:(j + 1) * P], attT[:, r % 2, j * P:(j + 1) * P],
                                  wh[:, r, j // 2, c:c + P], start=True, stop=True)
                    last.then_inc(a_av, 1)

                def tr_e(q, r):
                    t = group(q, r)
                    wait_done(pe, a_xn2, t)
                    wait_free(pe, a_xn2T, t, 1)
                    for j in range(G):
                        last = nc.tensor.transpose(psum[6][:, j * P:(j + 1) * P], xn2[:, r, j * P:(j + 1) * P], ident[:, :])
                    last.then_inc(a_tr2, 1)

                def gate_e(q, r):
                    t = group(q, r)
                    wait_done(pe, a_xn2T, t)
                    wait_free(pe, a_lg, t, 1)
                    for j in range(G):
                        last = mm(psum[7][:, j * E0:(j + 1) * E0], xn2T[:, r % 2, j * P:(j + 1) * P], gw_s[:, :],
                                  start=True, stop=True)
                    last.then_inc(a_gate, 1)

                steps(pe, [(6, att_c), (7, av_d), (10, tr_e), (11, gate_e), (3, wh_b), (2, tr_a)], NG)
        end_stage()
        scope.pop().close()

        s_w, r_v, r_mm, r_pe = sem("expert_weights"), sem("route_v"), sem("route_counts"), sem("route_list")
        r_oh, r_used = sem("route_onehot"), sem("route_onehot_used")
        r_exp, r_tot, r_last, r_inside = sem("route_exp"), sem("route_totals"), sem("route_last_tile"), sem("route_inside")
        scope.append(ExitStack())
        w12_hi, w12_lo, w3_s = sb("w12_hi", [P, E0, 2 * HID], F32R), sb("w12_lo", [P, E0, 2 * HID], F32R), sb("w3_s", [P, E0, HID // P, P])
        tile_token, tile_expert = sb("tile_token", [P, MT], I32), sb("tile_expert", [1, MT], I32)
        scope.append(ExitStack())
        w12_s = w12_lo[:, :, :].bitcast(F32)
        r_wh, r_wl = sem("route_w_hi"), sem("route_w_lo")
        oh = [sb(f"oh{k}", [P, E0, BATCH]) for k in range(2)]
        both, cum, rank = sb("both", [P, E0, BATCH]), sb("cum", [P, E0, BATCH]), sb("rank", [P, E0, BATCH])
        ends, tot, tot_bf = sb("ends", [P, E0 + 1]), sb("tot", [P, E0]), sb("tot_bf", [P, E0], BF16)
        need_i, need, last_tile, off = sb("need_i", [P, E0], I32), sb("need", [P, E0]), sb("last_tile", [P, E0]), sb("off", [P, E0])
        endcol, inside = sb("endcol", [E0, 1]), sb("inside", [E0, MT], BF16)
        slot_f = sb("slot_f", [P, BATCH, 2])
        lo_i, hi_i = sb("lo_i", [P, BATCH, 2], I32), sb("hi_i", [P, BATCH, 2], I32)
        lo, hi = sb("lo", [P, BATCH, 2]), sb("hi", [P, BATCH, 2])
        lo_row, lo_graph, hi_sign = sb("lo_row", [P, 4, 2, P], BF16), sb("lo_graph", [P, 4, 2, P], BF16), sb("hi_sign", [P, 4, 2, MT + 1], BF16)
        sums, twice = sb("sums", [P, MT + 1]), sb("twice", [P, MT])
        r_sign, r_hi = sem("route_sign"), sem("route_hi")
        pairs = psum[3][:, 0:MT + 1]
        ZC = 12
        zeros, r_z = sb("zeros", [P, PT * P // ZC], BF16), sem("zeros_set")
        sorted_z = sorted_d.rearrange("(p z k) f -> p z (k f)", p=P, z=ZC)
        with nc.Block() as block:
            @block.sync
            def _(sp):
                sp.dma_start(w12_s[:, :, :], w12).then_inc(s_w, 16)
                sp.wait_ge(s_w, 16)
                sp.dma_start(w3_s[:, :, :, :], w3).then_inc(s_w, 16)
                sp.wait_ge(r_z, 1)
                for i in range(ZC):
                    sp.dma_start(sorted_z[:, i, :], zeros[:, :]).then_inc(s_w, 16)
                sp.wait_ge(s_w, 16 * (2 + ZC))

            @block.gpsimd
            def _(pool):
                pool.memset(zeros[:, :], 0.0).then_inc(r_z, 1)
                pool.wait_ge(r_wh, 1)
                pool.tensor_tensor(w12_lo[:, :, :], w12_s[:, :, :], w12_hi[:, :, :].bitcast(F32), ALU.subtract).then_inc(r_wl, 1)

            @block.scalar
            def _(act):
                act.wait_ge(r_v, 1)
                nc.scalar.activation(share[:, :, 1], top[:, :, 1], ACT.Exp).then_inc(r_exp, 1)
                act.sem_inc(r_sign, CREDIT)
                act.wait_ge(s_w, 16)
                nc.scalar.activation(w12_hi[:, :, :], w12_s[:, :, :], ACT.Copy).then_inc(r_wh, 1)
                act.wait_ge(r_hi, 1)

                def signs_of_hi(q, r):
                    t = group(q, r)
                    wait_free(act, r_used, t, 4)
                    alone(act, ticks["scalar"])
                    for k in range(2):
                        last = nc.scalar.activation(hi_sign[:, r, k, :], count[:, 0:MT + 1], ACT.Sign, bias=hi[:, bass.ds(t, 1), k])
                    last.then_inc(r_sign, 1)

                steps(act, [(0, signs_of_hi)], BATCH)

            @block.vector
            def _(dve):
                v = nc.vector
                dve.sem_inc(r_oh, CREDIT)
                link = Links(dve, r_v)
                link.then(v.tensor_tensor(top[:, :, 1], top[:, :, 1], top[:, :, 0], ALU.subtract))
                for k in range(2):
                    v.tensor_tensor(oh[k][:, :, :], count[:, 0:E0].unsqueeze(2).to_broadcast([P, E0, BATCH]),
                                    expert[:, :, k].unsqueeze(1).to_broadcast([P, E0, BATCH]), ALU.is_equal)
                v.memset(ends[:, 0:1], 0.0)
                dve.wait_ge(r_exp, 1)
                link.then(v.tensor_scalar(share[:, :, 0], share[:, :, 1], 1.0, None, ALU.add))
                link.then(v.reciprocal(share[:, :, 0], share[:, :, 0]))
                v.tensor_tensor(share[:, :, 1], share[:, :, 1], share[:, :, 0], ALU.mult)
                link.then(v.tensor_tensor(both[:, :, :], oh[0][:, :, :], oh[1][:, :, :], ALU.add))
                flat = both[:, :, :].rearrange("p e b -> p (e b)")
                link.then(v.tensor_tensor_scan(cum[:, :, :].rearrange("p e b -> p (e b)"), flat, flat, 0.0, ALU.add, ALU.max))
                link.then(v.tensor_copy(ends[:, 1:], cum[:, :, BATCH - 1]))
                link.then(v.tensor_tensor(tot[:, :], ends[:, 1:], ends[:, 0:E0], ALU.subtract))
                v.tensor_copy(tot_bf[:, :], tot[:, :]).then_inc(r_tot, 1)
                dve.wait_ge(r_mm, 1)
                link.then(v.tensor_scalar(need[:, :], psum[0][:, E0:2 * E0], float(P - 1), None, ALU.add))
                link.then(v.tensor_copy(need_i[:, :], need[:, :]))
                link.then(v.tensor_scalar(need_i[:, :], need_i[:, :], P.bit_length() - 1, None, ALU.arith_shift_right))
                link.then(v.tensor_copy(need[:, :], need_i[:, :]))
                v.tensor_tensor_scan(last_tile[:, :], need[:, :], need[:, :], 0.0, ALU.add, ALU.max).then_inc(r_last, 1)
                dve.wait_ge(r_last, 1)
                link.then(v.tensor_tensor(off[:, :], last_tile[:, :], need[:, :], ALU.subtract))
                link.then(v.tensor_scalar(off[:, :], off[:, :], float(P), None, ALU.mult))
                link.then(v.tensor_tensor(off[:, :], off[:, :], psum[0][:, 0:E0], ALU.add))
                v.tensor_tensor(rank[:, :, :], cum[:, :, :], both[:, :, :], ALU.subtract)
                link.then(v.tensor_tensor(off[:, :], off[:, :], ends[:, 0:E0], ALU.subtract))
                link.then(v.tensor_tensor(rank[:, :, :], rank[:, :, :], off[:, :].unsqueeze(2).to_broadcast([P, E0, BATCH]), ALU.add))
                for k in range(2):
                    link.then(v.tensor_tensor(oh[k][:, :, :], oh[k][:, :, :], rank[:, :, :], ALU.mult))
                    link.then(v.tensor_reduce(slot_f[:, :, k], oh[k][:, :, :].rearrange("p e b -> p b e"), AX.X, ALU.add))
                link.then(v.tensor_copy(slot[:, :, :], slot_f[:, :, :]))
                v.tensor_scalar(lo_i[:, :, :], slot[:, :, :], P - 1, None, ALU.bitwise_and)
                link.then(v.tensor_scalar(hi_i[:, :, :], slot[:, :, :], P.bit_length() - 1, None, ALU.arith_shift_right))
                v.tensor_copy(lo[:, :, :], lo_i[:, :, :])
                link.then(v.tensor_copy(hi[:, :, :], hi_i[:, :, :]))
                v.tensor_scalar(hi[:, :, :], hi[:, :, :], -1.0, -0.5, ALU.mult, ALU.add).then_inc(r_hi, 1)

                dve.wait_ge(r_mm, 2)
                link.then(v.tensor_copy(endcol[:, :], psum[1][0:E0, 0:1]))
                v.tensor_scalar(inside[:, :], count[0:E0, 0:MT], endcol[:, :], None, ALU.is_ge).then_inc(r_inside, 1)
                dve.wait_ge(r_mm, 3)
                link.then(v.tensor_scalar(tile_expert[:, :], psum[2][0:1, 0:MT], float(E0 - 1), None, ALU.min))

                def onehots(q, r):
                    t = group(q, r)
                    wait_free(dve, r_used, t, 4)
                    for k in range(2):
                        v.tensor_scalar(lo_row[:, r, k, :], count_bf[:, 0:P], lo[:, bass.ds(t, 1), k], row_id[:, :],
                                        ALU.is_equal, ALU.mult)
                        last = v.tensor_scalar(lo_graph[:, r, k, :], count_bf[:, 0:P], lo[:, bass.ds(t, 1), k],
                                               count[:, bass.ds(t, 1)], ALU.is_equal, ALU.mult)
                    last.then_inc(r_oh, 1)

                steps(dve, [(0, onehots)], BATCH)
                dve.wait_ge(r_pe, 1)
                link.then(v.tensor_copy(sums[:, :], pairs))
                link.then(v.tensor_tensor(twice[:, :], sums[:, 1:], sums[:, 0:MT], ALU.subtract))
                link.then(v.tensor_scalar(tile_token[:, :], twice[:, :], 0.5, None, ALU.mult))

            @block.tensor
            def _(pe):
                mm = nc.tensor.matmul
                pe.sem_inc(r_used, CREDIT)
                pe.wait_ge(r_tot, 1)
                mm(psum[0][:, 0:E0], before[:, :], tot_bf[:, :], start=True, stop=True)
                mm(psum[0][:, E0:2 * E0], ones_bf[:, :], tot_bf[:, :], start=True, stop=True).then_inc(r_mm, 1)
                pe.wait_ge(r_last, 1)
                nc.tensor.transpose(psum[1][0:E0, 0:P], last_tile[:, :], ident[:, :]).then_inc(r_mm, 1)
                pe.wait_ge(r_inside, 1)
                mm(psum[2][0:1, 0:MT], ones_bf[0:E0, 0:1], inside[:, :], start=True, stop=True).then_inc(r_mm, 1)

                mm(pairs, zeros_bf[:, :], hi_zero[:, :], start=True, stop=False)

                def fill(q, r):
                    wait_done(pe, r_oh, group(q, r))
                    wait_done(pe, r_sign, group(q, r))
                    for k in range(2):
                        mm(pairs, lo_row[:, r, k, :], hi_sign[:, r, k, :], start=False, stop=False)
                        last = mm(pairs, lo_graph[:, r, k, :], hi_sign[:, r, k, :], start=False, stop=False)
                    last.then_inc(r_used, 1)

                steps(pe, [(0, fill)], BATCH)
                mm(pairs, zeros_bf[:, :], hi_zero[:, :], start=False, stop=True).then_inc(r_pe, 1)
        end_stage()
        scope.pop().close()

        g_in, y_st = sems("g_in"), sems("y_st")
        m_ix, m_tr, m_xT, m_h, m_silu, m_hid = sem("m_index"), sem("m_transposed"), sem("m_xT"), sem("m_h"), sem("m_silu"), sem("m_hid")
        m_trh, m_hT, m_y, m_yo = sem("m_hid_transposed"), sem("m_hidT"), sem("m_y"), sem("m_y_copied")
        scope.append(ExitStack())
        EG = MT // TE
        HC = HID // P
        ix = sb("ix", [P, 4, TE], I32)
        xg, yo = sb("xg", [P, 4, TE, P]), sb("yo", [P, 4, TE, P])
        xT_hi, xT_lo, m_xh = sb("xT_hi", [P, 4, TE, P], F32R), sb("xT_lo", [P, 4, TE, P], F32R), sem("m_xT_hi")
        gate, hid, hidT = sb("gate", [P, 4, TE, HID]), sb("hid", [P, 4, TE, HID]), sb("hidT", [P, 4, TE, HID])
        bx, bh, bt, by = [psum[0], psum[1]], [[psum[2], psum[3]], [psum[4], psum[5]]], psum[6], psum[7]
        with nc.Block() as block:
            @block.gpsimd
            def _(pool):
                pool.sem_inc(m_ix, CREDIT)

                def index(q, r):
                    t = group(q, r)
                    wait_free(pool, m_tr, t, 4)
                    alone(pool, pt)
                    pool.tensor_copy(ix[:, r, :], tile_token[:, bass.ds(t * TE, TE)]).then_inc(m_ix, 1)

                def gather(q, r):
                    wait_done(pool, m_ix, group(q, r))
                    alone(pool, pt)
                    for k in range(TE):
                        pool.indirect_dma_start(xg[:, r, k, :], None, xn_d,
                                                bass.IndirectOffsetOnAxis(ap=ix[:, r, k:k + 1], axis=0)).then_inc(g_in[r], 16)

                steps(pool, [(0, index), (1, gather)], EG)

            @block.tensor
            def _(pe):
                mm = nc.tensor.matmul
                for s in (m_tr, m_h, m_trh, m_y):
                    pe.sem_inc(s, CREDIT)

                def tr(q, r):
                    t = group(q, r)
                    wait_loaded(pe, g_in[r], q, TE)
                    wait_free(pe, m_xT, t, 2)
                    for k in range(TE):
                        last = nc.tensor.transpose(bx[r % 2][:, k * P:(k + 1) * P], xg[:, r, k, :], ident[:, :])
                    last.then_inc(m_tr, 1)

                def up(q, r):
                    t = group(q, r)
                    experts = load_indices(nc, tile_expert[0:1, bass.ds(t * TE, TE)], E0)
                    wait_done(pe, m_xT, t)
                    wait_free(pe, m_hid, t, 2)
                    for k in range(TE):
                        w_hi, w_lo = [w[:, bass.ds(experts[k], 1), :].rearrange("p a c -> p (a c)") for w in (w12_hi, w12_lo)]
                        mm(bh[r % 2][k][:, :], xT_hi[:, r, k, :], w_lo, start=True, stop=False)
                        mm(bh[r % 2][k][:, :], xT_lo[:, r, k, :], w_hi, start=False, stop=False)
                        last = mm(bh[r % 2][k][:, :], xT_hi[:, r, k, :], w_hi, start=False, stop=True)
                    last.then_inc(m_h, 1)

                def tr_hid(q, r):
                    t = group(q, r)
                    wait_done(pe, m_hid, t)
                    wait_free(pe, m_hT, t, 1)
                    for k in range(TE):
                        for c in range(HC):
                            last = nc.tensor.transpose(bt[:, (k * HC + c) * P:(k * HC + c + 1) * P],
                                                       hid[:, r, k, c * P:(c + 1) * P], ident[:, :])
                    last.then_inc(m_trh, 1)

                def down(q, r):
                    t = group(q, r)
                    experts = load_indices(nc, tile_expert[0:1, bass.ds(t * TE, TE)], E0)
                    wait_done(pe, m_hT, t)
                    wait_free(pe, m_yo, t, 1)
                    for k in range(TE):
                        for c in range(HC):
                            last = mm(by[:, k * P:(k + 1) * P], hidT[:, r, k, c * P:(c + 1) * P],
                                      w3_s[:, bass.ds(experts[k], 1), c, :].rearrange("p a c -> p (a c)"), start=c == 0, stop=c == HC - 1)
                    last.then_inc(m_y, 1)

                steps(pe, [(5, down), (4, tr_hid), (2, up), (0, tr)], EG)

            @block.scalar
            def _(act):
                for s in (m_xh, m_silu, m_yo):
                    act.sem_inc(s, CREDIT)

                def xT(q, r):
                    t = group(q, r)
                    wait_done(act, m_tr, t)
                    wait_free(act, m_h, t, 4)
                    nc.scalar.activation(xT_hi[:, r, :, :], bx[r % 2][:, 0:TE * P], ACT.Copy).then_inc(m_xh, 1)

                def silu(q, r):
                    t = group(q, r)
                    wait_done(act, m_h, t)
                    wait_free(act, m_hid, t, 4)
                    for k in range(TE):
                        last = nc.scalar.activation(gate[:, r, k, :], bh[r % 2][k][:, 0:HID], ACT.Silu)
                    last.then_inc(m_silu, 1)

                def y(q, r):
                    t = group(q, r)
                    wait_done(act, m_y, t)
                    wait_stored(act, y_st[r], q)
                    nc.scalar.activation(yo[:, r, :, :], by[:, 0:TE * P], ACT.Copy).then_inc(m_yo, 1)

                steps(act, [(5, y), (2, silu), (0, xT)], EG)

            @block.vector
            def _(dve):
                for s in (m_xT, m_hid, m_hT):
                    dve.sem_inc(s, CREDIT)

                def xT_low(q, r):
                    t = group(q, r)
                    wait_done(dve, m_xh, t)
                    wait_free(dve, m_h, t, 4)
                    nc.vector.tensor_tensor(xT_lo[:, r, :, :].rearrange("p k c -> p (k c)"), bx[r % 2][:, 0:TE * P],
                                            xT_hi[:, r, :, :].bitcast(F32).rearrange("p k c -> p (k c)"), ALU.subtract).then_inc(m_xT, 1)

                def mul(q, r):
                    t = group(q, r)
                    wait_done(dve, m_silu, t)
                    wait_free(dve, m_trh, t, 4)
                    for k in range(TE):
                        last = nc.vector.tensor_tensor(hid[:, r, k, :], gate[:, r, k, :], bh[r % 2][k][:, HID:2 * HID], ALU.mult)
                    last.then_inc(m_hid, 1)

                def hT(q, r):
                    t = group(q, r)
                    wait_done(dve, m_trh, t)
                    wait_free(dve, m_y, t, 4)
                    nc.vector.tensor_copy(hidT[:, r, :, :], bt[:, :]).then_inc(m_hT, 1)

                steps(dve, [(4, hT), (2, mul), (0, xT_low)], EG)

            @block.sync
            def _(sp):
                for r in range(4):
                    sp.sem_inc(y_st[r], 16)

                def store(q, r):
                    t = group(q, r)
                    wait_done(sp, m_yo, t)
                    sp.dma_start(y_d[bass.ds(t * (TE * P), TE * P), :].rearrange("(k p) f -> p k f", p=P),
                                 yo[:, r, :, :]).then_inc(y_st[r], 16)

                steps(sp, [(0, store)], EG)
                for r in range(4):
                    sp.wait_ge(y_st[r], 16 * (EG // 4 + 1))
        end_stage()
        scope.pop().close()
        scope.pop().close()

        c_x1, c_y, c_x3, c_sx = sems("c_x1"), sems("c_y"), sems("c_x3"), sems("c_sx")
        (c_ix, c_x2, c_p1, c_xn, c_tr, c_xnT, c_z, c_zs, c_h1, c_h1T, c_z2, c_z2s, c_h2, c_rl, c_xm, c_x3r, c_p2, c_xn4, c_sgn,
         c_tr4, c_xn4T, c_gate, c_oh, c_cntA, c_cntB, c_rkA, c_rkB, c_cnt) = [sem("c_" + n) for n in (
             "index x2 rstd xn transposed xnT z z_copied h1 h1T z2 z2_copied h2 relu xm x3 rstd3 xn3 sign transposed3 xn3T "
             "gate onehot countA countB rankA rankB counts").split()]
        c_v0, c_nb, c_nb3, c_zb, c_t1, c_xs, c_st, c_x3s, c_st3, c_gbit, c_pat, c_root, c_root3 = [sem("c_" + n) for n in (
            "zeroed shift shift3 gate_biased x1_y1 x2_sum stats x3_sum stats3 gate_bits pattern root root3").split()]
        scope.append(ExitStack())
        pat = sb("pat", [P, BATCH])
        rank1 = sb("rank1", [P, BATCH])
        scope.append(ExitStack())
        ix8 = sb("ix8", [P, 4, G * 2], I32)
        xa, yg = sb("c_xa", [P, 4, GW]), sb("yg", [P, 4, G * 2, P])
        t1, x2 = sb("t1", [P, GW]), sb("x2", [P, 4, GW])
        stats, mv, ve, nb = sb("stats", [P, G, 6]), sb("mv", [P, 4, G, 2]), sb("ve", [P, 4, G]), sb("nb", [P, 4, G])
        stats3, mv3, ve3, nb3 = sb("stats3", [P, G, 6]), sb("mv3", [P, 4, G, 2]), sb("ve3", [P, 4, G]), sb("nb3", [P, 4, G])
        xn, xnT, xm = sb("xn", [P, 4, GW]), sb("xnT", [P, 2, GW]), sb("xm", [P, 4, GW])
        zs, h1T, z2s, rl = sb("zs", [P, 2, GW]), sb("h1T", [P, 2, GW]), sb("z2s", [P, 2, GW]), sb("rl", [P, 2, GW])
        x3, xn4, xn4T, sx = sb("x3", [P, 4, GW]), sb("xn4", [P, 2, GW]), sb("xn4T", [P, 2, GW]), sb("sx", [P, 4, GW], BF16)
        zb, gbit = sb("zb", [P, G, E1]), sb("gbit", [P, G, E1])
        oh = sb("oh", [P, 4, G, PAT], BF16)
        junk = sb("junk", [P, G, PAT], BF16)
        bT, bZ, bH1, bZ2, bH2, bT4, bG, bR = psum
        with nc.Block() as block:
            @block.sync
            def _(sp):
                for r in range(4):
                    sp.sem_inc(c_x3[r], 16)
                    sp.sem_inc(c_sx[r], 16)

                def load(q, r):
                    t = group(q, r)
                    wait_free(sp, c_x2, t, 4)
                    alone(sp, ticks["sync"])
                    sp.dma_start(xa[:, r, :], x1_d[:, bass.ds(t * GW, GW)]).then_inc(c_x1[r], 16)

                def store_x(q, r):
                    t = group(q, r)
                    wait_done(sp, c_x3r, t)
                    alone(sp, ticks["sync"])
                    sp.dma_start(x2_d[:, bass.ds(t * GW, GW)], x3[:, r, :]).then_inc(c_x3[r], 16)

                def store_s(q, r):
                    t = group(q, r)
                    wait_done(sp, c_sgn, t)
                    alone(sp, ticks["sync"])
                    sp.dma_start(sx_v[:, bass.ds(t * GW, GW)], sx[:, r, :]).then_inc(c_sx[r], 16)

                steps(sp, [(0, load), (10, store_x), (12, store_s)], NG)
                for r in range(4):
                    sp.wait_ge(c_x3[r], 16 * (NG // 4 + 1))
                    sp.wait_ge(c_sx[r], 16 * (NG // 4 + 1))

            @block.gpsimd
            def _(pool):
                for s in (c_ix,):
                    pool.sem_inc(s, CREDIT)

                def gather(q, r):
                    t = group(q, r)
                    wait_free(pool, c_x2, t, 4)
                    alone(pool, pt)
                    pool.tensor_copy(ix8[:, r, :], slot[:, bass.ds(t * G, G), :].rearrange("p g k -> p (g k)")).then_inc(c_ix, 1)
                    wait_done(pool, c_ix, t)
                    alone(pool, pt)
                    for c in range(2 * G):
                        pool.indirect_dma_start(yg[:, r, c, :], None, y_d,
                                                bass.IndirectOffsetOnAxis(ap=ix8[:, r, c:c + 1], axis=0)).then_inc(c_y[r], 16)

                steps(pool, [(0, gather)], NG)

            @block.vector
            def _(dve):
                v = nc.vector
                for s in (c_p1, c_p2, c_t1, c_xs, c_st, c_x2, c_xm, c_x3s, c_st3, c_x3r, c_zb, c_gbit, c_pat, c_oh, c_rkA, c_rkB,
                          c_nb, c_nb3):
                    dve.sem_inc(s, CREDIT)

                def cols(j):
                    return slice(j * P, (j + 1) * P)

                def combine1(q, r):
                    t = group(q, r)
                    wait_loaded(dve, c_x1[r], q)
                    wait_loaded(dve, c_y[r], q, 2 * G)
                    alone(dve, vt)
                    for j in range(G):
                        last = v.scalar_tensor_tensor(t1[:, cols(j)], yg[:, r, 2 * j, :], share[:, bass.ds(t * G + j, 1), 0],
                                                      xa[:, r, cols(j)], ALU.mult, ALU.add)
                    last.then_inc(c_t1, 1)

                def combine2(q, r):
                    t = group(q, r)
                    wait_done(dve, c_t1, t)
                    wait_free(dve, c_xm, t, 4)
                    alone(dve, vt)
                    for j in range(G):
                        last = v.scalar_tensor_tensor(x2[:, r, cols(j)], yg[:, r, 2 * j + 1, :], share[:, bass.ds(t * G + j, 1), 1],
                                                      t1[:, cols(j)], ALU.mult, ALU.add)
                    last.then_inc(c_xs, 1)

                def inverses(root_done, ve_, done):
                    def work(q, r):
                        wait_done(dve, root_done, group(q, r))
                        v.reciprocal(ve_[:, r, :], ve_[:, r, :]).then_inc(done, 1)
                    return work

                def shifts(rstd_done, mv_, ve_, nb_, done):
                    def work(q, r):
                        wait_done(dve, rstd_done, group(q, r))
                        v.scalar_tensor_tensor(nb_[:, r, :], mv_[:, r, :, 0], -1.0, ve_[:, r, :], ALU.mult, ALU.mult).then_inc(done, 1)
                    return work

                def half(q, r):
                    t = group(q, r)
                    wait_done(dve, c_xn, t)
                    wait_free(dve, c_x3s, t, 4)
                    v.scalar_tensor_tensor(xm[:, r, :], xn[:, r, :], 0.5, x2[:, r, :], ALU.mult, ALU.add).then_inc(c_xm, 1)

                def add_x3(q, r):
                    t = group(q, r)
                    wait_done(dve, c_rl, t)
                    wait_stored(dve, c_x3[r], q)
                    wait_free(dve, c_xn4, t, 4)
                    v.tensor_tensor(x3[:, r, :], xm[:, r, :], rl[:, r % 2, :], ALU.add).then_inc(c_x3s, 1)

                def biased(q, r):
                    wait_done(dve, c_gate, group(q, r))
                    v.tensor_tensor(zb[:, :, :], bG[:, 0:G * E1].rearrange("p (g e) -> p g e", g=G),
                                    pbias.unsqueeze(1).to_broadcast([P, G, E1]), ALU.add).then_inc(c_zb, 1)

                def open_gates(q, r):
                    wait_done(dve, c_zb, group(q, r))
                    v.scalar_tensor_tensor(gbit[:, :, :], zb[:, :, :], 0.0, bits[:, :].unsqueeze(1).to_broadcast([P, G, E1]),
                                           ALU.is_gt, ALU.mult).then_inc(c_gbit, 1)

                def patterns(q, r):
                    t = group(q, r)
                    wait_done(dve, c_gbit, t)
                    v.tensor_reduce(pat[:, bass.ds(t * G, G)], gbit[:, :, :], AX.X, ALU.add).then_inc(c_pat, 1)

                def onehots(q, r):
                    t = group(q, r)
                    wait_done(dve, c_pat, t)
                    wait_free(dve, c_cntA, t, 3)
                    alone(dve, vt)
                    for j in range(G):
                        last = v.tensor_scalar(oh[:, r, j, :], count_bf[:, :], pat[:, bass.ds(t * G + j, 1)], None, ALU.is_equal)
                    last.then_inc(c_oh, 1)

                def ranks(h, counted, done):
                    def work(q, r):
                        t = group(q, r)
                        wait_done(dve, counted, t)
                        alone(dve, vt)
                        for j in range(2):
                            g = t * G + 2 * h + j
                            last = v.scalar_tensor_tensor(junk[:, 2 * h + j, :], count[:, 0:PAT], pat[:, bass.ds(g, 1)],
                                                          bR[:, j * PAT:(j + 1) * PAT], ALU.is_equal, ALU.mult,
                                                          accum_out=rank1[:, bass.ds(g, 1)])
                        last.then_inc(done, 1)
                    return work

                v.memset(oh[:, 3, 2, :], 0.0).then_inc(c_v0, 1)
                v.memset(oh[:, 3, 3, :], 0.0).then_inc(c_v0, 1)
                steps(dve, [(13, ranks(0, c_cntA, c_rkA)), (8, add_x3), (4, half), (8, stats_of(nc, vt, x3, c_x3s, stats3, c_x3r, c_st3)),
                            (12, biased), (9, inverses(c_root3, ve3, c_p2)), (1, combine1), (8, moments(nc, vt, stats3, c_st3, mv3, c_x3r)), (12, open_gates),
                            (2, inverses(c_root, ve, c_p1)), (1, combine2),
                            (12, patterns), (13, ranks(1, c_cntB, c_rkB)), (12, onehots),
                            (1, stats_of(nc, vt, x2, c_xs, stats, c_x2, c_st)), (9, shifts(c_p2, mv3, ve3, nb3, c_nb3)),
                            (2, shifts(c_p1, mv, ve, nb, c_nb)), (1, moments(nc, vt, stats, c_st, mv, c_x2))], NG)

            @block.scalar
            def _(act):
                s_ = nc.scalar
                for s in (c_root, c_root3, c_xn, c_xnT, c_zs, c_z2s, c_h1T, c_rl, c_xn4, c_sgn, c_xn4T):
                    act.sem_inc(s, CREDIT)

                def roots(have, mv_, ve_, done):
                    def work(q, r):
                        t = group(q, r)
                        wait_done(act, have, t)
                        s_.activation(ve_[:, r, :], mv_[:, r, :, 1], ACT.Sqrt, bias=eps_s[:, :]).then_inc(done, 1)
                    return work

                def norm(q, r):
                    t = group(q, r)
                    wait_done(act, c_nb, t)
                    wait_free(act, c_tr, t, 4)
                    wait_free(act, c_xm, t, 4)
                    for j in range(G):
                        c = slice(j * P, (j + 1) * P)
                        last = s_.activation(xn[:, r, c], x2[:, r, c], ACT.Identity, bias=nb[:, r, j:j + 1], scale=ve[:, r, j:j + 1])
                    last.then_inc(c_xn, 1)

                def copy_T(q, r):
                    t = group(q, r)
                    wait_done(act, c_tr, t)
                    wait_free(act, c_h1, t, 2)
                    s_.activation(xnT[:, r % 2, :], bT[:, :], ACT.Copy).then_inc(c_xnT, 1)

                def copy_z(q, r):
                    t = group(q, r)
                    wait_done(act, c_z, t)
                    wait_free(act, c_h1, t, 2)
                    s_.activation(zs[:, r % 2, :], bZ[:, :], ACT.Copy).then_inc(c_zs, 1)

                def copy_z2(q, r):
                    t = group(q, r)
                    wait_done(act, c_z2, t)
                    wait_free(act, c_h2, t, 2)
                    s_.activation(z2s[:, r % 2, :], bZ2[:, :], ACT.Copy).then_inc(c_z2s, 1)

                def relu1(q, r):
                    t = group(q, r)
                    wait_done(act, c_h1, t)
                    wait_free(act, c_h2, t, 2)
                    s_.activation(h1T[:, r % 2, :], bH1[:, :], ACT.Relu, bias=b1_s[:, :]).then_inc(c_h1T, 1)

                def relu2(q, r):
                    t = group(q, r)
                    wait_done(act, c_h2, t)
                    wait_free(act, c_x3r, t, 2)
                    s_.activation(rl[:, r % 2, :], bH2[:, :], ACT.Relu, scale=0.5).then_inc(c_rl, 1)

                def norm4(q, r):
                    t = group(q, r)
                    wait_done(act, c_nb3, t)
                    wait_free(act, c_tr4, t, 2)
                    for j in range(G):
                        c = slice(j * P, (j + 1) * P)
                        last = s_.activation(xn4[:, r % 2, c], x3[:, r, c], ACT.Identity, bias=nb3[:, r, j:j + 1], scale=ve3[:, r, j:j + 1])
                    last.then_inc(c_xn4, 1)
                    wait_done(act, c_xn4, t)
                    wait_stored(act, c_sx[r], q)
                    s_.activation(sx[:, r, :], xn4[:, r % 2, :], ACT.Sign).then_inc(c_sgn, 1)

                def copy_T4(q, r):
                    t = group(q, r)
                    wait_done(act, c_tr4, t)
                    wait_free(act, c_gate, t, 2)
                    s_.activation(xn4T[:, r % 2, :], bT4[:, :], ACT.Copy).then_inc(c_xn4T, 1)

                steps(act, [(2, roots(c_x2, mv, ve, c_root)), (9, roots(c_x3r, mv3, ve3, c_root3)), (3, norm), (10, norm4), (7, relu2), (6, copy_z2), (5, relu1), (4, copy_z), (10, copy_T4), (3, copy_T)], NG)

            @block.tensor
            def _(pe):
                mm = nc.tensor.matmul
                for s in (c_tr, c_z, c_h1, c_z2, c_h2, c_tr4, c_gate, c_cntA, c_cntB):
                    pe.sem_inc(s, CREDIT)

                def cols(j):
                    return slice(j * P, (j + 1) * P)

                def tr(q, r):
                    t = group(q, r)
                    wait_done(pe, c_xn, t)
                    wait_free(pe, c_xnT, t, 1)
                    for j in range(G):
                        last = nc.tensor.transpose(bT[:, cols(j)], xn[:, r, cols(j)], ident[:, :])
                    last.then_inc(c_tr, 1)

                def first(q, r):
                    t = group(q, r)
                    wait_done(pe, c_xnT, t)
                    wait_free(pe, c_zs, t, 1)
                    for j in range(G):
                        last = mm(bZ[:, cols(j)], xnT[:, r % 2, cols(j)], w1n_s[:, :], start=True, stop=True)
                    last.then_inc(c_z, 1)

                def neigh1(q, r):
                    t = group(q, r)
                    wait_done(pe, c_zs, t)
                    wait_free(pe, c_h1T, t, 1)
                    mm(bH1[:, :], w1l_s[:, :], xnT[:, r % 2, :], start=True, stop=False)
                    for j in range(G):
                        last = mm(bH1[:, cols(j)], zs[:, r % 2, cols(j)], adjT_s[:, :], start=False, stop=j == G - 1)
                    last.then_inc(c_h1, 1)

                def second(q, r):
                    t = group(q, r)
                    wait_done(pe, c_h1T, t)
                    wait_free(pe, c_z2s, t, 1)
                    for j in range(G):
                        last = mm(bZ2[:, cols(j)], h1T[:, r % 2, cols(j)], w2n_s[:, :], start=True, stop=True)
                    last.then_inc(c_z2, 1)

                def neigh2(q, r):
                    t = group(q, r)
                    wait_done(pe, c_z2s, t)
                    wait_free(pe, c_rl, t, 1)
                    mm(bH2[:, :], ones_row[:, :], b2x[:, :], start=True, stop=False)
                    for j in range(G):
                        mm(bH2[:, cols(j)], h1T[:, r % 2, cols(j)], w2l_s[:, :], start=False, stop=False)
                    mm(bH2[:, :], adjT_s[:, :], z2s[:, r % 2, :], start=False, stop=True).then_inc(c_h2, 1)

                def tr4(q, r):
                    t = group(q, r)
                    wait_done(pe, c_xn4, t)
                    wait_free(pe, c_xn4T, t, 1)
                    for j in range(G):
                        last = nc.tensor.transpose(bT4[:, cols(j)], xn4[:, r % 2, cols(j)], ident[:, :])
                    last.then_inc(c_tr4, 1)

                def gates(q, r):
                    t = group(q, r)
                    wait_done(pe, c_xn4T, t)
                    wait_free(pe, c_zb, t, 1)
                    for j in range(G):
                        last = mm(bG[:, j * E1:(j + 1) * E1], xn4T[:, r % 2, cols(j)], projT_s[:, :], start=True, stop=True)
                    last.then_inc(c_gate, 1)

                def counts(r_was, h_was, r, h):
                    a, b, c, d = oh[:, r_was, 2 * h_was, :], oh[:, r_was, 2 * h_was + 1, :], oh[:, r, 2 * h, :], oh[:, r, 2 * h + 1, :]
                    for to, mine, whole, new in ((0, a, b, c), (1, b, c, d)):
                        reg = bR[:, to * PAT:(to + 1) * PAT]
                        mm(reg, not_before[:, :], mine, start=False, stop=False, skip_group_check=True)
                        mm(reg, ones_bf[:, :], whole, start=False, stop=False, skip_group_check=True)
                        last = mm(reg, before[:, :], new, start=False, stop=True, skip_group_check=True)
                    return last

                def countA(q, r):
                    t = group(q, r)
                    wait_done(pe, c_oh, t)
                    wait_free(pe, c_rkB, t, 1)
                    counts((r + 3) % 4, 1, r, 0).then_inc(c_cntA, 1)

                def countB(q, r):
                    t = group(q, r)
                    wait_done(pe, c_rkA, t)
                    counts(r, 0, r, 1).then_inc(c_cntB, 1)

                pe.wait_ge(c_v0, 2)
                mm(bR[:, :], zeros_bf[:, :], oh[:, 3, 2:4, :], start=True, stop=True, skip_group_check=True)
                steps(pe, [(13, countA), (7, neigh2), (6, second), (13, countB), (5, neigh1), (4, first), (10, tr4),
                           (3, tr), (11, gates)], NG)
                pe.wait_ge(c_rkB, NG + CREDIT)
                mm(bR[:, 0:PAT], not_before[:, :], oh[:, 3, 2, :], start=False, stop=False, skip_group_check=True)
                mm(bR[:, 0:PAT], ones_bf[:, :], oh[:, 3, 3, :], start=False, stop=True, skip_group_check=True).then_inc(c_cnt, 1)
        end_stage()
        scope.pop().close()

        d_v, d_mm, d_last, d_in, d_out = [sem("d_" + n) for n in "link mm last_block inside scattered".split()]
        d_at, d_ix, d_x = sem("d_slot_link"), sem("d_index"), sems("d_x")
        d_sc = sems("d_scatter")
        d_wt, d_sign = sem("d_weights_summed"), sem("d_signs")
        signs = sb("signs", [P, PAT, P], BF16)
        PS = PAT // NG
        slot1 = sb("slot1", [P, BATCH], I32)
        block_pat = sb("block_pat", [1, NB * PT], I32)
        scope.append(ExitStack())
        need_i, need, last_b = sb("need_i", [P, PAT], I32), sb("need", [P, PAT]), sb("last_b", [P, PAT])
        start, endcol = sb("start", [P, PAT]), sb("endcol", [P, 2])
        inside = sb("inside", [P, 2, NB * PT], BF16)
        start_of, ix = sb("start_of", [P, 4, G]), sb("ix", [P, 4, G], I32)
        xs = sb("xs", [P, 4, G, P], BF16)
        junk = sb("junk", [P, 4, PAT], BF16)
        wt = sb("wt", [P, 2, PS, P])
        HB = NB * PT // 2
        with nc.Block() as block:
            @block.vector
            def _(dve):
                v = nc.vector
                for s in (d_wt, d_ix):
                    dve.sem_inc(s, CREDIT)
                link, at = Links(dve, d_v), Links(dve, d_at, 1)
                counted = psum[7][:, 0:PAT]
                link.then(v.tensor_scalar(need[:, :], counted, float(PB - 1), None, ALU.add))
                link.then(v.tensor_copy(need_i[:, :], need[:, :]))
                link.then(v.tensor_scalar(need_i[:, :], need_i[:, :], PB.bit_length() - 1, None, ALU.arith_shift_right))
                link.then(v.tensor_copy(need[:, :], need_i[:, :]))
                v.tensor_tensor_scan(last_b[:, :], need[:, :], need[:, :], 0.0, ALU.add, ALU.max).then_inc(d_last, 1)
                dve.wait_ge(d_last, 1)
                link.then(v.tensor_tensor(start[:, :], last_b[:, :], need[:, :], ALU.subtract))
                link.then(v.tensor_scalar(start[:, :], start[:, :], float(PB), None, ALU.mult))
                dve.wait_ge(d_mm, 1)
                for h in range(2):
                    last = v.tensor_copy(endcol[:, h:h + 1], psum[0][:, h * P:h * P + 1])
                link.then(last)
                for h in range(2):
                    last = v.tensor_scalar(inside[:, h, :], count[:, :], endcol[:, h:h + 1], None, ALU.is_ge)
                last.then_inc(d_in, 1)

                def slots(q, r):
                    t = group(q, r)
                    at.at(t)
                    wait_free(dve, d_ix, t, 4)
                    alone(dve, vt)
                    for j in range(G):
                        last = v.scalar_tensor_tensor(junk[:, j, :], count[:, 0:PAT], pat[:, bass.ds(t * G + j, 1)], start[:, :],
                                                      ALU.is_equal, ALU.mult, accum_out=start_of[:, r, j:j + 1])
                    at.then(last)
                    wait_free(dve, d_out, t, 4)
                    v.tensor_tensor(ix[:, r, :], start_of[:, r, :], rank1[:, bass.ds(t * G, G)], ALU.add).then_inc(d_ix, 1)
                    wait_done(dve, d_ix, t)
                    v.tensor_copy(slot1[:, bass.ds(t * G, G)], ix[:, r, :])

                def sum_weights(q, r):
                    t = group(q, r)
                    wait_free(dve, d_sign, t, 2)
                    alone(dve, vt)
                    v.tensor_tensor(wt[:, r % 2, :, :], wsum_lo[:, (r % 2) * PS:(r % 2 + 1) * PS, :],
                                    wsum_hi[:, bass.ds(2 * q + r // 2, 1), :].to_broadcast([P, PS, P]), ALU.add).then_inc(d_wt, 1)

                steps(dve, [(0, slots), (0, sum_weights)], NG)
                dve.wait_ge(d_mm, 2)
                for h in range(2):
                    last = v.tensor_scalar(block_pat[:, h * HB:(h + 1) * HB], psum[1 + h][0:1, 0:HB], float(PAT - 1), None, ALU.min)
                link.then(last)

            @block.scalar
            def _(act):
                act.sem_inc(d_sign, CREDIT)

                def sign(q, r):
                    t = group(q, r)
                    wait_done(act, d_wt, t)
                    nc.scalar.activation(signs[:, bass.ds(t * PS, PS), :], wt[:, r % 2, :, :], ACT.Sign).then_inc(d_sign, 1)

                steps(act, [(0, sign)], NG)

            @block.sync
            def _(sp):
                def load(q, r):
                    t = group(q, r)
                    wait_free(sp, d_out, t, 4)
                    alone(sp, ticks["sync"])
                    sp.dma_start(xs[:, r, :, :], sx_v[:, bass.ds(t * GW, GW)]).then_inc(d_x[r], 16)

                steps(sp, [(0, load)], NG)

            @block.gpsimd
            def _(pool):
                pool.sem_inc(d_out, CREDIT)

                def scatter(q, r):
                    wait_loaded(pool, d_x[r], q)
                    wait_done(pool, d_ix, group(q, r))
                    alone(pool, pt)
                    for j in range(G):
                        pool.indirect_dma_start(sorted_d, bass.IndirectOffsetOnAxis(ap=ix[:, r, j:j + 1], axis=0),
                                                xs[:, r, j, :], None).then_inc(d_sc[r], 16)

                def scattered(q, r):
                    pool.wait_ge(d_sc[r], (q + 1) * (16 * G))
                    pool.sem_inc(d_out, 1)

                steps(pool, [(0, scatter), (2, scattered)], NG)

            @block.tensor
            def _(pe):
                mm = nc.tensor.matmul
                pe.wait_ge(d_last, 1)
                for h in range(2):
                    last = nc.tensor.transpose(psum[0][:, h * P:(h + 1) * P], last_b[:, h * P:(h + 1) * P], ident[:, :])
                last.then_inc(d_mm, 1)
                pe.wait_ge(d_in, 1)
                for h in range(2):
                    for k in range(2):
                        last = mm(psum[1 + h][0:1, 0:HB], ones_bf[:, 0:1], inside[:, k, h * HB:(h + 1) * HB], start=k == 0, stop=k == 1)
                last.then_inc(d_mm, 1)
        end_stage()
        scope.pop().close()

        b_in, b_st = sems("b_in"), sems("b_st")
        b_tr, b_xT, b_y, b_yv, b_ya = [sem("b_" + n) for n in "transposed xT y y_vector y_scalar".split()]
        scope.append(ExitStack())
        xs, xsT, yb_s = sb("xs", [P, 4, TG, P], BF16), sb("xsT", [P, 4, TG * P], BF16), sb("yb_s", [PB, 4, TG, NB * P], BF16)
        bx = [psum[0], psum[1]]
        by = [psum[2 + k] for k in range(4)]
        HT = TG // 2
        with nc.Block() as block:
            @block.tensor
            def _(pe):
                mm = nc.tensor.matmul
                for s in (b_tr, b_y):
                    pe.sem_inc(s, CREDIT)

                def tr(q, r):
                    t = group(q, r)
                    wait_loaded(pe, b_in[r], q)
                    wait_free(pe, b_xT, t, 2)
                    for k in range(TG):
                        last = nc.tensor.transpose(bx[r % 2][:, 0:TG * P // 2].bitcast(BF16)[:, k * P:(k + 1) * P], xs[:, r, k, :],
                                                   ident_bf[:, :])
                    last.then_inc(b_tr, 1)

                def apply(q, r):
                    t = group(q, r)
                    wait_done(pe, b_xT, t)
                    for k in range(TG):
                        if k % 4 == 0:
                            pats = load_indices(nc, block_pat[0:1, bass.ds(t * (TG * NB) + k * NB, 4 * NB)], PAT)
                        wait_free(pe, b_ya if k % 2 else b_yv, t * HT + k // 2, 2)
                        for j in range(NB):
                            c = k * P + j * PB
                            last = mm(by[k % 4][0:PB, j * P:(j + 1) * P], xsT[:, r, c:c + PB],
                                      signs[:, bass.ds(pats[k % 4 * NB + j], 1), :].rearrange("p a c -> p (a c)"), start=True, stop=True)
                        last.then_inc(b_y, 1)

                steps(pe, [(0, tr), (1, apply)], PT // TG)

            @block.scalar
            def _(act):
                for s in (b_xT, b_ya):
                    act.sem_inc(s, CREDIT)

                def xT(q, r):
                    t = group(q, r)
                    wait_done(act, b_tr, t)
                    nc.scalar.activation(xsT[:, r, :], bx[r % 2][:, 0:TG * P // 2].bitcast(BF16), ACT.Copy).then_inc(b_xT, 1)

                def y(q, r):
                    t = group(q, r)
                    wait_stored(act, b_st[r], q)
                    for k in range(1, TG, 2):
                        wait_done(act, b_y, t * TG + k)
                        nc.scalar.activation(yb_s[:, r, k, :], by[k % 4][0:PB, :], ACT.Copy).then_inc(b_ya, 1)

                steps(act, [(0, xT), (1, y)], PT // TG)

            @block.vector
            def _(dve):
                dve.sem_inc(b_yv, CREDIT)

                def y(q, r):
                    t = group(q, r)
                    wait_stored(dve, b_st[r], q)
                    for k in range(0, TG, 2):
                        wait_done(dve, b_y, t * TG + k)
                        alone(dve, vt)
                        nc.vector.tensor_copy(yb_s[:, r, k, :], by[k % 4][0:PB, :]).then_inc(b_yv, 1)

                steps(dve, [(0, y)], PT // TG)

            @block.sync
            def _(sp):
                for r in range(4):
                    sp.sem_inc(b_st[r], 16)

                def load(q, r):
                    t = group(q, r)
                    wait_free(sp, b_tr, t, 4)
                    alone(sp, ticks["sync"])
                    sp.dma_start(xs[:, r, :, :], sorted_d[bass.ds(t * (TG * P), TG * P), :].rearrange("(k p) f -> p k f", p=P)).then_inc(b_in[r], 16)

                def store(q, r):
                    t = group(q, r)
                    wait_done(sp, b_yv, t * HT + HT - 1)
                    wait_done(sp, b_ya, t * HT + HT - 1)
                    alone(sp, ticks["sync"])
                    sp.dma_start(yb_d[bass.ds(t * (TG * P), TG * P), :].rearrange("(j p) o -> p j o", p=PB),
                                 yb_s[:, r, :, :].rearrange("p k (j o) -> p (k j) o", j=NB)).then_inc(b_st[r], 16)

                steps(sp, [(3, store), (0, load)], PT // TG)
                for r in range(4):
                    sp.wait_ge(b_st[r], 16 * (PT // TG // 4 + 1))
        end_stage()
        scope.pop().close()

        e_x, e_y, e_st = sems("e_x"), sems("e_y"), sems("e_st")
        e_ix, e_o, e_l = sem("e_index"), sem("e_out"), sem("e_link")
        scope.append(ExitStack())
        ix4 = sb("ix4", [P, 4, G], I32)
        xe, ye, oe = sb("xe", [P, 4, GW]), sb("ye", [P, 4, G, P], BF16), sb("oe", [P, 4, GW])
        with nc.Block() as block:
            @block.sync
            def _(sp):
                for r in range(4):
                    sp.sem_inc(e_st[r], 16)

                def load(q, r):
                    t = group(q, r)
                    wait_free(sp, e_o, t, 4)
                    alone(sp, ticks["sync"])
                    sp.dma_start(xe[:, r, :], x2_d[:, bass.ds(t * GW, GW)]).then_inc(e_x[r], 16)

                def store(q, r):
                    t = group(q, r)
                    wait_done(sp, e_o, t)
                    alone(sp, ticks["sync"])
                    sp.dma_start(out_v[:, bass.ds(t * GW, GW)], oe[:, r, :]).then_inc(e_st[r], 16)

                steps(sp, [(2, store), (0, load)], NG)
                for r in range(4):
                    sp.wait_ge(e_st[r], 16 * (NG // 4 + 1))

            @block.gpsimd
            def _(pool):
                pool.sem_inc(e_ix, CREDIT)

                def index(q, r):
                    t = group(q, r)
                    wait_free(pool, e_o, t, 4)
                    alone(pool, pt)
                    pool.tensor_copy(ix4[:, r, :], slot1[:, bass.ds(t * G, G)]).then_inc(e_ix, 1)

                def gather(q, r):
                    wait_done(pool, e_ix, group(q, r))
                    alone(pool, pt)
                    for j in range(G):
                        pool.indirect_dma_start(ye[:, r, j, :], None, yb_d,
                                                bass.IndirectOffsetOnAxis(ap=ix4[:, r, j:j + 1], axis=0)).then_inc(e_y[r], 16)

                steps(pool, [(0, index), (1, gather)], NG)

            @block.vector
            def _(dve):
                v = nc.vector
                dve.sem_inc(e_o, CREDIT)
                link = Links(dve, e_l, 1)

                def add(q, r):
                    t = group(q, r)
                    link.at(t)
                    wait_loaded(dve, e_x[r], q)
                    wait_loaded(dve, e_y[r], q, G)
                    wait_stored(dve, e_st[r], q)
                    link.then(v.tensor_tensor(as3(oe[:, r, :]), ye[:, r, :, :], scale.unsqueeze(1).to_broadcast([P, G, P]), ALU.mult))
                    v.tensor_tensor(oe[:, r, :], oe[:, r, :], xe[:, r, :], ALU.add).then_inc(e_o, 1)

                steps(dve, [(0, add)], NG)
        end_stage()
        while len(scope) > 1:
            scope.pop().close()


_OUTS = [((P, BATCH, P), "float32")]


def kernel(x, adj, L0_gnn_W, L0_gnn_a, L0_ffn_gate_w, L0_ffn_gate_b, L0_ffn_w1, L0_ffn_w2, L0_ffn_w3, L1_gnn_w1_loop,
           L1_gnn_w1_neigh, L1_gnn_b1, L1_gnn_w2_loop, L1_gnn_w2_neigh, L1_gnn_b2, L1_ffn_weight, L1_ffn_proj_w,
           L1_ffn_proj_b, L1_ffn_scale):
    import numpy as _np
    import concourse.bacc as _bacc
    from concourse import mybir as _mybir
    from concourse.bass_utils import run_bass_kernel_spmd as _run

    w3 = _np.asarray(L0_ffn_w3).reshape(E0, HID // P, P, P)
    laid = {
        "xt": _np.asarray(x).transpose(1, 0, 2),
        "adj": adj, "adjT": _np.asarray(adj).T,
        "W": L0_gnn_W, "WT": _np.asarray(L0_gnn_W).T, "a12": _np.asarray(L0_gnn_a).reshape(2, P).T,
        "gate_w": L0_ffn_gate_w,
        "w12": _np.concatenate([_np.asarray(L0_ffn_w1), _np.asarray(L0_ffn_w2)], axis=2).transpose(1, 0, 2),
        "w3": w3.transpose(2, 0, 1, 3),
        "w1l": L1_gnn_w1_loop, "w1n": L1_gnn_w1_neigh, "w2l": L1_gnn_w2_loop, "w2n": L1_gnn_w2_neigh,
        "b1": _np.asarray(L1_gnn_b1).reshape(P, 1), "b2": _np.asarray(L1_gnn_b2).reshape(1, P),
        "rows": _np.concatenate([_np.asarray(L0_ffn_gate_b), _np.asarray(L1_ffn_proj_b),
                                 _np.asarray(L1_ffn_scale).reshape(P)]).reshape(1, E0 + E1 + P),
        "wgt": _np.asarray(L1_ffn_weight)[0].transpose(1, 0, 2),
        "projT": _np.asarray(L1_ffn_proj_w).T,
    }
    nc = _bacc.Bacc("TRN2", target_bir_lowering=False, num_devices=1)
    arrays, args = {}, []
    for name, a in laid.items():
        a = _np.ascontiguousarray(a)
        arrays[f"in_{name}_dram"] = a
        args.append(nc.dram_tensor(f"in_{name}_dram", a.shape, _mybir.dt.from_np(a.dtype), kind="ExternalInput").ap())
    for i, (shape, dtype) in enumerate(_OUTS):
        dt = _mybir.dt.from_np(_np.dtype(dtype))
        args.append(nc.dram_tensor(f"out_{i}_dram", shape, dt, kind="ExternalOutput").ap())
    build(nc, *args)
    r = _run(nc, [arrays], core_ids=[0])
    return r.results[0]["out_0_dram"].transpose(1, 0, 2)
```
